# Optimizing a Trainium2 kernel written in Bass

```python
import numpy as np
import jax
import jax.numpy as jnp

def _softmax(x, axis=-1):
    return jax.nn.softmax(x, axis=axis)

def _gelu(x):
    return jax.nn.gelu(x, approximate=True)

def _silu(x):
    return jax.nn.silu(x)

def _sigmoid(x):
    return jax.nn.sigmoid(x)

def _layernorm(x, axis=-1, eps=1e-05):
    m = jnp.mean(x, axis=axis, keepdims=True)
    v = jnp.var(x, axis=axis, keepdims=True)
    return (x - m) / jnp.sqrt(v + eps)

def _scatter_add(tgt, idx, src, axis=0):
    return tgt.at[idx].add(src)

def _segment_sum(src, seg, n):
    return jax.ops.segment_sum(src, seg, n)
kernel_name = 'mk_gnn_preln_d2_gnn_r8_a1d78c'

def setup_inputs(seed: int=0):
    np.random.seed(seed)
    _w = jnp.asarray

    def _rec_inputs():
        import jax
        import jax.numpy as jnp
        _gk = jax.random.key(seed)
        x = -0.0005121 + 1.001 * jax.random.normal(jax.random.fold_in(_gk, 1), (12500, 64), jnp.float32)
        _s = jax.random.randint(jax.random.fold_in(_gk, 2), (200000,), 0, 12500, jnp.int32)
        _d = jax.random.randint(jax.random.fold_in(_gk, 3), (200000,), 0, 12500, jnp.int32)
        _loop = jnp.arange(12500, dtype=jnp.int32)
        src = jnp.concatenate([_s, _d, _loop])
        dst = jnp.concatenate([_d, _s, _loop])
        _o = jnp.argsort(dst, stable=True)
        src = src[_o]
        dst = dst[_o]
        edge_type_50 = jax.random.randint(jax.random.fold_in(_gk, 12), (412500,), 0, 50, jnp.int32)
        edge_weight = jax.random.uniform(jax.random.fold_in(_gk, 13), (412500,), jnp.float32, 0.0, 0.999999)
        return (x, src, dst, edge_type_50, edge_weight)
    x, src, dst, edge_type_50, edge_weight = _rec_inputs()

    def _L0_gnn_setup():
        import jax, jax.numpy as jnp
        import numpy as np
        N_NODES = 6250
        N_EDGES = 100000
        D_FEAT = 64
        EPS_NORM = 1e-12
        EPS_SOFTMAX = 1e-16
        key = jax.random.key(seed)
        k1, k2, k3, k4 = jax.random.split(key, 4)
        x = jax.random.normal(k1, (N_NODES, D_FEAT), dtype=jnp.float32)
        row = jax.random.randint(k2, (N_EDGES,), 0, N_NODES)
        col = jax.random.randint(k3, (N_EDGES,), 0, N_NODES)
        col = jnp.where(col == row, (col + 1) % N_NODES, col)
        edge_index = jnp.stack([row, col]).astype(jnp.int64)
        edge_attr = jax.random.uniform(k4, (N_EDGES,), dtype=jnp.float32)
        beta = jnp.ones((1,), dtype=jnp.float32)
        eps = jnp.zeros((1,), dtype=jnp.float32)
        return {'x': x, 'edge_attr': edge_attr, 'beta': beta, 'eps': eps, 'edge_index': edge_index}
    _L0_gnn_all = _L0_gnn_setup()
    _L0_gnn_in = {k: v for k, v in _L0_gnn_all.items() if k in ('beta', 'eps')}
    del _L0_gnn_all

    def _L1_gnn_setup():
        import jax, jax.numpy as jnp
        import numpy as np
        N_HOPS = 2
        LEAKY_SLOPE = 0.2
        EPS = 1e-12
        key = jax.random.key(seed)
        k1, k2, k3, k4, k5, k6 = jax.random.split(key, 6)
        N, R, C, E = (12500, 50, 64, 125000)
        return {'entity_emb': jax.random.normal(k1, (N, C), dtype=jnp.float32) * 0.1, 'relation_emb': jax.random.normal(k2, (R, C), dtype=jnp.float32) * 0.1, 'fc_w': jax.random.normal(k3, (C, 2 * C), dtype=jnp.float32) * 0.1, 'fc_b': jax.random.normal(k4, (C,), dtype=jnp.float32) * 0.1, 'edge_index': jax.random.randint(k5, (2, E), 0, N, dtype=jnp.int64), 'edge_type': jax.random.randint(k6, (E,), 0, R, dtype=jnp.int64)}
    _L1_gnn_all = _L1_gnn_setup()
    _L1_gnn_in = {k: v for k, v in _L1_gnn_all.items() if k in ('relation_emb', 'fc_w', 'fc_b')}
    del _L1_gnn_all
    return {'x': x, 'src': src, 'dst': dst, 'edge_type_50': edge_type_50, 'edge_weight': edge_weight, 'L0_gnn_beta': _L0_gnn_in['beta'], 'L0_gnn_eps': _L0_gnn_in['eps'], 'L1_gnn_relation_emb': _L1_gnn_in['relation_emb'], 'L1_gnn_fc_w': _L1_gnn_in['fc_w'], 'L1_gnn_fc_b': _L1_gnn_in['fc_b']}

def reference(x, src, dst, edge_type_50, edge_weight, L0_gnn_beta, L0_gnn_eps, L1_gnn_relation_emb, L1_gnn_fc_w, L1_gnn_fc_b):
    import jax
    import jax.numpy as jnp

    def _L0_gnn_ref(x, edge_attr, beta, eps, edge_index):
        import jax, jax.numpy as jnp
        import numpy as np
        N_NODES = 6250
        N_EDGES = 100000
        D_FEAT = 64
        EPS_NORM = 1e-12
        EPS_SOFTMAX = 1e-16
        N, d = x.shape
        row, col = (edge_index[0], edge_index[1])
        sq = jax.ops.segment_sum(edge_attr * edge_attr, row, num_segments=N)
        ea = edge_attr / jnp.maximum(jnp.sqrt(sq), EPS_NORM)[row]
        loop = jnp.arange(N)
        row_f = jnp.concatenate([row, loop])
        col_f = jnp.concatenate([col, loop])
        ea_f = jnp.concatenate([ea, jnp.ones((N,), ea.dtype)])
        xn = x / jnp.maximum(jnp.linalg.norm(x, axis=-1, keepdims=True), EPS_NORM)
        alpha = beta[0] * ea_f
        amax = jax.ops.segment_max(alpha, row_f, num_segments=N)
        ex = jnp.exp(alpha - amax[row_f])
        denom = jax.ops.segment_sum(ex, row_f, num_segments=N)
        a = ex / (denom[row_f] + EPS_SOFTMAX)
        out = jax.ops.segment_sum(a[:, None] * xn[col_f], row_f, num_segments=N)
        return (1.0 + eps[0]) * xn + out

    def _L1_gnn_ref(entity_emb, relation_emb, fc_w, fc_b, edge_index, edge_type):
        import jax, jax.numpy as jnp
        import numpy as np
        N_HOPS = 2
        LEAKY_SLOPE = 0.2
        EPS = 1e-12
        'RGAT.forward with mess_dropout=False: n_hops of relational-attention\n            gather -> leakyrelu -> scatter_softmax(head) -> scatter_sum -> residual -> L2 normalize.'
        N = entity_emb.shape[0]
        head, tail = (edge_index[0], edge_index[1])
        rel_e = relation_emb[edge_type]

        def agg(emb):
            a_input = jnp.concatenate([emb[head], emb[tail]], axis=-1)
            h = a_input @ fc_w.T + fc_b
            e = jnp.sum(h * rel_e, axis=-1)
            e = jnp.where(e > 0, e, LEAKY_SLOPE * e)
            m = jax.ops.segment_max(e, head, num_segments=N)
            ex = jnp.exp(e - m[head])
            denom = jax.ops.segment_sum(ex, head, num_segments=N)
            w = ex / denom[head]
            agg_emb = jax.ops.segment_sum(emb[tail] * w[:, None], head, num_segments=N)
            agg_emb = agg_emb + emb
            return agg_emb
        emb = entity_emb
        for _ in range(N_HOPS):
            emb = agg(emb)
            nrm = jnp.sqrt(jnp.sum(emb * emb, axis=-1, keepdims=True))
            emb = emb / jnp.maximum(nrm, EPS)
        return emb
    edge_index = jnp.stack([src, dst])
    h = jnp.maximum(_layernorm(x, axis=-1), 0.0)
    x = x + _L0_gnn_ref(h, edge_weight, L0_gnn_beta, L0_gnn_eps, edge_index)
    h = jnp.maximum(_layernorm(x, axis=-1), 0.0)
    x = x + _L1_gnn_ref(h, L1_gnn_relation_emb, L1_gnn_fc_w, L1_gnn_fc_b, edge_index, edge_type_50)
    return x

_drawn_inputs = setup_inputs


def setup_inputs(seed=0):
    import zlib

    import numpy as np

    out = dict(_drawn_inputs(seed))
    spreads = {}
    factors = {'edge_weight': 8.0, 'L1_gnn_relation_emb': 8.0, 'L1_gnn_fc_w': 8.0, 'L1_gnn_fc_b': 8.0}
    for name, (base, spread) in spreads.items():
        noise = np.random.default_rng([zlib.crc32(name.encode()), seed]).standard_normal(out[name].shape)
        drawn = base * np.exp(spread * noise) if base else spread * noise
        out[name] = jnp.asarray(drawn.astype(out[name].dtype))
    for name, factor in factors.items():
        out[name] = (out[name] * factor).astype(out[name].dtype)
    return out
```

```python
import numpy as np
import concourse.bass as bass
from concourse import mybir
from contextlib import ExitStack

F32 = mybir.dt.float32
BF16 = mybir.dt.bfloat16
I32 = mybir.dt.int32
ALU = mybir.AluOpType
ACT = mybir.ActivationFunctionType
AX = mybir.AxisListType

P = 128
NODES, D = 12500, 64
EDGES = 412500
RELS = 50
HEAD_TILES = -(-NODES // P)
LAST_NODES = NODES - (HEAD_TILES - 1) * P
PER_PART = -(-EDGES // P)
LAST_PART = EDGES - (P - 1) * PER_PART
GROUP = 8
UNROLL = 2
IN_GROUPS = -(-PER_PART // (GROUP * UNROLL)) * UNROLL
IN_TILES = IN_GROUPS * GROUP
BLOCKS = -(-(PER_PART + HEAD_TILES) // P)
TILES = BLOCKS * P
GROUPS = TILES // GROUP
POSITIONS = TILES * P
TABLE = HEAD_TILES * P
ROW = 128
W0 = D + 2
NEG = -1.5e38
LEAKY = 0.2
OUT_OF_BOUNDS = float(1 << 20)


def at_least(engine, sem, value):
    if isinstance(value, int) and value <= 0:
        return
    engine.wait_ge(sem, value)


def rounds(engine, count, body):
    body(0)
    with engine.Fori(1, count) as i:
        body(i)


def build(nc, x_d, src_d, dst_d, type_d, weight_d, beta_d, eps_d, rel_d, fcw_d, fcb_d, out_d):
    def dram(name, shape, dt=F32):
        return nc.dram_tensor(name, shape, dt, kind="Internal").ap()

    sorted_d = dram("sorted_records", (POSITIONS, 4))
    tile_of_d = dram("head_tile_of", (TILES,), I32)
    xn_d = dram("xn_table", (TABLE, D))
    x1_d = dram("x1_rows", (TABLE, D))
    hop_d = dram("hop_table", (TABLE, ROW))
    rows_d = dram("gathered_rows", (GROUPS * P, GROUP * D))

    ctx = ExitStack()
    with ctx:
        def sb(name, shape, dt=F32):
            return ctx.enter_context(nc.sbuf_tensor(name, shape, dt))

        def bank(name):
            return ctx.enter_context(nc.psum_tensor(name, [P, 512], F32))

        def sem(name):
            return ctx.enter_context(nc.semaphore(name))

        identity = sb("identity", [P, P])
        identity_bf = sb("identity_bf", [P, P], BF16)
        iota_i = sb("iota_i", [P, P], I32)
        iota_row = sb("iota_row", [P, P])
        iota_bf = sb("iota_bf", [P, P], BF16)
        iota_col_i = sb("iota_col_i", [P, 1], I32)
        iota_col = sb("iota_col", [P, 1])
        tile_no_i = sb("tile_no_i", [P, BLOCKS], I32)
        tile_no = sb("tile_no", [P, BLOCKS])
        earlier = sb("earlier", [P, P])
        lower_of = sb("lower_of", [P, P])
        ones = sb("ones", [P, P])
        from_prev = sb("from_prev", [P, P])
        from_next = sb("from_next", [P, P])
        zeros_bf = sb("zeros_bf", [P, P], BF16)
        params = sb("params", [P, 4])
        small = sb("small", [P, 8])
        small_sd = sb("small_sd", [P, HEAD_TILES])[:]
        small_mean = sb("small_mean", [P, HEAD_TILES])[:]
        rows1 = sb("rows1", [1, 4 * P + 8])
        fcw_sb = sb("fcw_sb", [D, 2 * D])
        fcwb = sb("fcwb", [D, D + 1])
        fcwa = sb("fcwa", [D, D + 1])
        rel_sb = sb("rel_sb", [RELS, D])
        relT = sb("relT", [D, RELS])
        ab = sb("ab", [D + 1, 2 * RELS])
        emb_t = sb("emb_t", [D + 1, 2 * P])

        A_TAIL, A_TYPE, A_HL, A_WT, A_EM, A_NS = (n * TILES for n in range(6))
        A_TJ = A_NS + TILES + 4
        A_ACC = A_TJ + TILES
        A_P = A_ACC + HEAD_TILES * W0
        A_V = A_P + HEAD_TILES * RELS
        A_T = A_V + HEAD_TILES * D
        A_END = A_T + HEAD_TILES * D
        arena = sb("arena", [P, A_END])

        def part(at, size, dt=F32):
            v = arena[:, at:at + size]
            return v if dt == F32 else v.bitcast(dt)

        tail_i = part(A_TAIL, TILES, I32)
        types = part(A_TYPE, TILES)
        local_head = part(A_HL, TILES)
        weight = part(A_WT, TILES)
        em = part(A_EM, TILES)
        same = part(A_NS, TILES + 1)
        tile_of = part(A_TJ, TILES, I32)[0:1, :]
        acc = part(A_ACC, HEAD_TILES * W0)
        acc3 = acc.rearrange("p (t c) -> p t c", c=W0)
        p_tab = part(A_P, HEAD_TILES * RELS)
        val = part(A_V, HEAD_TILES * D)
        val3 = val.rearrange("p (t d) -> p t d", d=D)
        tmp = part(A_T, HEAD_TILES * D)
        tmp3 = tmp.rearrange("p (t d) -> p t d", d=D)
        scan_a = part(A_ACC, TILES)
        scan_b = part(A_ACC + TILES, TILES)
        scan_c = part(A_ACC + 2 * TILES, TILES)
        scan_d = part(A_ACC + 3 * TILES, TILES)

        S_REC = A_ACC
        S_STG = S_REC + 4 * IN_TILES
        S_LO = S_STG + IN_TILES
        S_HI = S_LO + IN_TILES // 2
        rec = part(S_REC, 4 * IN_TILES).rearrange("p (j f) -> p j f", f=4)
        stage_i = part(S_STG, IN_TILES, I32)
        stage_f = part(S_STG, IN_TILES)
        lo_bf = part(S_LO, IN_TILES // 2, BF16)
        hi_bf = part(S_HI, IN_TILES // 2, BF16)
        half_i = part(0, IN_TILES, I32)
        blank = part(0, 4 * TILES)
        srec = part(S_REC, 4 * TILES).rearrange("p (j f) -> p j f", f=4)
        at = 0

        def take(size, dt=F32):
            nonlocal at
            v = part(at, size, dt)
            at += size
            return v

        oh_lo = [take(GROUP * P // 2, BF16) for _ in range(2)]
        oh_hi = [take(GROUP * HEAD_TILES // 2, BF16) for _ in range(2)]
        lo_t = [take(GROUP * P) for _ in range(2)]
        counts = [take(HEAD_TILES) for _ in range(2)]
        rec8 = [take(4 * GROUP) for _ in range(2)]
        junk = [take(P) for _ in range(GROUP)]
        junk2 = [take(HEAD_TILES) for _ in range(GROUP)]
        occ8 = [take(GROUP) for _ in range(2)]
        base8 = [take(GROUP) for _ in range(2)]
        pos8 = [take(GROUP, I32) for _ in range(2)]
        pos_lo = take(GROUP, I32)
        pos_hi = take(GROUP, I32)
        pad8 = take(GROUP)
        dest_f = take(GROUP)
        dest8 = [take(GROUP, I32) for _ in range(2)]
        hist = take(HEAD_TILES)
        tiles_i = take(HEAD_TILES, I32)
        tiles_f = take(HEAD_TILES)
        cum = take(HEAD_TILES)
        cum_x = take(HEAD_TILES)
        start_pos = take(HEAD_TILES)
        tile_f = take(BLOCKS)
        tile_i = take(BLOCKS, I32)
        assert at <= A_TJ

        at = A_V
        rows = [take(GROUP * ROW) for _ in range(2)]
        rhs = [take(GROUP * W0) for _ in range(2)]
        oh = [take(GROUP * P) for _ in range(2)]
        idx8 = [take(GROUP, I32) for _ in range(2)]
        hl8 = [take(GROUP) for _ in range(2)]
        type_oh = [take(GROUP * RELS) for _ in range(2)]
        zed = take(GROUP * RELS)
        assert at <= A_END
        scratch3 = part(A_WT, HEAD_TILES * D).rearrange("p (t d) -> p t d", d=D)
        stg = sb("stg", [P, 2 * ROW])

        banks = [bank(f"bank{n}") for n in range(8)]

        loaded = sem("loaded")
        const_ready = sem("const_ready")
        pool_step = sem("pool_step")
        dve_step = sem("dve_step")
        stage_in = sem("stage_in")
        stage_free = sem("stage_free")
        blank_ready = sem("blank_ready")
        blank_done = sem("blank_done")
        hist_oh = sem("hist_oh")
        hist_mm = sem("hist_mm")
        to_pe = sem("to_pe")
        from_pe = sem("from_pe")
        tile_i_ready = sem("tile_i_ready")
        tile_saved = sem("tile_saved")
        tile_loaded = sem("tile_loaded")
        rec_ready = sem("rec_ready")
        oh_ready = sem("oh_ready")
        hb_ready = sem("hb_ready")
        ot_ready = sem("ot_ready")
        lo_t_ready = sem("lo_t_ready")
        counts_ready = sem("counts_ready")
        updated = sem("updated")
        queried = sem("queried")
        rank_read = sem("rank_read")
        rank_step = sem("rank_step")
        lot_begun = sem("lot_begun")
        dest_ready = sem("dest_ready")
        scattered = [sem("scattered0"), sem("scattered1")]
        srec_in = sem("srec_in")
        sort_read = sem("sort_read")
        flip_ready = sem("flip_ready")
        flip_mm = sem("flip_mm")
        flipped = sem("flipped")
        act_in = sem("act_in")
        act_out = sem("act_out")
        node_in = sem("node_in")
        node_ready = sem("node_ready")
        node_out = sem("node_out")
        tab_ready = [None, sem("tab_ready1"), sem("tab_ready2")]
        tab_emb = [None, sem("tab_emb1"), sem("tab_emb2")]
        tab_t = [None, sem("tab_t1"), sem("tab_t2")]
        tab_copied = [None, sem("tab_copied1"), sem("tab_copied2")]
        tab_mm = [None, sem("tab_mm1"), sem("tab_mm2")]
        tab_staged = [None, sem("tab_staged1"), sem("tab_staged2")]
        tab_out = [None, [sem("tab_out1a"), sem("tab_out1b")], [sem("tab_out2a"), sem("tab_out2b")]]
        idx_ready = [sem(f"idx_ready{p}") for p in range(3)]
        gathered = [[sem(f"gathered{p}{b}") for b in range(2)] for p in range(3)]
        hl_ready = [None] + [sem(f"hl_ready{p}") for p in (1, 2)]
        hlb_ready = [None] + [sem(f"hlb_ready{p}") for p in (1, 2)]
        oht_ready = [None] + [sem(f"oht_ready{p}") for p in (1, 2)]
        toh_ready = [None] + [sem(f"toh_ready{p}") for p in (1, 2)]
        p_done = [None] + [sem(f"p_done{p}") for p in (1, 2)]
        z_step = [None] + [sem(f"z_step{p}") for p in (1, 2)]
        score_done = [None] + [sem(f"score_done{p}") for p in (1, 2)]
        kept = [None] + [[sem(f"kept{p}{b}") for b in range(2)] for p in (1, 2)]
        back_in = [None] + [[sem(f"back_in{p}{b}") for b in range(2)] for p in (1, 2)]
        sum_begin = [sem(f"sum_begin{p}") for p in range(3)]
        rhs_ready = [sem(f"rhs_ready{p}") for p in range(3)]
        scaled = [sem(f"scaled{p}") for p in range(3)]
        summed = [sem(f"summed{p}") for p in range(3)]
        added = [sem(f"added{p}") for p in range(3)]
        stored = sem("stored")

        block = ctx.enter_context(nc.Block())

        IN_ROUNDS = IN_GROUPS // UNROLL
        ROUNDS = GROUPS // UNROLL
        flips = [(em, scan_a, True)]
        flips += [(weight, scan_a, True), (scan_b, weight, False), (scan_c, em, False)]
        flips += [(em, scan_a, True), (scan_b, weight, False)] * 2

        carry_col = small[:, 0:1]
        reset_col = small[:, 1:2]
        carry_in = small[:, 2:3]
        edge_col = small[:, 3:4]
        edge_in = small[:, 4:5]
        max_row = rows1[:, 0:P]
        reset_row = rows1[:, P:2 * P]
        carried_row = rows1[:, 2 * P:3 * P + 4]

        @block.sync
        def _(sp):
            sp.dma_start(params[:, 0:1], beta_d[:].unsqueeze(0).to_broadcast([P, 1])).then_inc(loaded, 16)
            sp.dma_start(params[:, 1:2], eps_d[:].unsqueeze(0).to_broadcast([P, 1])).then_inc(loaded, 16)
            sp.dma_start(fcw_sb[:], fcw_d).then_inc(loaded, 16)
            sp.dma_start(fcwb[:, D:D + 1], fcb_d[:].unsqueeze(1)).then_inc(loaded, 16)
            sp.dma_start(rel_sb[:], rel_d).then_inc(loaded, 16)
            for n, (col, view) in enumerate([(src_d, stage_i), (dst_d, stage_i), (type_d, stage_i), (weight_d, stage_f)]):
                sp.wait_ge(stage_free, n + 1)
                sp.dma_start(view[0:P - 1, 0:PER_PART],
                             col[0:(P - 1) * PER_PART].rearrange("(p j) -> p j", p=P - 1)).then_inc(stage_in, 16)
                sp.dma_start(view[P - 1:P, 0:LAST_PART],
                             col[(P - 1) * PER_PART:EDGES].unsqueeze(0)).then_inc(stage_in, 16)
            sp.wait_ge(blank_ready, 2)
            sp.dma_start(sorted_d.rearrange("(p j) f -> p (j f)", p=P), blank).then_inc(blank_done, 16)
            sp.wait_ge(tile_i_ready, 1)
            sp.dma_start(tile_of_d.rearrange("(r k) -> r k", k=BLOCKS), tile_i).then_inc(tile_saved, 16)
            sp.wait_ge(tile_saved, 16)
            sp.dma_start(tile_of, tile_of_d.unsqueeze(0)).then_inc(tile_loaded, 16)
            for b in range(2):
                sp.wait_ge(scattered[b], 16 * GROUP * IN_ROUNDS)
            sp.wait_ge(sort_read, 1)
            sp.dma_start(part(S_REC, 4 * TILES), sorted_d.rearrange("(p j) f -> p (j f)", p=P)).then_inc(srec_in, 16)

            def load_nodes(view3, table, n_ready, whole=True):
                sp.wait_ge(node_ready, n_ready)
                if whole:
                    sp.dma_start(view3, table.rearrange("(t p) d -> p t d", p=P)).then_inc(node_in, 16)
                else:
                    sp.dma_start(view3[:, 0:HEAD_TILES - 1, :],
                                 table[0:(HEAD_TILES - 1) * P, :].rearrange("(t p) d -> p t d", p=P)).then_inc(node_in, 16)
                    sp.dma_start(view3[0:LAST_NODES, HEAD_TILES - 1, :],
                                 table[(HEAD_TILES - 1) * P:NODES, :]).then_inc(node_in, 16)

            load_nodes(val3, x_d, 1, whole=False)
            sp.wait_ge(node_ready, 2)
            sp.dma_start(xn_d.rearrange("(t p) d -> p t d", p=P), val3).then_inc(node_out, 16)
            load_nodes(val3, x_d, 3, whole=False)
            load_nodes(tmp3, xn_d, 3)
            sp.wait_ge(node_ready, 4)
            sp.dma_start(x1_d.rearrange("(t p) d -> p t d", p=P), val3).then_inc(node_out, 16)
            for p in (1, 2):
                def out_round(i):
                    for b in range(2):
                        sp.wait_ge(tab_staged[p], 2 * i + b + 1)
                        sp.dma_start(hop_d[bass.ds((2 * i + b) * P, P), :],
                                     stg[:, b * ROW:(b + 1) * ROW]).then_inc(tab_out[p][b], 16)
                rounds(sp, HEAD_TILES // 2, out_round)

                def keep_round(i):
                    for b in range(2):
                        sp.wait_ge(gathered[p][b], 16 * GROUP * (i + 1))
                        g = 2 * i + b
                        sp.dma_start(rows_d[bass.ds(g * P, P), :].rearrange("p (s d) -> p s d", d=D),
                                     rows[b].rearrange("p (s r) -> p s r", r=ROW)[:, :, 0:D]).then_inc(kept[p][b], 16)
                rounds(sp, ROUNDS, keep_round)
                for b in range(2):
                    sp.wait_ge(kept[p][b], 16 * ROUNDS)
                sp.wait_ge(sum_begin[p], 1)

                def back_round(i):
                    for b in range(2):
                        g = 2 * i + b
                        at_least(sp, scaled[p], g - 1)
                        sp.dma_start(rows[b][:, 0:GROUP * D],
                                     rows_d[bass.ds(g * P, P), :]).then_inc(back_in[p][b], 16)
                rounds(sp, ROUNDS, back_round)
                sp.wait_ge(node_ready, 4 + p)
                sp.dma_start(tmp3, hop_d.rearrange("(t p) r -> p t r", p=P)[:, :, 0:D]).then_inc(node_in, 16)
            sp.wait_ge(node_ready, 7)
            sp.dma_start(tmp3, x1_d.rearrange("(t p) d -> p t d", p=P)).then_inc(node_in, 16)
            sp.wait_ge(node_ready, 8)
            sp.dma_start(out_d[0:(HEAD_TILES - 1) * P, :].rearrange("(t p) d -> p t d", p=P),
                         val3[:, 0:HEAD_TILES - 1, :]).then_inc(stored, 16)
            sp.dma_start(out_d[(HEAD_TILES - 1) * P:NODES, :],
                         val3[0:LAST_NODES, HEAD_TILES - 1, :]).then_inc(stored, 16)
            sp.wait_ge(stored, 32)

        @block.gpsimd
        def _(pool):
            g = nc.gpsimd
            steps = [0]

            def link(ins):
                steps[0] += 1
                ins.then_inc(pool_step, 1)
                pool.wait_ge(pool_step, steps[0])

            def diagonal(out, base):
                link(g.memset(out[:], 0.0))
                link(g.affine_select(out=out[:], in_=out[:], compare_op=ALU.not_equal, fill=1.0, base=base,
                                     pattern=[[-1, P]], channel_multiplier=1))

            diagonal(identity, 0)
            diagonal(from_prev, 1)
            diagonal(from_next, -1)
            link(g.memset(earlier[:], 1.0))
            link(g.affine_select(out=earlier[:], in_=earlier[:], compare_op=ALU.is_gt, fill=0.0, base=0,
                                 pattern=[[-1, P]], channel_multiplier=1))
            link(g.memset(lower_of[:], 1.0))
            link(g.affine_select(out=lower_of[:], in_=lower_of[:], compare_op=ALU.is_gt, fill=0.0, base=0,
                                 pattern=[[1, P]], channel_multiplier=-1))
            link(g.memset(ones[:], 1.0))
            link(g.memset(zeros_bf[:], 0.0))
            link(g.iota(iota_i[:], pattern=[[1, P]], base=0, channel_multiplier=0))
            link(g.iota(iota_col_i[:], pattern=[[0, 1]], base=0, channel_multiplier=1))
            link(g.iota(tile_no_i[:], pattern=[[1, BLOCKS]], base=0, channel_multiplier=BLOCKS))
            link(g.memset(emb_t[:], 1.0))
            link(g.memset(stg[:], 0.0))
            g.memset(fcwa[:, D:D + 1], 0.0).then_inc(const_ready, 1)

            pool.wait_ge(blank_done, 16)

            def scatter_round(i):
                for b in range(2):
                    pool.wait_ge(dest_ready, 2 * i + b + 1)
                    pool.sem_inc(lot_begun, 1)
                    for s in range(GROUP):
                        g.indirect_dma_start(
                            out=sorted_d, out_offset=bass.IndirectOffsetOnAxis(ap=dest8[b][:, s:s + 1], axis=0),
                            in_=rec8[b][:, 4 * s:4 * s + 4], in_offset=None,
                            bounds_check=POSITIONS - 1, oob_is_err=False).then_inc(scattered[b], 16)
            rounds(pool, IN_ROUNDS, scatter_round)

            pool.wait_ge(node_out, 16)

            def gather_round0(i):
                for b in range(2):
                    pool.wait_ge(idx_ready[0], 2 * i + b + 1)
                    at_least(pool, scaled[0], 2 * i + b - 1)
                    pool.sem_inc(lot_begun, 1)
                    for s in range(GROUP):
                        g.indirect_dma_start(
                            out=rows[b][:, s * D:(s + 1) * D], out_offset=None, in_=xn_d,
                            in_offset=bass.IndirectOffsetOnAxis(ap=idx8[b][:, s:s + 1], axis=0)).then_inc(gathered[0][b], 16)
            rounds(pool, ROUNDS, gather_round0)

            for p in (1, 2):
                for b in range(2):
                    pool.wait_ge(tab_out[p][b], 16 * (HEAD_TILES // 2))

                def gather_round(i):
                    for b in range(2):
                        pool.wait_ge(idx_ready[p], 2 * i + b + 1)
                        at_least(pool, score_done[p], 2 * i + b - 1)
                        at_least(pool, kept[p][b], 16 * i)
                        pool.sem_inc(lot_begun, 1)
                        for s in range(GROUP):
                            g.indirect_dma_start(
                                out=rows[b][:, s * ROW:(s + 1) * ROW], out_offset=None, in_=hop_d,
                                in_offset=bass.IndirectOffsetOnAxis(ap=idx8[b][:, s:s + 1], axis=0)).then_inc(gathered[p][b], 16)
                rounds(pool, ROUNDS, gather_round)

        def flip_from(n, k):
            src, dst, linear = flips[n]
            return src.rearrange("p (r k) -> p k r", k=BLOCKS)[:, k, :] if linear else src[:, k * P:(k + 1) * P]

        def flip_to(n, k, count):
            src, dst, linear = flips[n]
            if linear:
                return dst[:, k * P:(k + count) * P].rearrange("p (k r) -> p k r", k=count)
            return dst.rearrange("p (r k) -> p k r", k=BLOCKS)[:, k:k + count, :]

        flip_lots = [(k, min(4, BLOCKS - k)) for k in range(0, BLOCKS, 4)]
        FLIP_STEPS = len(flip_lots)
        flip_banks = [banks[5], banks[6]]

        @block.scalar
        def _(act):
            a = nc.scalar
            waits = [0]

            def sort_round(i):
                for b in range(2):
                    grp = 2 * i + b
                    act.wait_ge(ot_ready, grp + 1)
                    at_least(act, queried, GROUP * (grp - 1))
                    a.copy(lo_t[b], banks[3][:].bitcast(BF16)).then_inc(lo_t_ready, 1)
                    for s in range(GROUP):
                        n = grp * GROUP + s
                        act.wait_ge(updated, n + 1)
                        at_least(act, queried, n - 1)
                        a.copy(counts[s % 2], banks[0][:, 0:HEAD_TILES]).then_inc(counts_ready, 1)
            rounds(act, IN_ROUNDS, sort_round)

            def flip(n):
                for m, (k, count) in enumerate(flip_lots):
                    act.wait_ge(flip_mm, FLIP_STEPS * n + m + 1)
                    a.copy(flip_to(n, k, count),
                           flip_banks[m % 2][:, 0:count * P].rearrange("p (k r) -> p k r", k=count)).then_inc(flipped, 1)

            def request(fn):
                waits[0] += 1
                act.wait_ge(act_in, waits[0])
                fn().then_inc(act_out, 1)

            def scale_round(p):
                def one(i):
                    for b in range(2):
                        grp = 2 * i + b
                        if p == 0:
                            act.wait_ge(gathered[0][b], 16 * GROUP * (i + 1))
                        else:
                            act.wait_ge(back_in[p][b], 16 * (i + 1))
                        act.wait_ge(rhs_ready[p], grp + 1)
                        for s in range(GROUP):
                            ins = a.activation(rhs[b][:, s * W0:s * W0 + D], rows[b][:, s * D:(s + 1) * D],
                                               ACT.Copy, scale=rhs[b][:, s * W0 + D:s * W0 + D + 1])
                        ins.then_inc(scaled[p], 1)
                return one

            def table(p):
                act.wait_ge(tab_ready[p], 1)

                def one(i):
                    for b in range(2):
                        t = 2 * i + b
                        at_least(act, tab_out[p][b], 16 * i)
                        a.copy(stg[:, b * ROW:b * ROW + D], val3[:, t, :]).then_inc(tab_emb[p], 1)
                        act.wait_ge(tab_t[p], t + 1)
                        a.copy(emb_t[0:D, b * P:(b + 1) * P], banks[b][0:D, 0:P]).then_inc(tab_copied[p], 1)
                        act.wait_ge(tab_mm[p], t + 1)
                        a.copy(p_tab[:, bass.ds(t * RELS, RELS)], banks[2 + b][:, RELS:2 * RELS])
                        a.copy(stg[:, b * ROW + D:b * ROW + D + RELS], banks[2 + b][:, 0:RELS]).then_inc(tab_staged[p], 1)
                rounds(act, HEAD_TILES // 2, one)

            flip(0)
            request(lambda: a.activation(small_sd, small_sd, ACT.Sqrt))
            request(lambda: a.activation(small_sd, small_sd, ACT.Sqrt))
            flip(1)
            request(lambda: a.activation(scan_b, scan_b, ACT.Sqrt))
            request(lambda: a.activation(scan_b, scan_b, ACT.Exp))
            flip(2)
            flip(3)
            rounds(act, ROUNDS, scale_round(0))
            request(lambda: a.activation(small_sd, small_sd, ACT.Exp))
            request(lambda: a.activation(small_sd, small_sd, ACT.Sqrt))
            for p in (1, 2):
                table(p)
                flip(2 * p + 2)
                request(lambda: a.activation(scan_b, scan_b, ACT.Exp))
                flip(2 * p + 3)
                rounds(act, ROUNDS, scale_round(p))
                request(lambda: a.activation(small_sd, small_sd, ACT.Sqrt))

        @block.vector
        def _(dve):
            v = nc.vector
            steps = [0]
            asked = [0]
            act_asked = [0]
            node_steps = [0]
            flips_asked = [0]
            nodes_loaded = [0]

            def link(ins):
                steps[0] += 1
                ins.then_inc(dve_step, 1)
                dve.wait_ge(dve_step, steps[0])

            def ask():
                asked[0] += 1
                dve.sem_inc(to_pe, 1)
                dve.wait_ge(from_pe, asked[0])

            def ask_act():
                act_asked[0] += 1
                dve.sem_inc(act_in, 1)
                dve.wait_ge(act_out, act_asked[0])

            def flip():
                flips_asked[0] += 1
                dve.sem_inc(flip_ready, 1)
                dve.wait_ge(flipped, FLIP_STEPS * flips_asked[0])

            def node_step():
                dve.sem_inc(node_ready, 1)

            dve.wait_ge(const_ready, 1)
            link(v.tensor_copy(iota_row[:], iota_i[:]))
            link(v.tensor_copy(iota_bf[:], iota_i[:]))
            link(v.tensor_copy(iota_col[:], iota_col_i[:]))
            link(v.tensor_copy(tile_no[:], tile_no_i[:]))
            link(v.tensor_copy(identity_bf[:], identity[:]))

            for n in range(4):
                if n < 3:
                    link(v.memset(stage_f if n == 3 else stage_i, -1 if n == 0 else 0))
                else:
                    link(v.memset(stage_f, 0.0))
                dve.sem_inc(stage_free, 1)
                dve.wait_ge(stage_in, 32 * (n + 1))
                link(v.tensor_copy(rec[:, :, n], stage_f if n == 3 else stage_i))
                if n == 0:
                    link(v.tensor_single_scalar(half_i, stage_i, 127, ALU.bitwise_and))
                    link(v.tensor_copy(lo_bf, half_i))
                    link(v.tensor_single_scalar(half_i, stage_i, 7, ALU.arith_shift_right))
                    link(v.tensor_copy(hi_bf, half_i))
            link(v.memset(blank, 0.0))
            link(v.memset(blank.rearrange("p (j f) -> p j f", f=4)[:, :, 0], -1.0))
            dve.sem_inc(blank_ready, 2)
            dve.wait_ge(loaded, 16 * 5)
            link(v.tensor_scalar_add(params[:, 2:3], params[:, 1:2], 1.0))
            link(v.tensor_copy(fcwb[:, 0:D], fcw_sb[:, D:2 * D]))
            link(v.tensor_copy(fcwa[:, 0:D], fcw_sb[:, 0:D]))
            ask()
            link(v.tensor_copy(relT[:], banks[7][0:D, 0:RELS]))
            ask()
            link(v.tensor_copy(ab[:], banks[7][0:D + 1, 0:2 * RELS]))
            dve.wait_ge(blank_done, 16)

            def one_hots(b, first):
                lo = v.tensor_tensor(oh_lo[b].rearrange("p (s c) -> p s c", s=GROUP),
                                     iota_bf[:].unsqueeze(1).to_broadcast([P, GROUP, P]),
                                     lo_bf[:, bass.ds(first, GROUP)].unsqueeze(2).to_broadcast([P, GROUP, P]),
                                     ALU.is_equal)
                hi = v.tensor_tensor(oh_hi[b].rearrange("p (s c) -> p s c", s=GROUP),
                                     iota_bf[:, 0:HEAD_TILES].unsqueeze(1).to_broadcast([P, GROUP, HEAD_TILES]),
                                     hi_bf[:, bass.ds(first, GROUP)].unsqueeze(2).to_broadcast([P, GROUP, HEAD_TILES]),
                                     ALU.is_equal)
                return lo, hi

            def hist_round(i):
                for b in range(2):
                    grp = 2 * i + b
                    at_least(dve, hist_mm, grp - 1)
                    lo, hi = one_hots(b, grp * GROUP)
                    hi.then_inc(hist_oh, 1)
            rounds(dve, IN_ROUNDS, hist_round)
            dve.wait_ge(hist_mm, IN_GROUPS + 1)
            link(v.tensor_copy(hist, banks[6][:, 0:HEAD_TILES]))
            ask()
            link(v.tensor_scalar(tiles_i, banks[7][:, 0:HEAD_TILES], 127.0, None, ALU.add))
            link(v.tensor_single_scalar(tiles_i, tiles_i, 7, ALU.arith_shift_right))
            link(v.tensor_copy(tiles_f, tiles_i))
            link(v.tensor_tensor_scan(out=cum, data0=ones[:, 0:HEAD_TILES], data1=tiles_f, initial=0.0,
                                      op0=ALU.mult, op1=ALU.add))
            link(v.tensor_tensor(cum_x, cum, tiles_f, ALU.subtract))
            link(v.scalar_tensor_tensor(start_pos, cum_x, float(P), banks[7][:, P:P + HEAD_TILES], ALU.mult, ALU.add))
            for k in range(BLOCKS):
                link(v.tensor_scalar(junk2[0], cum, tile_no[:, k:k + 1], 0.0, ALU.is_le, ALU.add,
                                     accum_out=tile_f[:, k:k + 1]))
            link(v.tensor_scalar(tile_i, tile_f, float(HEAD_TILES - 1), None, ALU.min))
            dve.sem_inc(tile_i_ready, 1)
            dve.sem_inc(to_pe, 1)

            def rank_round(i):
                for b in range(2):
                    grp = 2 * i + b
                    at_least(dve, scattered[b], 16 * GROUP * i)
                    v.tensor_copy(rec8[b].rearrange("p (s f) -> p s f", f=4),
                                  rec[:, bass.ds(grp * GROUP, GROUP), :]).then_inc(rec_ready, 1)
                    at_least(dve, queried, GROUP * (grp - 1))
                    lo, hi = one_hots(b, grp * GROUP)
                    hi.then_inc(oh_ready, 1)
                    dve.wait_ge(rec_ready, grp + 1)
                    dve.wait_ge(oh_ready, grp + 1)
                    for h in range(2):
                        dve.wait_ge(hb_ready, 2 * grp + h + 1)
                        for s in range(4 * h, 4 * h + 4):
                            v.scalar_tensor_tensor(
                                junk[s], banks[1 + h][:, (s % 4) * P:(s % 4 + 1) * P], rec8[b][:, 4 * s:4 * s + 1],
                                earlier[:], ALU.is_equal, ALU.mult, accum_out=occ8[b][:, s:s + 1])
                        dve.wait_ge(queried, GROUP * grp + 4 * h + 4)
                        for s in range(4 * h, 4 * h + 4):
                            ins = v.tensor_tensor_reduce(
                                out=junk2[s],
                                in0=banks[4 + h][:, (s % 4) * HEAD_TILES:(s % 4 + 1) * HEAD_TILES],
                                in1=oh_hi[b][:, s * HEAD_TILES:(s + 1) * HEAD_TILES], scale=1.0, scalar=0.0,
                                op0=ALU.mult, op1=ALU.add, accum_out=base8[b][:, s:s + 1])
                        ins.then_inc(rank_read, 1)
                    dve.wait_ge(rank_read, 2 * grp + 2)
                    v.tensor_tensor(pos8[b], occ8[b], base8[b], ALU.add).then_inc(rank_step, 1)
                    dve.wait_ge(rank_step, 3 * grp + 1)
                    v.tensor_single_scalar(pos_lo, pos8[b], 127, ALU.bitwise_and)
                    v.tensor_single_scalar(pos_hi, pos8[b], 7, ALU.arith_shift_right)
                    v.tensor_scalar(pad8, rec8[b].rearrange("p (s f) -> p s f", f=4)[:, :, 0], 0.0, OUT_OF_BOUNDS,
                                    ALU.is_lt, ALU.mult).then_inc(rank_step, 1)
                    dve.wait_ge(rank_step, 3 * grp + 2)
                    v.scalar_tensor_tensor(dest_f, pos_lo, float(TILES), pos_hi, ALU.mult, ALU.add).then_inc(rank_step, 1)
                    dve.wait_ge(rank_step, 3 * grp + 3)
                    v.tensor_tensor(dest8[b], dest_f, pad8, ALU.add).then_inc(dest_ready, 1)
            rounds(dve, IN_ROUNDS, rank_round)
            dve.wait_ge(dest_ready, IN_GROUPS)
            for b in range(2):
                dve.wait_ge(scattered[b], 16 * GROUP * IN_ROUNDS)
            dve.sem_inc(sort_read, 1)

            dve.wait_ge(srec_in, 16)
            dve.wait_ge(tile_loaded, 16)
            link(v.tensor_copy(em, srec[:, :, 0]))
            link(v.tensor_copy(tail_i, srec[:, :, 1]))
            link(v.tensor_copy(types, srec[:, :, 2]))
            link(v.tensor_copy(weight, srec[:, :, 3]))
            same_i = part(A_NS, TILES, I32)
            link(v.tensor_copy(same_i, em))
            link(v.tensor_single_scalar(same_i, same_i, 127, ALU.bitwise_and))
            link(v.tensor_scalar(scan_a, em, 0.0, -1000.0, ALU.is_lt, ALU.mult))
            link(v.tensor_tensor(local_head, same_i, scan_a, ALU.add))
            flip()
            link(v.tensor_copy(edge_col, scan_a[:, TILES - 1:TILES]))
            ask()
            link(v.tensor_copy(edge_in, banks[7][:, 0:1]))
            link(v.tensor_tensor(same[:, 1:TILES], scan_a[:, 1:TILES], scan_a[:, 0:TILES - 1], ALU.is_equal))
            link(v.tensor_tensor(same[:, 0:1], scan_a[:, 0:1], edge_in, ALU.is_equal))
            link(v.memset(same[0:1, 0:1], 0.0))
            ask()
            link(v.tensor_copy(same[:, TILES:TILES + 1], banks[7][:, 0:1]))
            first = same[:, 0:TILES]
            after = same[:, 1:TILES + 1]

            def layernorm(v3, t3):
                mean = small_mean
                link(v.tensor_reduce(mean, v3, AX.X, ALU.add))
                link(v.tensor_scalar(mean, mean, 1.0 / D, None, ALU.mult))
                link(v.tensor_tensor(v3, v3, mean.unsqueeze(2).to_broadcast([P, HEAD_TILES, D]), ALU.subtract))
                link(v.tensor_tensor(t3, v3, v3, ALU.mult))
                link(v.tensor_reduce(small_sd, t3, AX.X, ALU.add))
                link(v.tensor_scalar(small_sd, small_sd, 1.0 / D, 1e-5, ALU.mult, ALU.add))
                ask_act()
                link(v.reciprocal(small_sd, small_sd))
                link(v.tensor_tensor(v3, v3, small_sd.unsqueeze(2).to_broadcast([P, HEAD_TILES, D]), ALU.mult))
                link(v.tensor_scalar(v3, v3, 0.0, None, ALU.max))

            def unit_rows(v3, t3):
                link(v.tensor_tensor(t3, v3, v3, ALU.mult))
                link(v.tensor_reduce(small_sd, t3, AX.X, ALU.add))
                ask_act()
                link(v.tensor_scalar(small_sd, small_sd, 1e-12, None, ALU.max))
                link(v.reciprocal(small_sd, small_sd))
                link(v.tensor_tensor(v3, v3, small_sd.unsqueeze(2).to_broadcast([P, HEAD_TILES, D]), ALU.mult))

            link(v.memset(val, 0.0))
            node_step()
            dve.wait_ge(node_in, 32)
            layernorm(val3, tmp3)
            unit_rows(val3, tmp3)
            node_step()
            dve.wait_ge(node_out, 16)

            def row_carry(back, biggest):
                ask()
                link(v.tensor_copy(rows1[:, 0:2 * P], banks[7][0:1, 0:2 * P]))
                step = -1 if back else 1
                if back:
                    link(v.memset(carried_row[:, P + 3:P + 4], 0.0))
                    out = carried_row[:, 3:P + 3]
                else:
                    link(v.memset(carried_row[:, 0:1], NEG if biggest else 0.0))
                    out = carried_row[:, 1:P + 1]
                link(v.tensor_tensor_scan(
                    out=out[:, ::step], data0=reset_row[:, ::step], data1=max_row[:, ::step],
                    initial=NEG if biggest else 0.0,
                    op0=ALU.add if biggest else ALU.mult, op1=ALU.max if biggest else ALU.add))
                ask()
                link(v.tensor_copy(carry_in, banks[7][:, 2 * P:2 * P + 1]))

            def forward(out, data0, data1, biggest):
                ops = dict(op0=ALU.add, op1=ALU.max) if biggest else dict(op0=ALU.mult, op1=ALU.add)
                init = NEG if biggest else 0.0
                link(v.tensor_tensor_scan(out=out, data0=data0, data1=data1, initial=init, **ops))
                link(v.tensor_copy(carry_col, out[:, TILES - 1:TILES]))
                link(v.tensor_reduce(reset_col, data0, AX.X, ALU.min))
                row_carry(False, biggest)
                link(v.tensor_tensor_scan(out=out, data0=data0, data1=data1, initial=carry_in, **ops))

            def spread(out, at_end):
                ops = dict(op0=ALU.mult, op1=ALU.add)
                link(v.tensor_tensor_scan(out=out[:, ::-1], data0=after[:, ::-1], data1=at_end[:, ::-1],
                                          initial=0.0, **ops))
                link(v.tensor_copy(carry_col, out[:, 0:1]))
                link(v.tensor_reduce(reset_col, after, AX.X, ALU.min))
                row_carry(True, False)
                link(v.tensor_tensor_scan(out=out[:, ::-1], data0=after[:, ::-1], data1=at_end[:, ::-1],
                                          initial=carry_in, **ops))

            def only_last(out, in_):
                link(v.tensor_tensor(out, in_, after, ALU.mult))
                link(v.tensor_tensor(out, in_, out, ALU.subtract))

            flip()
            link(v.tensor_tensor(scan_b, scan_a, scan_a, ALU.mult))
            forward(scan_c, first, scan_b, False)
            only_last(scan_d, scan_c)
            spread(scan_b, scan_d)
            ask_act()
            link(v.tensor_scalar(scan_b, scan_b, 1e-12, None, ALU.max))
            link(v.reciprocal(scan_b, scan_b))
            link(v.tensor_tensor(scan_a, scan_a, scan_b, ALU.mult))
            link(v.tensor_scalar(scan_a, scan_a, params[:, 0:1], None, ALU.mult))

            def head_max():
                link(v.tensor_scalar(scan_b, first, 1.0, -NEG, ALU.subtract, ALU.mult))
                forward(scan_c, scan_b, scan_a, True)
                only_last(scan_d, scan_c)
                spread(scan_b, scan_d)

            head_max()
            link(v.tensor_scalar(scan_b, scan_b, params[:, 0:1], None, ALU.max))
            link(v.tensor_scalar(scan_c, scan_b, params[:, 0:1], None, ALU.subtract))
            only_last(scan_d, scan_c)
            link(v.tensor_copy(scan_c, scan_d))
            link(v.tensor_tensor(scan_b, scan_a, scan_b, ALU.subtract))
            ask_act()
            flip()
            flip()

            def sums(p):
                link(v.memset(acc, 0.0))
                dve.sem_inc(sum_begin[p], 1)

                def prepare(i, b):
                    grp = 2 * i + b
                    if p == 0:
                        at_least(dve, gathered[0][b], 16 * GROUP * i)
                        v.tensor_copy(idx8[b], tail_i[:, bass.ds(grp * GROUP, GROUP)]).then_inc(idx_ready[0], 1)
                    at_least(dve, summed[p], grp - 1)
                    r3 = rhs[b].rearrange("p (s c) -> p s c", c=W0)
                    v.tensor_copy(r3[:, :, D], weight[:, bass.ds(grp * GROUP, GROUP)])
                    if p == 0:
                        v.tensor_copy(r3[:, :, D + 1], em[:, bass.ds(grp * GROUP, GROUP)])
                    v.tensor_tensor(oh[b].rearrange("p (s c) -> p s c", s=GROUP),
                                    iota_row[:].unsqueeze(1).to_broadcast([P, GROUP, P]),
                                    local_head[:, bass.ds(grp * GROUP, GROUP)].unsqueeze(2).to_broadcast([P, GROUP, P]),
                                    ALU.is_equal).then_inc(rhs_ready[p], 1)

                def add(grp, b):
                    width = W0 if p == 0 else W0 - 1
                    _, tiles = nc.values_load_multi_w_load_instructions(
                        tile_of[:, bass.ds(grp * GROUP, GROUP)], engines=[mybir.EngineType.DVE], min_val=0,
                        max_val=HEAD_TILES - 1, skip_runtime_bounds_check_because="clamped when made")
                    dve.wait_ge(summed[p], grp + 1)
                    for s in range(GROUP):
                        at_least(dve, added[p], grp * GROUP + s)
                        to = acc[:, bass.ds(tiles[s] * W0, width)]
                        v.tensor_tensor(to, to, banks[2 * b + s // 4][:, (s % 4) * W0:(s % 4) * W0 + width],
                                        ALU.add).then_inc(added[p], 1)

                def sum_round(i):
                    prepare(i, 0)
                    if not (isinstance(i, int) and i == 0):
                        add(2 * i - 1, 1)
                    prepare(i, 1)
                    add(2 * i, 0)
                rounds(dve, ROUNDS, sum_round)
                add(GROUPS - 1, 1)
                dve.wait_ge(added[p], TILES)

            sums(0)
            link(v.tensor_copy(small_mean, acc3[:, :, D + 1]))
            link(v.tensor_scalar(small_sd, small_mean, -1.0, None, ALU.mult))
            ask_act()
            link(v.memset(val, 0.0))
            node_step()
            dve.wait_ge(node_in, 32 + 48)
            sd3 = small_sd.unsqueeze(2).to_broadcast([P, HEAD_TILES, D])
            link(v.tensor_tensor(small_mean, acc3[:, :, D], small_sd, ALU.add))
            link(v.tensor_scalar(small_mean, small_mean, 1e-16, None, ALU.add))
            link(v.reciprocal(small_mean, small_mean))
            link(v.tensor_tensor(scratch3, tmp3, sd3, ALU.mult))
            link(v.tensor_tensor(acc3[:, :, 0:D], acc3[:, :, 0:D], scratch3, ALU.add))
            link(v.tensor_tensor(acc3[:, :, 0:D], acc3[:, :, 0:D],
                                 small_mean.unsqueeze(2).to_broadcast([P, HEAD_TILES, D]), ALU.mult))
            link(v.tensor_scalar(tmp, tmp, params[:, 2:3], None, ALU.mult))
            link(v.tensor_tensor(tmp3, tmp3, acc3[:, :, 0:D], ALU.add))
            link(v.tensor_tensor(val, val, tmp, ALU.add))
            node_step()
            dve.wait_ge(node_out, 32)
            layernorm(val3, tmp3)

            def scores(p):
                def prepare(i, b):
                    grp = 2 * i + b
                    at_least(dve, gathered[p][b], 16 * GROUP * i)
                    v.tensor_copy(idx8[b], tail_i[:, bass.ds(grp * GROUP, GROUP)]).then_inc(idx_ready[p], 1)
                    at_least(dve, hlb_ready[p], 2 * grp - 2)
                    v.tensor_copy(hl8[b], local_head[:, bass.ds(grp * GROUP, GROUP)]).then_inc(hl_ready[p], 1)
                    v.tensor_tensor(type_oh[b].rearrange("p (s c) -> p s c", s=GROUP),
                                    iota_row[:, 0:RELS].unsqueeze(1).to_broadcast([P, GROUP, RELS]),
                                    types[:, bass.ds(grp * GROUP, GROUP)].unsqueeze(2).to_broadcast([P, GROUP, RELS]),
                                    ALU.is_equal).then_inc(toh_ready[p], 1)
                    at_least(dve, p_done[p], grp - 1)
                    for h in range(2):
                        dve.wait_ge(hlb_ready[p], 2 * grp + h + 1)
                        v.tensor_scalar(oh[b][:, h * 512:(h + 1) * 512], banks[4 + h][:], iota_col[:], None,
                                        ALU.is_equal).then_inc(oht_ready[p], 1)

                def score(grp, i, b):
                    z3 = zed.rearrange("p (s c) -> p s c", s=GROUP)
                    dve.wait_ge(gathered[p][b], 16 * GROUP * (i + 1))
                    dve.wait_ge(p_done[p], grp + 1)
                    at_least(dve, score_done[p], grp)
                    v.tensor_tensor(z3, banks[b][:, 0:GROUP * RELS].rearrange("p (s c) -> p s c", s=GROUP),
                                    rows[b].rearrange("p (s r) -> p s r", r=ROW)[:, :, D:D + RELS],
                                    ALU.add).then_inc(z_step[p], 1)
                    dve.wait_ge(toh_ready[p], grp + 1)
                    dve.wait_ge(z_step[p], 2 * grp + 1)
                    v.tensor_tensor(zed, zed, type_oh[b], ALU.mult).then_inc(z_step[p], 1)
                    dve.wait_ge(z_step[p], 2 * grp + 2)
                    v.tensor_reduce(em[:, bass.ds(grp * GROUP, GROUP)], z3, AX.X, ALU.add).then_inc(score_done[p], 1)

                def score_round(i):
                    prepare(i, 0)
                    if not (isinstance(i, int) and i == 0):
                        score(2 * i - 1, i - 1, 1)
                    prepare(i, 1)
                    score(2 * i, i, 0)
                rounds(dve, ROUNDS, score_round)
                score(GROUPS - 1, ROUNDS - 1, 1)
                dve.wait_ge(score_done[p], GROUPS)

            for p in (1, 2):
                dve.sem_inc(tab_ready[p], 1)
                for b in range(2):
                    dve.wait_ge(tab_out[p][b], 16 * (HEAD_TILES // 2))
                dve.wait_ge(tab_staged[p], HEAD_TILES)
                scores(p)
                for b in range(2):
                    dve.wait_ge(kept[p][b], 16 * ROUNDS)
                flip()
                link(v.scalar_tensor_tensor(scan_a, scan_a, LEAKY, scan_a, ALU.mult, ALU.max))
                head_max()
                link(v.tensor_tensor(scan_b, scan_a, scan_b, ALU.subtract))
                ask_act()
                flip()
                sums(p)
                node_step()
                link(v.tensor_scalar(small_mean, acc3[:, :, D], 1e-30, None, ALU.max))
                link(v.reciprocal(small_mean, small_mean))
                link(v.tensor_tensor(val3, acc3[:, :, 0:D], small_mean.unsqueeze(2).to_broadcast([P, HEAD_TILES, D]),
                                     ALU.mult))
                dve.wait_ge(node_in, 80 + 16 * p)
                link(v.tensor_tensor(val, val, tmp, ALU.add))
                unit_rows(val3, tmp3)
            node_step()
            dve.wait_ge(node_in, 80 + 48)
            link(v.tensor_tensor(val, val, tmp, ALU.add))
            node_step()

        @block.tensor
        def _(pe):
            t = nc.tensor
            asked = [0]

            def run(lot):
                asked[0] += 1
                pe.wait_ge(to_pe, asked[0])
                for kind, out, lhs, r in lot[:-1]:
                    (t.transpose(out, lhs, r) if kind == "T" else t.matmul(out, lhs, r, start=True, stop=True))
                kind, out, lhs, r = lot[-1]
                (t.transpose(out, lhs, r) if kind == "T"
                 else t.matmul(out, lhs, r, start=True, stop=True)).then_inc(from_pe, 1)

            def carry(back):
                run([("T", banks[7][0:1, 0:P], carry_col, identity[:]),
                     ("T", banks[7][0:1, P:2 * P], reset_col, identity[:])])
                at = 4 if back else 0
                run([("T", banks[7][:, 2 * P:2 * P + 1], carried_row[:, at:at + P], identity[0:1, 0:1])])

            run([("T", banks[7][0:D, 0:RELS], rel_sb[:], identity[0:RELS, 0:RELS])])
            run([("M", banks[7][0:D + 1, 0:RELS], fcwb[:], relT[:]),
                 ("M", banks[7][0:D + 1, RELS:2 * RELS], fcwa[:], relT[:])])

            count = banks[6][:, 0:HEAD_TILES]
            t.matmul(count, zeros_bf[:], zeros_bf[:, 0:HEAD_TILES], start=True, stop=False, skip_group_check=True)

            def hist_round(i):
                for b in range(2):
                    pe.wait_ge(hist_oh, 2 * i + b + 1)
                    for s in range(GROUP):
                        ins = t.matmul(count, oh_lo[b][:, s * P:(s + 1) * P],
                                       oh_hi[b][:, s * HEAD_TILES:(s + 1) * HEAD_TILES],
                                       start=False, stop=False, skip_group_check=True)
                    ins.then_inc(hist_mm, 1)
            rounds(pe, IN_ROUNDS, hist_round)
            t.matmul(count, zeros_bf[:], zeros_bf[:, 0:HEAD_TILES], start=False, stop=True,
                     skip_group_check=True).then_inc(hist_mm, 1)
            run([("M", banks[7][:, 0:HEAD_TILES], ones[:], hist),
                 ("M", banks[7][:, P:P + HEAD_TILES], lower_of[:], hist)])

            nxt = banks[0][:, 0:HEAD_TILES]
            asked[0] += 1
            pe.wait_ge(to_pe, asked[0])
            t.matmul(nxt, identity[:], start_pos, start=True, stop=False, skip_group_check=True).then_inc(updated, 1)

            def rank_round(i):
                for b in range(2):
                    grp = 2 * i + b
                    pe.wait_ge(rec_ready, grp + 1)
                    for h in range(2):
                        at_least(pe, rank_read, 2 * grp + h - 1)
                        for s in range(4 * h, 4 * h + 4):
                            ins = t.transpose(banks[1 + h][:, (s % 4) * P:(s % 4 + 1) * P],
                                              rec8[b][:, 4 * s:4 * s + 1].to_broadcast([P, P]), identity[:])
                        ins.then_inc(hb_ready, 1)
                    pe.wait_ge(oh_ready, grp + 1)
                    at_least(pe, lo_t_ready, grp)
                    for s in range(GROUP):
                        ins = t.transpose(banks[3][:].bitcast(BF16)[:, s * P:(s + 1) * P],
                                          oh_lo[b][:, s * P:(s + 1) * P], identity_bf[:])
                    ins.then_inc(ot_ready, 1)
                    for s in range(GROUP):
                        n = grp * GROUP + s
                        pe.wait_ge(counts_ready, n + 1)
                        t.matmul(nxt, oh_lo[b][:, s * P:(s + 1) * P], oh_hi[b][:, s * HEAD_TILES:(s + 1) * HEAD_TILES],
                                 start=False, stop=False, skip_group_check=True).then_inc(updated, 1)
                        if s == 0:
                            pe.wait_ge(lo_t_ready, grp + 1)
                        h = s // 4
                        t.matmul(banks[4 + h][:, (s % 4) * HEAD_TILES:(s % 4 + 1) * HEAD_TILES],
                                 lo_t[b][:, s * P:(s + 1) * P], counts[s % 2], start=True, stop=True).then_inc(queried, 1)
            rounds(pe, IN_ROUNDS, rank_round)

            def flip(n):
                pe.wait_ge(flip_ready, n + 1)
                for m, (k, count) in enumerate(flip_lots):
                    at_least(pe, flipped, FLIP_STEPS * n + m - 1)
                    for c in range(count):
                        ins = t.transpose(flip_banks[m % 2][:, c * P:(c + 1) * P], flip_from(n, k + c), identity[:])
                    ins.then_inc(flip_mm, 1)

            flip(0)
            run([("M", banks[7][:, 0:1], from_prev[:], edge_col)])
            run([("M", banks[7][:, 0:1], from_next[:], same[:, 0:1])])
            flip(1)
            carry(False)
            carry(True)
            carry(False)
            carry(True)
            flip(2)
            flip(3)

            def sums(p):
                width = W0 if p == 0 else W0 - 1

                def one(i):
                    for b in range(2):
                        grp = 2 * i + b
                        pe.wait_ge(rhs_ready[p], grp + 1)
                        pe.wait_ge(scaled[p], grp + 1)
                        at_least(pe, added[p], GROUP * (grp - 1))
                        for s in range(GROUP):
                            ins = t.matmul(banks[2 * b + s // 4][:, (s % 4) * W0:(s % 4) * W0 + width],
                                           oh[b][:, s * P:(s + 1) * P], rhs[b][:, s * W0:s * W0 + width],
                                           start=True, stop=True)
                        ins.then_inc(summed[p], 1)
                rounds(pe, ROUNDS, one)

            sums(0)
            for p in (1, 2):
                pe.wait_ge(tab_ready[p], 1)

                def tab_round(i):
                    for b in range(2):
                        pe.wait_ge(tab_emb[p], 2 * i + b + 1)
                        at_least(pe, tab_copied[p], 2 * i + b - 1)
                        t.transpose(banks[b][:, 0:P], stg[:, b * ROW:(b + 1) * ROW], identity[:]).then_inc(tab_t[p], 1)
                        pe.wait_ge(tab_copied[p], 2 * i + b + 1)
                        at_least(pe, tab_staged[p], 2 * i + b - 1)
                        t.matmul(banks[2 + b][:, 0:2 * RELS], emb_t[:, b * P:(b + 1) * P], ab[:],
                                 start=True, stop=True).then_inc(tab_mm[p], 1)
                rounds(pe, HEAD_TILES // 2, tab_round)
                pe.wait_ge(tab_staged[p], HEAD_TILES)

                def p_round(i):
                    for b in range(2):
                        grp = 2 * i + b
                        pe.wait_ge(hl_ready[p], grp + 1)
                        for h in range(2):
                            at_least(pe, oht_ready[p], 2 * grp + h - 1)
                            for s in range(4 * h, 4 * h + 4):
                                ins = t.transpose(banks[4 + h][:, (s % 4) * P:(s % 4 + 1) * P],
                                                  hl8[b][:, s:s + 1].to_broadcast([P, P]), identity[:])
                            ins.then_inc(hlb_ready[p], 1)
                        _, tiles = nc.values_load_multi_w_load_instructions(
                            tile_of[:, bass.ds(grp * GROUP, GROUP)], engines=[mybir.EngineType.PE], min_val=0,
                            max_val=HEAD_TILES - 1, skip_runtime_bounds_check_because="clamped when made")
                        at_least(pe, z_step[p], 2 * grp - 3)
                        for h in range(2):
                            pe.wait_ge(oht_ready[p], 2 * grp + h + 1)
                            for s in range(4 * h, 4 * h + 4):
                                ins = t.matmul(banks[b][:, s * RELS:(s + 1) * RELS], oh[b][:, s * P:(s + 1) * P],
                                               p_tab[:, bass.ds(tiles[s] * RELS, RELS)], start=True, stop=True)
                        ins.then_inc(p_done[p], 1)
                rounds(pe, ROUNDS, p_round)
                flip(2 * p + 2)
                carry(False)
                carry(True)
                flip(2 * p + 3)
                sums(p)


_INS = ['x', 'src', 'dst', 'edge_type_50', 'edge_weight', 'L0_gnn_beta', 'L0_gnn_eps', 'L1_gnn_relation_emb',
        'L1_gnn_fc_w', 'L1_gnn_fc_b']


def kernel(**inputs):
    import numpy as _np
    import concourse.bacc as _bacc
    from concourse import mybir as _mybir
    from concourse.bass_utils import run_bass_kernel_spmd as _run

    nc = _bacc.Bacc("TRN2", target_bir_lowering=False, num_devices=1)
    arrays, args = {}, []
    for name in _INS:
        a = _np.ascontiguousarray(inputs[name])
        arrays[f"in_{name}"] = a
        args.append(nc.dram_tensor(f"in_{name}", a.shape, _mybir.dt.from_np(a.dtype), kind="ExternalInput").ap())
    out = nc.dram_tensor("out_x", (NODES, D), _mybir.dt.float32, kind="ExternalOutput").ap()
    build(nc, *args, out)
    r = _run(nc, [arrays], core_ids=[0])
    return r.results[0]["out_x"]
```

```python
import numpy as np
import concourse.bass as bass
from concourse import mybir
from contextlib import ExitStack

F32 = mybir.dt.float32
BF16 = mybir.dt.bfloat16
I32 = mybir.dt.int32
ALU = mybir.AluOpType
ACT = mybir.ActivationFunctionType
AX = mybir.AxisListType

P = 128
NODES, D = 12500, 64
EDGES = 412500
RELS = 50
HEAD_TILES = -(-NODES // P)
LAST_NODES = NODES - (HEAD_TILES - 1) * P
PER_PART = -(-EDGES // P)
LAST_PART = EDGES - (P - 1) * PER_PART
GROUP = 8
PAIRS = GROUP // 2
HALF = GROUP // 2
TAB = 7
TAB_STEPS = HEAD_TILES // TAB
assert TAB * TAB_STEPS == HEAD_TILES and TAB_STEPS % 2 == 0
UNROLL = 2
DEPTH = 4
IN_GROUPS = -(-PER_PART // (GROUP * DEPTH)) * DEPTH
IN_TILES = IN_GROUPS * GROUP
BLOCKS = -(-(PER_PART + HEAD_TILES) // P)
TILES = BLOCKS * P
GROUPS = TILES // GROUP
POSITIONS = TILES * P
TABLE = HEAD_TILES * P
ROW = 128
W0 = D + 2
WINDOW = HALF * W0
NEG = -1.5e38
LEAKY = 0.2
OUT_OF_BOUNDS = float(1 << 20)


def at_least(engine, sem, value):
    if isinstance(value, int) and value <= 0:
        return
    engine.wait_ge(sem, value)


def rounds(engine, count, body):
    body(0)
    with engine.Fori(1, count - 1) as i:
        body(i)
    body(count - 1)


def build(nc, x_d, src_d, dst_d, type_d, weight_d, beta_d, eps_d, rel_d, fcw_d, fcb_d, out_d):
    def dram(name, shape, dt=F32):
        return nc.dram_tensor(name, shape, dt, kind="Internal").ap()

    sorted_d = dram("sorted_records", (POSITIONS, 4))
    tile_of_d = dram("head_tile_of", (TILES,), I32)
    xn_d = dram("xn_table", (TABLE, D))
    x1_d = dram("x1_rows", (TABLE, D))
    hop_d = dram("hop_table", (TABLE, ROW))
    rows_d = dram("gathered_rows", (GROUPS * P, GROUP * D))

    ctx = ExitStack()
    with ctx:
        def sb(name, shape, dt=F32):
            return ctx.enter_context(nc.sbuf_tensor(name, shape, dt))

        def bank(name):
            return ctx.enter_context(nc.psum_tensor(name, [P, 512], F32))

        def sem(name):
            return ctx.enter_context(nc.semaphore(name))

        identity = sb("identity", [P, P])
        identity_bf = sb("identity_bf", [P, P], BF16)
        iota_i = sb("iota_i", [P, P], I32)
        iota_row = sb("iota_row", [P, P])
        iota_bf = sb("iota_bf", [P, P], BF16)
        iota_col_i = sb("iota_col_i", [P, 1], I32)
        iota_col = sb("iota_col", [P, 1])
        tile_no_i = sb("tile_no_i", [P, BLOCKS], I32)
        tile_no = sb("tile_no", [P, BLOCKS])
        earlier2 = sb("earlier2", [P, 2 * P])
        earlier = earlier2[:, P:2 * P]
        lower_of = sb("lower_of", [P, P])
        ones = sb("ones", [P, P])
        from_prev = sb("from_prev", [P, P])
        from_next = sb("from_next", [P, P])
        zeros_bf = sb("zeros_bf", [P, P], BF16)
        zeros_wide = sb("zeros_wide", [P, WINDOW], BF16)
        params = sb("params", [P, 4])
        small = sb("small", [P, 8])
        small_sd = sb("small_sd", [P, HEAD_TILES])[:]
        small_mean = sb("small_mean", [P, HEAD_TILES])[:]
        rows1 = sb("rows1", [1, 4 * P + 8])
        fcw_sb = sb("fcw_sb", [D, 2 * D])
        fcwb = sb("fcwb", [D, D + 1])
        fcwa = sb("fcwa", [D, D + 1])
        rel_sb = sb("rel_sb", [RELS, D])
        relT = sb("relT", [D, RELS])
        ab = sb("ab", [D + 1, 2 * RELS])

        A_TAIL, A_TYPE, A_HL, A_WT, A_EM, A_NS = (n * TILES for n in range(6))
        A_TJ = A_NS + TILES + 4
        A_ACC = A_TJ + TILES
        A_P = A_ACC + (HEAD_TILES + HALF - 1) * W0
        A_V = A_P + HEAD_TILES * RELS
        A_T = A_V + HEAD_TILES * D
        A_END = A_T + HEAD_TILES * D
        arena = sb("arena", [P, A_END])

        def part(at, size, dt=F32):
            v = arena[:, at:at + size]
            return v if dt == F32 else v.bitcast(dt)

        tail_i = part(A_TAIL, TILES, I32)
        types = part(A_TYPE, TILES)
        local_head = part(A_HL, TILES)
        weight = part(A_WT, TILES)
        em = part(A_EM, TILES)
        same = part(A_NS, TILES + 1)
        tile_of = part(A_TJ, TILES, I32)[0:1, :]
        acc = part(A_ACC, (HEAD_TILES + HALF - 1) * W0)
        acc3 = acc[:, 0:HEAD_TILES * W0].rearrange("p (t c) -> p t c", c=W0)
        p_tab = part(A_P, HEAD_TILES * RELS)
        val = part(A_V, HEAD_TILES * D)
        val3 = val.rearrange("p (t d) -> p t d", d=D)
        tmp = part(A_T, HEAD_TILES * D)
        tmp3 = tmp.rearrange("p (t d) -> p t d", d=D)
        scan_a = part(A_ACC, TILES)
        scan_b = part(A_ACC + TILES, TILES)
        scan_c = part(A_ACC + 2 * TILES, TILES)
        scan_d = part(A_ACC + 3 * TILES, TILES)

        S_REC = A_ACC
        S_STG = S_REC + 4 * IN_TILES
        S_LO = S_STG + IN_TILES
        S_HI = S_LO + IN_TILES // 2
        rec = part(S_REC, 4 * IN_TILES).rearrange("p (j f) -> p j f", f=4)
        stage_i = part(S_STG, IN_TILES, I32)
        stage_f = part(S_STG, IN_TILES)
        lo_bf = part(S_LO, IN_TILES // 2, BF16)
        hi_bf = part(S_HI, IN_TILES // 2, BF16)
        half_i = part(0, IN_TILES, I32)
        blank = part(0, 4 * TILES)
        srec = part(S_REC, 4 * TILES).rearrange("p (j f) -> p j f", f=4)
        at = 0

        def take(size, dt=F32):
            nonlocal at
            v = part(at, size, dt)
            at += size
            return v

        oh_lo = [take(GROUP * P // 2, BF16) for _ in range(2)]
        oh_hi = [take(GROUP * HEAD_TILES // 2, BF16) for _ in range(2)]
        lo_t = [take(GROUP * P) for _ in range(2)]
        counts = [take(HEAD_TILES) for _ in range(2)]
        rec8 = [take(4 * GROUP) for _ in range(DEPTH)]
        junk = [take(2 * P) for _ in range(GROUP)]
        junk2 = [take(HEAD_TILES) for _ in range(GROUP)]
        occ8 = [take(GROUP) for _ in range(2)]
        base8 = [take(GROUP) for _ in range(2)]
        pos8 = [take(GROUP, I32) for _ in range(2)]
        pos_lo = take(GROUP, I32)
        pos_hi = take(GROUP, I32)
        pad8 = take(GROUP)
        dest_f = take(GROUP)
        dest8 = [take(GROUP, I32) for _ in range(DEPTH)]
        hist = take(HEAD_TILES)
        tiles_i = take(HEAD_TILES, I32)
        tiles_f = take(HEAD_TILES)
        cum = take(HEAD_TILES)
        cum_x = take(HEAD_TILES)
        start_pos = take(HEAD_TILES)
        tile_f = take(BLOCKS)
        tile_i = take(BLOCKS, I32)
        assert at <= A_TJ

        at = A_V
        rows = [take(GROUP * ROW) for _ in range(DEPTH)]
        rhs = [take(GROUP * W0) for _ in range(2)]
        oh = [take(GROUP * P) for _ in range(2)]
        idx8 = [take(GROUP, I32) for _ in range(DEPTH)]
        hl8 = [take(GROUP) for _ in range(2)]
        type_oh = [take(GROUP * RELS) for _ in range(2)]
        zed = take(GROUP * RELS)
        assert at <= A_END
        scratch3 = part(A_WT, HEAD_TILES * D).rearrange("p (t d) -> p t d", d=D)
        stg = [part(A_T + n * TAB * ROW, TAB * ROW).rearrange("p (m r) -> p m r", r=ROW) for n in range(2)]
        emb_t = [part(A_T + (2 + n) * TAB * P, TAB * P)[0:D + 1, :] for n in range(2)]
        assert A_T + 4 * TAB * P <= A_END

        banks = [bank(f"bank{n}") for n in range(8)]

        loaded = sem("loaded")
        const_ready = sem("const_ready")
        pool_step = sem("pool_step")
        dve_step = sem("dve_step")
        stage_in = sem("stage_in")
        stage_free = sem("stage_free")
        blank_ready = sem("blank_ready")
        blank_done = sem("blank_done")
        hist_oh = sem("hist_oh")
        hist_mm = sem("hist_mm")
        to_pe = sem("to_pe")
        from_pe = sem("from_pe")
        tile_i_ready = sem("tile_i_ready")
        tile_saved = sem("tile_saved")
        tile_loaded = sem("tile_loaded")
        rec_ready = sem("rec_ready")
        oh_ready = sem("oh_ready")
        hb_ready = sem("hb_ready")
        ot_ready = sem("ot_ready")
        lo_t_ready = sem("lo_t_ready")
        counts_ready = sem("counts_ready")
        updated = sem("updated")
        queried = sem("queried")
        rank_read = sem("rank_read")
        heads_read = sem("heads_read")
        rank_step = sem("rank_step")
        lot_begun = sem("lot_begun")
        dest_ready = sem("dest_ready")
        scattered = [sem(f"scattered{k}") for k in range(DEPTH)]
        srec_in = sem("srec_in")
        sort_read = sem("sort_read")
        flip_ready = sem("flip_ready")
        flip_mm = sem("flip_mm")
        flipped = sem("flipped")
        act_in = sem("act_in")
        act_out = sem("act_out")
        node_in = sem("node_in")
        node_ready = sem("node_ready")
        node_out = sem("node_out")
        tab_ready = [None, sem("tab_ready1"), sem("tab_ready2")]
        tab_emb = [None, sem("tab_emb1"), sem("tab_emb2")]
        tab_t = [None, sem("tab_t1"), sem("tab_t2")]
        tab_copied = [None, sem("tab_copied1"), sem("tab_copied2")]
        tab_mm = [None, sem("tab_mm1"), sem("tab_mm2")]
        tab_staged = [None, sem("tab_staged1"), sem("tab_staged2")]
        tab_out = [None, [sem("tab_out1a"), sem("tab_out1b")], [sem("tab_out2a"), sem("tab_out2b")]]
        idx_ready = [sem(f"idx_ready{p}") for p in range(3)]
        gathered = [[sem(f"gathered{p}{k}") for k in range(DEPTH)] for p in range(3)]
        hl_ready = [None] + [sem(f"hl_ready{p}") for p in (1, 2)]
        hlb_ready = [None] + [sem(f"hlb_ready{p}") for p in (1, 2)]
        oht_ready = [None] + [sem(f"oht_ready{p}") for p in (1, 2)]
        toh_ready = [None] + [sem(f"toh_ready{p}") for p in (1, 2)]
        p_done = [None] + [sem(f"p_done{p}") for p in (1, 2)]
        z_step = [None] + [sem(f"z_step{p}") for p in (1, 2)]
        score_done = [None] + [sem(f"score_done{p}") for p in (1, 2)]
        kept = [None] + [[sem(f"kept{p}{k}") for k in range(DEPTH)] for p in (1, 2)]
        back_in = [None] + [[sem(f"back_in{p}{k}") for k in range(DEPTH)] for p in (1, 2)]
        sum_begin = [sem(f"sum_begin{p}") for p in range(3)]
        rhs_ready = [sem(f"rhs_ready{p}") for p in range(3)]
        scaled = [sem(f"scaled{p}") for p in range(3)]
        summed = [sem(f"summed{p}") for p in range(3)]
        added = [sem(f"added{p}") for p in range(3)]
        stored = sem("stored")

        block = ctx.enter_context(nc.Block())

        IN_ROUNDS = IN_GROUPS // UNROLL
        RANK_ROUNDS = IN_GROUPS // DEPTH
        GATHER_ROUNDS = GROUPS // DEPTH
        ROUNDS = GROUPS // UNROLL
        flips = [(em, scan_a, True)]
        flips += [(weight, scan_a, True), (scan_b, weight, False), (scan_c, em, False)]
        flips += [(em, scan_a, True), (scan_b, weight, False)] * 2

        carry_col = small[:, 0:1]
        reset_col = small[:, 1:2]
        carry_in = small[:, 2:3]
        edge_col = small[:, 3:4]
        edge_in = small[:, 4:5]
        max_row = rows1[:, 0:P]
        reset_row = rows1[:, P:2 * P]
        carried_row = rows1[:, 2 * P:3 * P + 4]

        @block.sync
        def _(sp):
            sp.dma_start(params[:, 0:1], beta_d[:].unsqueeze(0).to_broadcast([P, 1])).then_inc(loaded, 16)
            sp.dma_start(params[:, 1:2], eps_d[:].unsqueeze(0).to_broadcast([P, 1])).then_inc(loaded, 16)
            sp.dma_start(fcw_sb[:], fcw_d).then_inc(loaded, 16)
            sp.dma_start(fcwb[:, D:D + 1], fcb_d[:].unsqueeze(1)).then_inc(loaded, 16)
            sp.dma_start(rel_sb[:], rel_d).then_inc(loaded, 16)
            for n, (col, view) in enumerate([(src_d, stage_i), (dst_d, stage_i), (type_d, stage_i), (weight_d, stage_f)]):
                sp.wait_ge(stage_free, n + 1)
                sp.dma_start(view[0:P - 1, 0:PER_PART],
                             col[0:(P - 1) * PER_PART].rearrange("(p j) -> p j", p=P - 1)).then_inc(stage_in, 16)
                sp.dma_start(view[P - 1:P, 0:LAST_PART],
                             col[(P - 1) * PER_PART:EDGES].unsqueeze(0)).then_inc(stage_in, 16)
            sp.wait_ge(blank_ready, 2)
            sp.dma_start(sorted_d.rearrange("(p j) f -> p (j f)", p=P), blank).then_inc(blank_done, 16)
            sp.wait_ge(tile_i_ready, 1)
            sp.dma_start(tile_of_d.rearrange("(r k) -> r k", k=BLOCKS), tile_i).then_inc(tile_saved, 16)
            sp.wait_ge(tile_saved, 16)
            sp.dma_start(tile_of, tile_of_d.unsqueeze(0)).then_inc(tile_loaded, 16)
            for k in range(DEPTH):
                sp.wait_ge(scattered[k], 16 * GROUP * RANK_ROUNDS)
            sp.wait_ge(sort_read, 1)
            sp.dma_start(part(S_REC, 4 * TILES), sorted_d.rearrange("(p j) f -> p (j f)", p=P)).then_inc(srec_in, 16)

            def load_nodes(view3, table, n_ready, whole=True):
                sp.wait_ge(node_ready, n_ready)
                if whole:
                    sp.dma_start(view3, table.rearrange("(t p) d -> p t d", p=P)).then_inc(node_in, 16)
                else:
                    sp.dma_start(view3[:, 0:HEAD_TILES - 1, :],
                                 table[0:(HEAD_TILES - 1) * P, :].rearrange("(t p) d -> p t d", p=P)).then_inc(node_in, 16)
                    sp.dma_start(view3[0:LAST_NODES, HEAD_TILES - 1, :],
                                 table[(HEAD_TILES - 1) * P:NODES, :]).then_inc(node_in, 16)

            load_nodes(val3, x_d, 1, whole=False)
            sp.wait_ge(node_ready, 2)
            sp.dma_start(xn_d.rearrange("(t p) d -> p t d", p=P), val3).then_inc(node_out, 16)
            load_nodes(val3, x_d, 3, whole=False)
            load_nodes(tmp3, xn_d, 3)
            sp.wait_ge(node_ready, 4)
            sp.dma_start(x1_d.rearrange("(t p) d -> p t d", p=P), val3).then_inc(node_out, 16)
            for p in (1, 2):
                for n in range(TAB_STEPS):
                    sp.wait_ge(tab_staged[p], n + 1)
                    sp.dma_start(hop_d[n * TAB * P:(n + 1) * TAB * P, :].rearrange("(m p) r -> p m r", p=P),
                                 stg[n % 2]).then_inc(tab_out[p][n % 2], 16)

                def keep_round(i):
                    for k in range(DEPTH):
                        sp.wait_ge(gathered[p][k], 16 * GROUP * (i + 1))
                        g = DEPTH * i + k
                        sp.dma_start(rows_d[bass.ds(g * P, P), :].rearrange("p (s d) -> p s d", d=D),
                                     rows[k].rearrange("p (s r) -> p s r", r=ROW)[:, :, 0:D]).then_inc(kept[p][k], 16)
                rounds(sp, GATHER_ROUNDS, keep_round)
                for k in range(DEPTH):
                    sp.wait_ge(kept[p][k], 16 * GATHER_ROUNDS)
                sp.wait_ge(sum_begin[p], 1)

                def back_round(i):
                    for k in range(DEPTH):
                        g = DEPTH * i + k
                        at_least(sp, scaled[p], g - DEPTH + 1)
                        sp.dma_start(rows[k][:, 0:GROUP * D],
                                     rows_d[bass.ds(g * P, P), :]).then_inc(back_in[p][k], 16)
                rounds(sp, GATHER_ROUNDS, back_round)
                sp.wait_ge(node_ready, 4 + p)
                sp.dma_start(tmp3, hop_d.rearrange("(t p) r -> p t r", p=P)[:, :, 0:D]).then_inc(node_in, 16)
            sp.wait_ge(node_ready, 7)
            sp.dma_start(tmp3, x1_d.rearrange("(t p) d -> p t d", p=P)).then_inc(node_in, 16)
            sp.wait_ge(node_ready, 8)
            sp.dma_start(out_d[0:(HEAD_TILES - 1) * P, :].rearrange("(t p) d -> p t d", p=P),
                         val3[:, 0:HEAD_TILES - 1, :]).then_inc(stored, 16)
            sp.dma_start(out_d[(HEAD_TILES - 1) * P:NODES, :],
                         val3[0:LAST_NODES, HEAD_TILES - 1, :]).then_inc(stored, 16)
            sp.wait_ge(stored, 32)

        @block.gpsimd
        def _(pool):
            g = nc.gpsimd
            steps = [0]

            def link(ins):
                steps[0] += 1
                ins.then_inc(pool_step, 1)
                pool.wait_ge(pool_step, steps[0])

            def diagonal(out, base):
                link(g.memset(out[:], 0.0))
                link(g.affine_select(out=out[:], in_=out[:], compare_op=ALU.not_equal, fill=1.0, base=base,
                                     pattern=[[-1, P]], channel_multiplier=1))

            diagonal(identity, 0)
            diagonal(from_prev, 1)
            diagonal(from_next, -1)
            link(g.memset(earlier2[:], 1.0))
            link(g.affine_select(out=earlier, in_=earlier, compare_op=ALU.is_gt, fill=0.0, base=0,
                                 pattern=[[-1, P]], channel_multiplier=1))
            link(g.memset(lower_of[:], 1.0))
            link(g.affine_select(out=lower_of[:], in_=lower_of[:], compare_op=ALU.is_gt, fill=0.0, base=0,
                                 pattern=[[1, P]], channel_multiplier=-1))
            link(g.memset(ones[:], 1.0))
            link(g.memset(zeros_bf[:], 0.0))
            link(g.memset(zeros_wide[:], 0.0))
            link(g.iota(iota_i[:], pattern=[[1, P]], base=0, channel_multiplier=0))
            link(g.iota(iota_col_i[:], pattern=[[0, 1]], base=0, channel_multiplier=1))
            link(g.iota(tile_no_i[:], pattern=[[1, BLOCKS]], base=0, channel_multiplier=BLOCKS))
            g.memset(fcwa[:, D:D + 1], 0.0).then_inc(const_ready, 1)

            pool.wait_ge(blank_done, 16)

            def scatter_round(i):
                for k in range(DEPTH):
                    pool.wait_ge(dest_ready, DEPTH * i + k + 1)
                    pool.sem_inc(lot_begun, 1)
                    for s in range(GROUP):
                        g.indirect_dma_start(
                            out=sorted_d, out_offset=bass.IndirectOffsetOnAxis(ap=dest8[k][:, s:s + 1], axis=0),
                            in_=rec8[k][:, 4 * s:4 * s + 4], in_offset=None,
                            bounds_check=POSITIONS - 1, oob_is_err=False).then_inc(scattered[k], 16)
            rounds(pool, RANK_ROUNDS, scatter_round)

            pool.wait_ge(node_out, 16)

            def gather_round0(i):
                for k in range(DEPTH):
                    grp = DEPTH * i + k
                    pool.wait_ge(idx_ready[0], grp + 1)
                    at_least(pool, scaled[0], grp - DEPTH + 1)
                    pool.sem_inc(lot_begun, 1)
                    for s in range(GROUP):
                        g.indirect_dma_start(
                            out=rows[k][:, s * D:(s + 1) * D], out_offset=None, in_=xn_d,
                            in_offset=bass.IndirectOffsetOnAxis(ap=idx8[k][:, s:s + 1], axis=0)).then_inc(gathered[0][k], 16)
            rounds(pool, GATHER_ROUNDS, gather_round0)

            for p in (1, 2):
                for b in range(2):
                    pool.wait_ge(tab_out[p][b], 16 * (TAB_STEPS // 2))

                def gather_round(i):
                    for k in range(DEPTH):
                        grp = DEPTH * i + k
                        pool.wait_ge(idx_ready[p], grp + 1)
                        at_least(pool, score_done[p], grp - DEPTH + 1)
                        at_least(pool, kept[p][k], 16 * i)
                        pool.sem_inc(lot_begun, 1)
                        for s in range(GROUP):
                            g.indirect_dma_start(
                                out=rows[k][:, s * ROW:(s + 1) * ROW], out_offset=None, in_=hop_d,
                                in_offset=bass.IndirectOffsetOnAxis(ap=idx8[k][:, s:s + 1], axis=0)).then_inc(gathered[p][k], 16)
                rounds(pool, GATHER_ROUNDS, gather_round)

        def flip_from(n, k):
            src, dst, linear = flips[n]
            return src.rearrange("p (r k) -> p k r", k=BLOCKS)[:, k, :] if linear else src[:, k * P:(k + 1) * P]

        def flip_to(n, k, count):
            src, dst, linear = flips[n]
            if linear:
                return dst[:, k * P:(k + count) * P].rearrange("p (k r) -> p k r", k=count)
            return dst.rearrange("p (r k) -> p k r", k=BLOCKS)[:, k:k + count, :]

        flip_lots = [(k, min(4, BLOCKS - k)) for k in range(0, BLOCKS, 4)]
        FLIP_STEPS = len(flip_lots)
        flip_banks = [banks[5], banks[6]]

        @block.scalar
        def _(act):
            a = nc.scalar
            waits = [0]

            def copy_lo(grp, b):
                act.wait_ge(ot_ready, grp + 1)
                at_least(act, queried, PAIRS * (grp - 1))
                a.copy(lo_t[b], banks[6 + b][:].bitcast(BF16)).then_inc(lo_t_ready, 1)

            def sort_round(i):
                for k in range(DEPTH):
                    grp = DEPTH * i + k
                    for s in range(PAIRS):
                        n = grp * PAIRS + s
                        act.wait_ge(updated, n + 1)
                        at_least(act, queried, n - 1)
                        a.copy(counts[s % 2], banks[0][:, 0:HEAD_TILES]).then_inc(counts_ready, 1)
                        if s == PAIRS - 1 and not (isinstance(grp, int) and grp == IN_GROUPS - 1):
                            copy_lo(grp + 1, (k + 1) % 2)
            copy_lo(0, 0)
            rounds(act, RANK_ROUNDS, sort_round)

            def flip(n):
                for m, (k, count) in enumerate(flip_lots):
                    act.wait_ge(flip_mm, FLIP_STEPS * n + m + 1)
                    a.copy(flip_to(n, k, count),
                           flip_banks[m % 2][:, 0:count * P].rearrange("p (k r) -> p k r", k=count)).then_inc(flipped, 1)

            def request(fn):
                waits[0] += 1
                act.wait_ge(act_in, waits[0])
                fn().then_inc(act_out, 1)

            def scale_round(p):
                def one(i):
                    for k in range(DEPTH):
                        grp, b = DEPTH * i + k, k % 2
                        if p == 0:
                            act.wait_ge(gathered[0][k], 16 * GROUP * (i + 1))
                        else:
                            act.wait_ge(back_in[p][k], 16 * (i + 1))
                        act.wait_ge(rhs_ready[p], grp + 1)
                        for s in range(GROUP):
                            ins = a.activation(rhs[b][:, s * W0:s * W0 + D], rows[k][:, s * D:(s + 1) * D],
                                               ACT.Copy, scale=rhs[b][:, s * W0 + D:s * W0 + D + 1])
                        ins.then_inc(scaled[p], 1)
                return one

            def table(p):
                act.wait_ge(tab_ready[p], 1)
                for n in range(TAB_STEPS):
                    b = n % 2
                    at_least(act, tab_out[p][b], 16 * (n // 2))
                    a.copy(stg[b][:, :, 0:D], val3[:, n * TAB:(n + 1) * TAB, :]).then_inc(tab_emb[p], 1)
                    act.wait_ge(tab_t[p], n + 1)
                    at_least(act, tab_mm[p], n - 1)
                    a.copy(emb_t[b][0:D, 0:4 * P], banks[2 * b][0:D, :])
                    a.copy(emb_t[b][0:D, 4 * P:TAB * P], banks[2 * b + 1][0:D, 0:(TAB - 4) * P]).then_inc(tab_copied[p], 1)

            flip(0)
            request(lambda: a.activation(small_sd, small_sd, ACT.Sqrt))
            request(lambda: a.activation(small_sd, small_sd, ACT.Sqrt))
            flip(1)
            request(lambda: a.activation(scan_b, scan_b, ACT.Sqrt))
            request(lambda: a.activation(scan_b, scan_b, ACT.Exp))
            flip(2)
            flip(3)
            rounds(act, GATHER_ROUNDS, scale_round(0))
            request(lambda: a.activation(small_sd, small_sd, ACT.Exp))
            request(lambda: a.activation(small_sd, small_sd, ACT.Sqrt))
            for p in (1, 2):
                table(p)
                flip(2 * p + 2)
                request(lambda: a.activation(scan_b, scan_b, ACT.Exp))
                flip(2 * p + 3)
                rounds(act, GATHER_ROUNDS, scale_round(p))
                request(lambda: a.activation(small_sd, small_sd, ACT.Sqrt))

        @block.vector
        def _(dve):
            v = nc.vector
            steps = [0]
            asked = [0]
            act_asked = [0]
            node_steps = [0]
            flips_asked = [0]
            nodes_loaded = [0]

            def link(ins):
                steps[0] += 1
                ins.then_inc(dve_step, 1)
                dve.wait_ge(dve_step, steps[0])

            def ask():
                asked[0] += 1
                dve.sem_inc(to_pe, 1)
                dve.wait_ge(from_pe, asked[0])

            def ask_act():
                act_asked[0] += 1
                dve.sem_inc(act_in, 1)
                dve.wait_ge(act_out, act_asked[0])

            def flip():
                flips_asked[0] += 1
                dve.sem_inc(flip_ready, 1)
                dve.wait_ge(flipped, FLIP_STEPS * flips_asked[0])

            def node_step():
                dve.sem_inc(node_ready, 1)

            dve.wait_ge(const_ready, 1)
            link(v.tensor_copy(iota_row[:], iota_i[:]))
            link(v.tensor_copy(iota_bf[:], iota_i[:]))
            link(v.tensor_copy(iota_col[:], iota_col_i[:]))
            link(v.tensor_copy(tile_no[:], tile_no_i[:]))
            link(v.tensor_copy(identity_bf[:], identity[:]))

            for n in range(4):
                if n < 3:
                    link(v.memset(stage_f if n == 3 else stage_i, -1 if n == 0 else 0))
                else:
                    link(v.memset(stage_f, 0.0))
                dve.sem_inc(stage_free, 1)
                dve.wait_ge(stage_in, 32 * (n + 1))
                link(v.tensor_copy(rec[:, :, n], stage_f if n == 3 else stage_i))
                if n == 0:
                    link(v.tensor_single_scalar(half_i, stage_i, 127, ALU.bitwise_and))
                    link(v.tensor_copy(lo_bf, half_i))
                    link(v.tensor_single_scalar(half_i, stage_i, 7, ALU.arith_shift_right))
                    link(v.tensor_copy(hi_bf, half_i))
            link(v.memset(blank, 0.0))
            link(v.memset(blank.rearrange("p (j f) -> p j f", f=4)[:, :, 0], -1.0))
            dve.sem_inc(blank_ready, 2)
            dve.wait_ge(loaded, 16 * 5)
            link(v.tensor_scalar_add(params[:, 2:3], params[:, 1:2], 1.0))
            link(v.tensor_copy(fcwb[:, 0:D], fcw_sb[:, D:2 * D]))
            link(v.tensor_copy(fcwa[:, 0:D], fcw_sb[:, 0:D]))
            ask()
            link(v.tensor_copy(relT[:], banks[7][0:D, 0:RELS]))
            ask()
            link(v.tensor_copy(ab[:], banks[7][0:D + 1, 0:2 * RELS]))
            dve.wait_ge(blank_done, 16)

            def one_hots(b, first):
                lo = v.tensor_tensor(oh_lo[b].rearrange("p (s c) -> p s c", s=GROUP),
                                     iota_bf[:].unsqueeze(1).to_broadcast([P, GROUP, P]),
                                     lo_bf[:, bass.ds(first, GROUP)].unsqueeze(2).to_broadcast([P, GROUP, P]),
                                     ALU.is_equal)
                hi = v.tensor_tensor(oh_hi[b].rearrange("p (s c) -> p s c", s=GROUP),
                                     iota_bf[:, 0:HEAD_TILES].unsqueeze(1).to_broadcast([P, GROUP, HEAD_TILES]),
                                     hi_bf[:, bass.ds(first, GROUP)].unsqueeze(2).to_broadcast([P, GROUP, HEAD_TILES]),
                                     ALU.is_equal)
                return lo, hi

            def hist_round(i):
                for b in range(2):
                    grp = 2 * i + b
                    at_least(dve, hist_mm, grp - 1)
                    lo, hi = one_hots(b, grp * GROUP)
                    hi.then_inc(hist_oh, 1)
            rounds(dve, IN_ROUNDS, hist_round)
            dve.wait_ge(hist_mm, IN_GROUPS + 1)
            link(v.tensor_copy(hist, banks[6][:, 0:HEAD_TILES]))
            ask()
            link(v.tensor_scalar(tiles_i, banks[7][:, 0:HEAD_TILES], 127.0, None, ALU.add))
            link(v.tensor_single_scalar(tiles_i, tiles_i, 7, ALU.arith_shift_right))
            link(v.tensor_scalar(tiles_f, tiles_i, 1.0, None, ALU.max))
            link(v.tensor_tensor_scan(out=cum, data0=ones[:, 0:HEAD_TILES], data1=tiles_f, initial=0.0,
                                      op0=ALU.mult, op1=ALU.add))
            link(v.tensor_tensor(cum_x, cum, tiles_f, ALU.subtract))
            link(v.scalar_tensor_tensor(start_pos, cum_x, float(P), banks[7][:, P:P + HEAD_TILES], ALU.mult, ALU.add))
            for k in range(BLOCKS):
                link(v.tensor_scalar(junk2[0], cum, tile_no[:, k:k + 1], 0.0, ALU.is_le, ALU.add,
                                     accum_out=tile_f[:, k:k + 1]))
            link(v.tensor_scalar(tile_i, tile_f, float(HEAD_TILES - 1), None, ALU.min))
            dve.sem_inc(tile_i_ready, 1)
            dve.sem_inc(to_pe, 1)

            def prepare_rank(i, k):
                grp, b = DEPTH * i + k, k % 2
                at_least(dve, scattered[k], 16 * GROUP * i)
                v.tensor_copy(rec8[k].rearrange("p (s f) -> p s f", f=4),
                              rec[:, bass.ds(grp * GROUP, GROUP), :]).then_inc(rec_ready, 1)
                at_least(dve, queried, PAIRS * (grp - 1))
                lo, hi = one_hots(b, grp * GROUP)
                hi.then_inc(oh_ready, 1)

            def rank(grp, k):
                b = k % 2
                dve.wait_ge(rec_ready, grp + 1)
                dve.wait_ge(oh_ready, grp + 1)
                at_least(dve, rank_step, 3 * grp)
                for h in range(2):
                    dve.wait_ge(hb_ready, 2 * grp + h + 1)
                    at_least(dve, rank_read, 2 * grp)
                    for s in range(4 * h, 4 * h + 4):
                        width = P * (1 + s % 2)
                        ins = v.scalar_tensor_tensor(
                            junk[s][:, 0:width], banks[1 + h][:, (s % 4 + 1) * P - width:(s % 4 + 1) * P],
                            rec8[k][:, 4 * s:4 * s + 1], earlier2[:, 2 * P - width:2 * P],
                            ALU.is_equal, ALU.mult, accum_out=occ8[b][:, s:s + 1])
                    ins.then_inc(heads_read, 1)
                for h in range(2):
                    dve.wait_ge(queried, PAIRS * grp + 2 * h + 2)
                    for s in range(4 * h, 4 * h + 4):
                        ins = v.tensor_tensor_reduce(
                            out=junk2[s],
                            in0=banks[4 + h][:, (s % 4) * HEAD_TILES:(s % 4 + 1) * HEAD_TILES],
                            in1=oh_hi[b][:, s * HEAD_TILES:(s + 1) * HEAD_TILES], scale=1.0, scalar=0.0,
                            op0=ALU.mult, op1=ALU.add, accum_out=base8[b][:, s:s + 1])
                    ins.then_inc(rank_read, 1)
                dve.wait_ge(rank_read, 2 * grp + 2)
                v.tensor_tensor(pos8[b], occ8[b], base8[b], ALU.add).then_inc(rank_step, 1)
                dve.wait_ge(rank_step, 3 * grp + 1)
                v.tensor_single_scalar(pos_lo, pos8[b], 127, ALU.bitwise_and)
                v.tensor_single_scalar(pos_hi, pos8[b], 7, ALU.arith_shift_right)
                v.tensor_scalar(pad8, rec8[k].rearrange("p (s f) -> p s f", f=4)[:, :, 0], 0.0, OUT_OF_BOUNDS,
                                ALU.is_lt, ALU.mult).then_inc(rank_step, 1)
                dve.wait_ge(rank_step, 3 * grp + 2)
                v.scalar_tensor_tensor(dest_f, pos_lo, float(TILES), pos_hi, ALU.mult, ALU.add).then_inc(rank_step, 1)
                dve.wait_ge(rank_step, 3 * grp + 3)
                v.tensor_tensor(dest8[k], dest_f, pad8, ALU.add).then_inc(dest_ready, 1)

            def rank_round(i):
                for k in range(DEPTH):
                    prepare_rank(i, k)
                    if not (isinstance(i, int) and i == k == 0):
                        rank(DEPTH * i + k - 1, (k - 1) % DEPTH)
            rounds(dve, RANK_ROUNDS, rank_round)
            rank(IN_GROUPS - 1, DEPTH - 1)
            dve.wait_ge(dest_ready, IN_GROUPS)
            for k in range(DEPTH):
                dve.wait_ge(scattered[k], 16 * GROUP * RANK_ROUNDS)
            dve.sem_inc(sort_read, 1)

            dve.wait_ge(srec_in, 16)
            dve.wait_ge(tile_loaded, 16)
            link(v.tensor_copy(em, srec[:, :, 0]))
            link(v.tensor_copy(tail_i, srec[:, :, 1]))
            link(v.tensor_copy(types, srec[:, :, 2]))
            link(v.tensor_copy(weight, srec[:, :, 3]))
            same_i = part(A_NS, TILES, I32)
            link(v.tensor_copy(same_i, em))
            link(v.tensor_single_scalar(same_i, same_i, 127, ALU.bitwise_and))
            link(v.tensor_scalar(scan_a, em, 0.0, -1000.0, ALU.is_lt, ALU.mult))
            link(v.tensor_tensor(local_head, same_i, scan_a, ALU.add))
            flip()
            link(v.tensor_copy(edge_col, scan_a[:, TILES - 1:TILES]))
            ask()
            link(v.tensor_copy(edge_in, banks[7][:, 0:1]))
            link(v.tensor_tensor(same[:, 1:TILES], scan_a[:, 1:TILES], scan_a[:, 0:TILES - 1], ALU.is_equal))
            link(v.tensor_tensor(same[:, 0:1], scan_a[:, 0:1], edge_in, ALU.is_equal))
            link(v.memset(same[0:1, 0:1], 0.0))
            ask()
            link(v.tensor_copy(same[:, TILES:TILES + 1], banks[7][:, 0:1]))
            first = same[:, 0:TILES]
            after = same[:, 1:TILES + 1]

            def layernorm(v3, t3):
                mean = small_mean
                link(v.tensor_reduce(mean, v3, AX.X, ALU.add))
                link(v.tensor_scalar(mean, mean, 1.0 / D, None, ALU.mult))
                link(v.tensor_tensor(v3, v3, mean.unsqueeze(2).to_broadcast([P, HEAD_TILES, D]), ALU.subtract))
                link(v.tensor_tensor(t3, v3, v3, ALU.mult))
                link(v.tensor_reduce(small_sd, t3, AX.X, ALU.add))
                link(v.tensor_scalar(small_sd, small_sd, 1.0 / D, 1e-5, ALU.mult, ALU.add))
                ask_act()
                link(v.reciprocal(small_sd, small_sd))
                link(v.tensor_tensor(v3, v3, small_sd.unsqueeze(2).to_broadcast([P, HEAD_TILES, D]), ALU.mult))
                link(v.tensor_scalar(v3, v3, 0.0, None, ALU.max))

            def unit_rows(v3, t3):
                link(v.tensor_tensor(t3, v3, v3, ALU.mult))
                link(v.tensor_reduce(small_sd, t3, AX.X, ALU.add))
                ask_act()
                link(v.tensor_scalar(small_sd, small_sd, 1e-12, None, ALU.max))
                link(v.reciprocal(small_sd, small_sd))
                link(v.tensor_tensor(v3, v3, small_sd.unsqueeze(2).to_broadcast([P, HEAD_TILES, D]), ALU.mult))

            link(v.memset(val, 0.0))
            node_step()
            dve.wait_ge(node_in, 32)
            layernorm(val3, tmp3)
            unit_rows(val3, tmp3)
            node_step()
            dve.wait_ge(node_out, 16)

            def row_carry(back, biggest):
                ask()
                link(v.tensor_copy(rows1[:, 0:2 * P], banks[7][0:1, 0:2 * P]))
                step = -1 if back else 1
                if back:
                    link(v.memset(carried_row[:, P + 3:P + 4], 0.0))
                    out = carried_row[:, 3:P + 3]
                else:
                    link(v.memset(carried_row[:, 0:1], NEG if biggest else 0.0))
                    out = carried_row[:, 1:P + 1]
                link(v.tensor_tensor_scan(
                    out=out[:, ::step], data0=reset_row[:, ::step], data1=max_row[:, ::step],
                    initial=NEG if biggest else 0.0,
                    op0=ALU.add if biggest else ALU.mult, op1=ALU.max if biggest else ALU.add))
                ask()
                link(v.tensor_copy(carry_in, banks[7][:, 2 * P:2 * P + 1]))

            def forward(out, data0, data1, biggest):
                ops = dict(op0=ALU.add, op1=ALU.max) if biggest else dict(op0=ALU.mult, op1=ALU.add)
                init = NEG if biggest else 0.0
                link(v.tensor_tensor_scan(out=out, data0=data0, data1=data1, initial=init, **ops))
                link(v.tensor_copy(carry_col, out[:, TILES - 1:TILES]))
                link(v.tensor_reduce(reset_col, data0, AX.X, ALU.min))
                row_carry(False, biggest)
                link(v.tensor_tensor_scan(out=out, data0=data0, data1=data1, initial=carry_in, **ops))

            def spread(out, at_end):
                ops = dict(op0=ALU.mult, op1=ALU.add)
                link(v.tensor_tensor_scan(out=out[:, ::-1], data0=after[:, ::-1], data1=at_end[:, ::-1],
                                          initial=0.0, **ops))
                link(v.tensor_copy(carry_col, out[:, 0:1]))
                link(v.tensor_reduce(reset_col, after, AX.X, ALU.min))
                row_carry(True, False)
                link(v.tensor_tensor_scan(out=out[:, ::-1], data0=after[:, ::-1], data1=at_end[:, ::-1],
                                          initial=carry_in, **ops))

            def only_last(out, in_):
                link(v.tensor_tensor(out, in_, after, ALU.mult))
                link(v.tensor_tensor(out, in_, out, ALU.subtract))

            flip()
            link(v.tensor_tensor(scan_b, scan_a, scan_a, ALU.mult))
            forward(scan_c, first, scan_b, False)
            only_last(scan_d, scan_c)
            spread(scan_b, scan_d)
            ask_act()
            link(v.tensor_scalar(scan_b, scan_b, 1e-12, None, ALU.max))
            link(v.reciprocal(scan_b, scan_b))
            link(v.tensor_tensor(scan_a, scan_a, scan_b, ALU.mult))
            link(v.tensor_scalar(scan_a, scan_a, params[:, 0:1], None, ALU.mult))

            def head_max():
                link(v.tensor_scalar(scan_b, first, 1.0, -NEG, ALU.subtract, ALU.mult))
                forward(scan_c, scan_b, scan_a, True)
                only_last(scan_d, scan_c)
                spread(scan_b, scan_d)

            head_max()
            link(v.tensor_scalar(scan_b, scan_b, params[:, 0:1], None, ALU.max))
            link(v.tensor_scalar(scan_c, scan_b, params[:, 0:1], None, ALU.subtract))
            only_last(scan_d, scan_c)
            link(v.tensor_copy(scan_c, scan_d))
            link(v.tensor_tensor(scan_b, scan_a, scan_b, ALU.subtract))
            ask_act()
            flip()
            flip()

            def sums(p):
                link(v.memset(acc, 0.0))
                dve.sem_inc(sum_begin[p], 1)

                def indices(i, k):
                    at_least(dve, gathered[0][k], 16 * GROUP * i)
                    v.tensor_copy(idx8[k], tail_i[:, bass.ds((DEPTH * i + k) * GROUP, GROUP)]).then_inc(idx_ready[0], 1)

                def prepare(grp, b):
                    at_least(dve, summed[p], 2 * grp - 2)
                    r3 = rhs[b].rearrange("p (s c) -> p s c", c=W0)
                    v.tensor_copy(r3[:, :, D], weight[:, bass.ds(grp * GROUP, GROUP)])
                    if p == 0:
                        v.tensor_copy(r3[:, :, D + 1], em[:, bass.ds(grp * GROUP, GROUP)])
                    v.tensor_tensor(oh[b].rearrange("p (s c) -> p s c", s=GROUP),
                                    iota_row[:].unsqueeze(1).to_broadcast([P, GROUP, P]),
                                    local_head[:, bass.ds(grp * GROUP, GROUP)].unsqueeze(2).to_broadcast([P, GROUP, P]),
                                    ALU.is_equal).then_inc(rhs_ready[p], 1)

                def add(grp, b):
                    width = W0 if p == 0 else W0 - 1
                    _, tiles = nc.values_load_multi_w_load_instructions(
                        tile_of[:, bass.ds(grp * GROUP, GROUP)], engines=[mybir.EngineType.DVE], min_val=0,
                        max_val=HEAD_TILES - 1, skip_runtime_bounds_check_because="clamped when made")
                    for h in range(2):
                        dve.wait_ge(summed[p], 2 * grp + h + 1)
                        at_least(dve, added[p], 2 * grp + h)
                        to = acc[:, bass.ds(tiles[HALF * h] * W0, WINDOW)]
                        v.tensor_tensor(to, to, banks[2 * b + h][:, 0:WINDOW], ALU.add).then_inc(added[p], 1)

                def sum_round(i):
                    for k in range(DEPTH):
                        if p == 0 and not isinstance(i, int):
                            indices(i + (k + 2) // DEPTH, (k + 2) % DEPTH)
                        elif p == 0 and DEPTH * i + k + 2 < GROUPS:
                            indices(i + (k + 2) // DEPTH, (k + 2) % DEPTH)
                        prepare(DEPTH * i + k, k % 2)
                        if not (isinstance(i, int) and i == k == 0):
                            add(DEPTH * i + k - 1, (k - 1) % 2)
                if p == 0:
                    indices(0, 0)
                    indices(0, 1)
                rounds(dve, GATHER_ROUNDS, sum_round)
                add(GROUPS - 1, 1)
                dve.wait_ge(added[p], 2 * GROUPS)

            sums(0)
            link(v.tensor_copy(small_mean, acc3[:, :, D + 1]))
            link(v.tensor_scalar(small_sd, small_mean, -1.0, None, ALU.mult))
            ask_act()
            link(v.memset(val, 0.0))
            node_step()
            dve.wait_ge(node_in, 32 + 48)
            sd3 = small_sd.unsqueeze(2).to_broadcast([P, HEAD_TILES, D])
            link(v.tensor_tensor(small_mean, acc3[:, :, D], small_sd, ALU.add))
            link(v.tensor_scalar(small_mean, small_mean, 1e-16, None, ALU.add))
            link(v.reciprocal(small_mean, small_mean))
            link(v.tensor_tensor(scratch3, tmp3, sd3, ALU.mult))
            link(v.tensor_tensor(acc3[:, :, 0:D], acc3[:, :, 0:D], scratch3, ALU.add))
            link(v.tensor_tensor(acc3[:, :, 0:D], acc3[:, :, 0:D],
                                 small_mean.unsqueeze(2).to_broadcast([P, HEAD_TILES, D]), ALU.mult))
            link(v.tensor_scalar(tmp, tmp, params[:, 2:3], None, ALU.mult))
            link(v.tensor_tensor(tmp3, tmp3, acc3[:, :, 0:D], ALU.add))
            link(v.tensor_tensor(val, val, tmp, ALU.add))
            node_step()
            dve.wait_ge(node_out, 32)
            layernorm(val3, tmp3)

            def scores(p):
                def indices(i, k):
                    at_least(dve, gathered[p][k], 16 * GROUP * i)
                    v.tensor_copy(idx8[k], tail_i[:, bass.ds((DEPTH * i + k) * GROUP, GROUP)]).then_inc(idx_ready[p], 1)

                def prepare(grp, b):
                    at_least(dve, hlb_ready[p], 2 * grp - 2)
                    v.tensor_copy(hl8[b], local_head[:, bass.ds(grp * GROUP, GROUP)]).then_inc(hl_ready[p], 1)
                    v.tensor_tensor(type_oh[b].rearrange("p (s c) -> p s c", s=GROUP),
                                    iota_row[:, 0:RELS].unsqueeze(1).to_broadcast([P, GROUP, RELS]),
                                    types[:, bass.ds(grp * GROUP, GROUP)].unsqueeze(2).to_broadcast([P, GROUP, RELS]),
                                    ALU.is_equal).then_inc(toh_ready[p], 1)
                    at_least(dve, p_done[p], grp - 1)
                    for h in range(2):
                        dve.wait_ge(hlb_ready[p], 2 * grp + h + 1)
                        v.tensor_scalar(oh[b][:, h * 512:(h + 1) * 512], banks[4 + h][:], iota_col[:], None,
                                        ALU.is_equal).then_inc(oht_ready[p], 1)

                def score(grp, i, k):
                    b = k % 2
                    z3 = zed.rearrange("p (s c) -> p s c", s=GROUP)
                    dve.wait_ge(gathered[p][k], 16 * GROUP * (i + 1))
                    dve.wait_ge(p_done[p], grp + 1)
                    at_least(dve, score_done[p], grp)
                    v.tensor_tensor(z3, banks[b][:, 0:GROUP * RELS].rearrange("p (s c) -> p s c", s=GROUP),
                                    rows[k].rearrange("p (s r) -> p s r", r=ROW)[:, :, D:D + RELS],
                                    ALU.add).then_inc(z_step[p], 1)
                    dve.wait_ge(toh_ready[p], grp + 1)
                    dve.wait_ge(z_step[p], 2 * grp + 1)
                    v.tensor_tensor(zed, zed, type_oh[b], ALU.mult).then_inc(z_step[p], 1)
                    dve.wait_ge(z_step[p], 2 * grp + 2)
                    v.tensor_reduce(em[:, bass.ds(grp * GROUP, GROUP)], z3, AX.X, ALU.add).then_inc(score_done[p], 1)

                def score_round(i):
                    for k in range(DEPTH):
                        if not isinstance(i, int) or DEPTH * i + k + 2 < GROUPS:
                            indices(i + (k + 2) // DEPTH, (k + 2) % DEPTH)
                        prepare(DEPTH * i + k, k % 2)
                        if not (isinstance(i, int) and i == k == 0):
                            score(DEPTH * i + k - 1, i - (k == 0), (k - 1) % DEPTH)
                indices(0, 0)
                indices(0, 1)
                rounds(dve, GATHER_ROUNDS, score_round)
                score(GROUPS - 1, GATHER_ROUNDS - 1, DEPTH - 1)
                dve.wait_ge(score_done[p], GROUPS)

            for p in (1, 2):
                link(v.memset(part(A_T, 2 * TAB * ROW), 0.0))
                link(v.memset(part(A_T + 2 * TAB * P, 2 * TAB * P), 1.0))
                dve.sem_inc(tab_ready[p], 1)
                for n in range(TAB_STEPS):
                    b = n % 2
                    dve.wait_ge(tab_mm[p], n + 1)
                    for m, count in ((0, 4), (4, TAB - 4)):
                        both = banks[4 + 2 * b + m // 4][:, 0:count * 2 * RELS].rearrange("p (m c) -> p m c", m=count)
                        v.tensor_copy(stg[b][:, m:m + count, D:D + RELS], both[:, :, 0:RELS])
                        first_rel = (n * TAB + m) * RELS
                        ins = v.tensor_copy(p_tab[:, first_rel:first_rel + count * RELS].rearrange("p (m c) -> p m c", m=count),
                                            both[:, :, RELS:2 * RELS])
                    ins.then_inc(tab_staged[p], 1)
                for b in range(2):
                    dve.wait_ge(tab_out[p][b], 16 * (TAB_STEPS // 2))
                scores(p)
                for k in range(DEPTH):
                    dve.wait_ge(kept[p][k], 16 * GATHER_ROUNDS)
                flip()
                link(v.scalar_tensor_tensor(scan_a, scan_a, LEAKY, scan_a, ALU.mult, ALU.max))
                head_max()
                link(v.tensor_tensor(scan_b, scan_a, scan_b, ALU.subtract))
                ask_act()
                flip()
                sums(p)
                node_step()
                link(v.tensor_scalar(small_mean, acc3[:, :, D], 1e-30, None, ALU.max))
                link(v.reciprocal(small_mean, small_mean))
                link(v.tensor_tensor(val3, acc3[:, :, 0:D], small_mean.unsqueeze(2).to_broadcast([P, HEAD_TILES, D]),
                                     ALU.mult))
                dve.wait_ge(node_in, 80 + 16 * p)
                link(v.tensor_tensor(val, val, tmp, ALU.add))
                unit_rows(val3, tmp3)
            node_step()
            dve.wait_ge(node_in, 80 + 48)
            link(v.tensor_tensor(val, val, tmp, ALU.add))
            node_step()

        @block.tensor
        def _(pe):
            t = nc.tensor
            asked = [0]

            def run(lot):
                asked[0] += 1
                pe.wait_ge(to_pe, asked[0])
                for kind, out, lhs, r in lot[:-1]:
                    (t.transpose(out, lhs, r) if kind == "T" else t.matmul(out, lhs, r, start=True, stop=True))
                kind, out, lhs, r = lot[-1]
                (t.transpose(out, lhs, r) if kind == "T"
                 else t.matmul(out, lhs, r, start=True, stop=True)).then_inc(from_pe, 1)

            def carry(back):
                run([("T", banks[7][0:1, 0:P], carry_col, identity[:]),
                     ("T", banks[7][0:1, P:2 * P], reset_col, identity[:])])
                at = 4 if back else 0
                run([("T", banks[7][:, 2 * P:2 * P + 1], carried_row[:, at:at + P], identity[0:1, 0:1])])

            run([("T", banks[7][0:D, 0:RELS], rel_sb[:], identity[0:RELS, 0:RELS])])
            run([("M", banks[7][0:D + 1, 0:RELS], fcwb[:], relT[:]),
                 ("M", banks[7][0:D + 1, RELS:2 * RELS], fcwa[:], relT[:])])

            count = banks[6][:, 0:HEAD_TILES]
            t.matmul(count, zeros_bf[:], zeros_bf[:, 0:HEAD_TILES], start=True, stop=False, skip_group_check=True)

            def hist_round(i):
                for b in range(2):
                    pe.wait_ge(hist_oh, 2 * i + b + 1)
                    for s in range(GROUP):
                        ins = t.matmul(count, oh_lo[b][:, s * P:(s + 1) * P],
                                       oh_hi[b][:, s * HEAD_TILES:(s + 1) * HEAD_TILES],
                                       start=False, stop=False, skip_group_check=True)
                    ins.then_inc(hist_mm, 1)
            rounds(pe, IN_ROUNDS, hist_round)
            t.matmul(count, zeros_bf[:], zeros_bf[:, 0:HEAD_TILES], start=False, stop=True,
                     skip_group_check=True).then_inc(hist_mm, 1)
            run([("M", banks[7][:, 0:HEAD_TILES], ones[:], hist),
                 ("M", banks[7][:, P:P + HEAD_TILES], lower_of[:], hist)])

            nxt = banks[0][:, 0:HEAD_TILES]
            asked[0] += 1
            pe.wait_ge(to_pe, asked[0])
            t.matmul(nxt, identity[:], start_pos, start=True, stop=False, skip_group_check=True).then_inc(updated, 1)

            def heads_as_rows(grp, k, h):
                pe.wait_ge(rec_ready, grp + 1)
                at_least(pe, heads_read, 2 * grp + h - 1)
                for s in range(4 * h, 4 * h + 4):
                    ins = t.transpose(banks[1 + h][:, (s % 4) * P:(s % 4 + 1) * P],
                                      rec8[k][:, 4 * s:4 * s + 1].to_broadcast([P, P]), identity[:])
                ins.then_inc(hb_ready, 1)

            def lo_transposed(grp, b):
                pe.wait_ge(oh_ready, grp + 1)
                at_least(pe, lo_t_ready, grp - 1)
                for s in range(GROUP):
                    ins = t.transpose(banks[6 + b][:].bitcast(BF16)[:, s * P:(s + 1) * P],
                                      oh_lo[b][:, s * P:(s + 1) * P], identity_bf[:])
                ins.then_inc(ot_ready, 1)

            def rank_round(i):
                for k in range(DEPTH):
                    grp, b = DEPTH * i + k, k % 2
                    more = not (isinstance(grp, int) and grp == IN_GROUPS - 1)
                    for q in range(PAIRS):
                        n, h = grp * PAIRS + q, q // 2
                        pe.wait_ge(counts_ready, n + 1)
                        for s in (2 * q, 2 * q + 1):
                            ins = t.matmul(nxt, oh_lo[b][:, s * P:(s + 1) * P],
                                           oh_hi[b][:, s * HEAD_TILES:(s + 1) * HEAD_TILES],
                                           start=False, stop=False, skip_group_check=True)
                        ins.then_inc(updated, 1)
                        if q == 0:
                            pe.wait_ge(lo_t_ready, grp + 1)
                        if q % 2 == 0:
                            at_least(pe, rank_read, 2 * grp + h - 1)
                        for s in (2 * q, 2 * q + 1):
                            ins = t.matmul(banks[4 + h][:, (s % 4) * HEAD_TILES:(s % 4 + 1) * HEAD_TILES],
                                           lo_t[b][:, s * P:(s + 1) * P], counts[q % 2], start=True, stop=True)
                        ins.then_inc(queried, 1)
                        if more and q < 2:
                            heads_as_rows(grp + 1, (k + 1) % DEPTH, q)
                        if more and q == 2:
                            lo_transposed(grp + 1, (k + 1) % 2)
            heads_as_rows(0, 0, 0)
            heads_as_rows(0, 0, 1)
            lo_transposed(0, 0)
            rounds(pe, RANK_ROUNDS, rank_round)

            def flip(n):
                pe.wait_ge(flip_ready, n + 1)
                for m, (k, count) in enumerate(flip_lots):
                    at_least(pe, flipped, FLIP_STEPS * n + m - 1)
                    for c in range(count):
                        ins = t.transpose(flip_banks[m % 2][:, c * P:(c + 1) * P], flip_from(n, k + c), identity[:])
                    ins.then_inc(flip_mm, 1)

            flip(0)
            run([("M", banks[7][:, 0:1], from_prev[:], edge_col)])
            run([("M", banks[7][:, 0:1], from_next[:], same[:, 0:1])])
            flip(1)
            carry(False)
            carry(True)
            carry(False)
            carry(True)
            flip(2)
            flip(3)

            def in_window(window, tile, first, n, width):
                if n == 0:
                    return window[:, 0:width]
                slot = nc.s_assert_within(tile - first, 0, n, skip_runtime_bounds_check_because=
                                          "every head tile has an edge tile, so the next is at most one further")
                return window[:, bass.ds(slot * W0, width)]

            def sums(p):
                width = W0 if p == 0 else W0 - 1

                def one(i):
                    for b in range(2):
                        grp = 2 * i + b
                        pe.wait_ge(rhs_ready[p], grp + 1)
                        pe.wait_ge(scaled[p], grp + 1)
                        at_least(pe, added[p], 2 * grp - 2)
                        _, tiles = nc.values_load_multi_w_load_instructions(
                            tile_of[:, bass.ds(grp * GROUP, GROUP)], engines=[mybir.EngineType.PE], min_val=0,
                            max_val=HEAD_TILES - 1, skip_runtime_bounds_check_because="clamped when made")
                        for h in range(2):
                            window = banks[2 * b + h]
                            first = tiles[HALF * h]
                            t.matmul(window[:, 0:WINDOW], zeros_bf[:], zeros_wide[:, 0:WINDOW], start=True, stop=False,
                                     skip_group_check=True)
                            for s in range(HALF * h, HALF * (h + 1)):
                                ins = t.matmul(in_window(window, tiles[s], first, s % HALF, width),
                                               oh[b][:, s * P:(s + 1) * P], rhs[b][:, s * W0:s * W0 + width],
                                               start=False, stop=s == HALF * h + HALF - 1, skip_group_check=True)
                            ins.then_inc(summed[p], 1)
                rounds(pe, ROUNDS, one)

            sums(0)
            for p in (1, 2):
                pe.wait_ge(tab_ready[p], 1)

                for n in range(TAB_STEPS):
                    b = n % 2
                    pe.wait_ge(tab_emb[p], n + 1)
                    at_least(pe, tab_copied[p], n - 1)
                    for m in range(TAB):
                        ins = t.transpose(banks[2 * b + m // 4][:, (m % 4) * P:(m % 4 + 1) * P], stg[b][:, m, :],
                                          identity[:])
                    ins.then_inc(tab_t[p], 1)
                    pe.wait_ge(tab_copied[p], n + 1)
                    at_least(pe, tab_staged[p], n - 1)
                    for m in range(TAB):
                        ins = t.matmul(banks[4 + 2 * b + m // 4][:, (m % 4) * 2 * RELS:(m % 4 + 1) * 2 * RELS],
                                       emb_t[b][:, m * P:(m + 1) * P], ab[:], start=True, stop=True)
                    ins.then_inc(tab_mm[p], 1)
                pe.wait_ge(tab_staged[p], TAB_STEPS)

                def p_round(i):
                    for b in range(2):
                        grp = 2 * i + b
                        pe.wait_ge(hl_ready[p], grp + 1)
                        for h in range(2):
                            at_least(pe, oht_ready[p], 2 * grp + h - 1)
                            for s in range(4 * h, 4 * h + 4):
                                ins = t.transpose(banks[4 + h][:, (s % 4) * P:(s % 4 + 1) * P],
                                                  hl8[b][:, s:s + 1].to_broadcast([P, P]), identity[:])
                            ins.then_inc(hlb_ready[p], 1)
                        _, tiles = nc.values_load_multi_w_load_instructions(
                            tile_of[:, bass.ds(grp * GROUP, GROUP)], engines=[mybir.EngineType.PE], min_val=0,
                            max_val=HEAD_TILES - 1, skip_runtime_bounds_check_because="clamped when made")
                        at_least(pe, z_step[p], 2 * grp - 3)
                        for h in range(2):
                            pe.wait_ge(oht_ready[p], 2 * grp + h + 1)
                            for s in range(4 * h, 4 * h + 4):
                                ins = t.matmul(banks[b][:, s * RELS:(s + 1) * RELS], oh[b][:, s * P:(s + 1) * P],
                                               p_tab[:, bass.ds(tiles[s] * RELS, RELS)], start=True, stop=True)
                        ins.then_inc(p_done[p], 1)
                rounds(pe, ROUNDS, p_round)
                flip(2 * p + 2)
                carry(False)
                carry(True)
                flip(2 * p + 3)
                sums(p)


_INS = ['x', 'src', 'dst', 'edge_type_50', 'edge_weight', 'L0_gnn_beta', 'L0_gnn_eps', 'L1_gnn_relation_emb',
        'L1_gnn_fc_w', 'L1_gnn_fc_b']


def kernel(**inputs):
    import numpy as _np
    import concourse.bacc as _bacc
    from concourse import mybir as _mybir
    from concourse.bass_utils import run_bass_kernel_spmd as _run

    nc = _bacc.Bacc("TRN2", target_bir_lowering=False, num_devices=1)
    arrays, args = {}, []
    for name in _INS:
        a = _np.ascontiguousarray(inputs[name])
        arrays[f"in_{name}"] = a
        args.append(nc.dram_tensor(f"in_{name}", a.shape, _mybir.dt.from_np(a.dtype), kind="ExternalInput").ap())
    out = nc.dram_tensor("out_x", (NODES, D), _mybir.dt.float32, kind="ExternalOutput").ap()
    build(nc, *args, out)
    r = _run(nc, [arrays], core_ids=[0])
    return r.results[0]["out_x"]
```

```python
import numpy as np
import concourse.bass as bass
from concourse import mybir
from contextlib import ExitStack

F32 = mybir.dt.float32
BF16 = mybir.dt.bfloat16
I32 = mybir.dt.int32
ALU = mybir.AluOpType
ACT = mybir.ActivationFunctionType
AX = mybir.AxisListType

P = 128
NODES, D = 12500, 64
EDGES = 412500
RELS = 50
HEAD_TILES = -(-NODES // P)
LAST_NODES = NODES - (HEAD_TILES - 1) * P
PER_PART = -(-EDGES // P)
LAST_PART = EDGES - (P - 1) * PER_PART
GROUP = 8
PAIRS = GROUP // 2
HALF = GROUP // 2
TAB = 7
TAB_STEPS = HEAD_TILES // TAB
assert TAB * TAB_STEPS == HEAD_TILES and TAB_STEPS % 2 == 0
UNROLL = 2
DEPTH = 4
IN_GROUPS = -(-PER_PART // (GROUP * DEPTH)) * DEPTH
IN_TILES = IN_GROUPS * GROUP
BLOCKS = -(-(PER_PART + HEAD_TILES) // P)
TILES = BLOCKS * P
GROUPS = TILES // GROUP
POSITIONS = TILES * P
CHUNK_GROUPS = P // GROUP
CHUNKS = BLOCKS
HOP_STEPS = 26
HOP_ASKS = 6
TABLE = HEAD_TILES * P
ROW = 128
W0 = D + 2
WINDOW = HALF * W0
NEG = -1.5e38
LEAKY = 0.2
OUT_OF_BOUNDS = float(1 << 20)


def at_least(engine, sem, value):
    if isinstance(value, int) and value <= 0:
        return
    engine.wait_ge(sem, value)


def rounds(engine, count, body):
    body(0)
    with engine.Fori(1, count - 1) as i:
        body(i)
    body(count - 1)


def build(nc, x_d, src_d, dst_d, type_d, weight_d, beta_d, eps_d, rel_d, fcw_d, fcb_d, out_d):
    def dram(name, shape, dt=F32):
        return nc.dram_tensor(name, shape, dt, kind="Internal").ap()

    sorted_d = dram("sorted_records", (POSITIONS, 4))
    tile_of_d = dram("head_tile_of", (TILES,), I32)
    xn_d = dram("xn_table", (TABLE, D))
    x1_d = dram("x1_rows", (TABLE, D))
    hop_d = dram("hop_table", (TABLE, ROW))
    flags_d = dram("same_head_flags", (2, POSITIONS))
    rows_d = dram("gathered_rows", (GROUPS * P, GROUP * D))

    ctx = ExitStack()
    with ctx:
        def sb(name, shape, dt=F32):
            return ctx.enter_context(nc.sbuf_tensor(name, shape, dt))

        def bank(name):
            return ctx.enter_context(nc.psum_tensor(name, [P, 512], F32))

        def sem(name):
            return ctx.enter_context(nc.semaphore(name))

        identity = sb("identity", [P, P])
        identity_bf = sb("identity_bf", [P, P], BF16)
        iota_i = sb("iota_i", [P, P], I32)
        iota_row = sb("iota_row", [P, P])
        iota_bf = sb("iota_bf", [P, P], BF16)
        iota_col_i = sb("iota_col_i", [P, 1], I32)
        iota_col = sb("iota_col", [P, 1])
        tile_no_i = sb("tile_no_i", [P, BLOCKS], I32)
        tile_no = sb("tile_no", [P, BLOCKS])
        earlier2 = sb("earlier2", [P, 2 * P])
        earlier = earlier2[:, P:2 * P]
        lower_of = sb("lower_of", [P, P])
        ones = sb("ones", [P, P])
        from_prev = sb("from_prev", [P, P])
        from_next = sb("from_next", [P, P])
        zeros_bf = sb("zeros_bf", [P, P], BF16)
        zeros_wide = sb("zeros_wide", [P, WINDOW], BF16)
        params = sb("params", [P, 4])
        small = sb("small", [P, 8])
        small_sd = sb("small_sd", [P, HEAD_TILES])[:]
        small_mean = sb("small_mean", [P, HEAD_TILES])[:]
        rows1 = sb("rows1", [1, 5 * P + 8])
        not_last = sb("not_last", [P, 1])
        fcw_sb = sb("fcw_sb", [D, 2 * D])
        fcwb = sb("fcwb", [D, D + 1])
        fcwa = sb("fcwa", [D, D + 1])
        rel_sb = sb("rel_sb", [RELS, D])
        relT = sb("relT", [D, RELS])
        ab = sb("ab", [D + 1, 2 * RELS])

        A_TAIL, A_TYPE, A_HL, A_WT, A_EM, A_NS = (n * TILES for n in range(6))
        A_TJ = A_NS + TILES + 4
        A_ACC = A_TJ + TILES
        A_P = A_ACC + (HEAD_TILES + HALF - 1) * W0
        A_V = A_P + HEAD_TILES * RELS
        A_T = A_V + HEAD_TILES * D
        A_END = A_T + HEAD_TILES * D
        arena = sb("arena", [P, A_END])

        def part(at, size, dt=F32):
            v = arena[:, at:at + size]
            return v if dt == F32 else v.bitcast(dt)

        tail_i = part(A_TAIL, TILES, I32)
        types = part(A_TYPE, TILES)
        local_head = part(A_HL, TILES)
        weight = part(A_WT, TILES)
        em = part(A_EM, TILES)
        same = part(A_NS, TILES + 1)
        tile_of = part(A_TJ, TILES, I32)[0:1, :]
        acc = part(A_ACC, (HEAD_TILES + HALF - 1) * W0)
        acc3 = acc[:, 0:HEAD_TILES * W0].rearrange("p (t c) -> p t c", c=W0)
        p_tab = part(A_P, HEAD_TILES * RELS)
        val = part(A_V, HEAD_TILES * D)
        val3 = val.rearrange("p (t d) -> p t d", d=D)
        tmp = part(A_T, HEAD_TILES * D)
        tmp3 = tmp.rearrange("p (t d) -> p t d", d=D)
        scan_a = part(A_ACC, TILES)
        scan_b = part(A_ACC + TILES, TILES)
        scan_c = part(A_ACC + 2 * TILES, TILES)
        scan_d = part(A_ACC + 3 * TILES, TILES)

        S_REC = A_ACC
        S_STG = S_REC + 4 * IN_TILES
        S_LO = S_STG + IN_TILES
        S_HI = S_LO + IN_TILES // 2
        rec = part(S_REC, 4 * IN_TILES).rearrange("p (j f) -> p j f", f=4)
        stage_i = part(S_STG, IN_TILES, I32)
        stage_f = part(S_STG, IN_TILES)
        lo_bf = part(S_LO, IN_TILES // 2, BF16)
        hi_bf = part(S_HI, IN_TILES // 2, BF16)
        half_i = part(0, IN_TILES, I32)
        blank = part(0, 4 * TILES)
        srec = part(S_REC, 4 * TILES).rearrange("p (j f) -> p j f", f=4)
        at = 0

        def take(size, dt=F32):
            nonlocal at
            v = part(at, size, dt)
            at += size
            return v

        oh_lo = [take(GROUP * P // 2, BF16) for _ in range(2)]
        oh_hi = [take(GROUP * HEAD_TILES // 2, BF16) for _ in range(2)]
        lo_t = [take(GROUP * P) for _ in range(2)]
        counts = [take(HEAD_TILES) for _ in range(2)]
        rec8 = [take(4 * GROUP) for _ in range(DEPTH)]
        junk = [take(2 * P) for _ in range(GROUP)]
        junk2 = [take(HEAD_TILES) for _ in range(GROUP)]
        occ8 = [take(GROUP) for _ in range(2)]
        base8 = [take(GROUP) for _ in range(2)]
        pos8 = [take(GROUP, I32) for _ in range(2)]
        pos_lo = take(GROUP, I32)
        pos_hi = take(GROUP, I32)
        pad8 = take(GROUP)
        dest_f = take(GROUP)
        dest8 = [take(GROUP, I32) for _ in range(DEPTH)]
        hist = take(HEAD_TILES)
        tiles_i = take(HEAD_TILES, I32)
        tiles_f = take(HEAD_TILES)
        cum = take(HEAD_TILES)
        cum_x = take(HEAD_TILES)
        start_pos = take(HEAD_TILES)
        tile_f = take(BLOCKS)
        tile_i = take(BLOCKS, I32)
        assert at <= A_TJ

        at = A_V
        rows = [take(GROUP * ROW) for _ in range(DEPTH)]
        rhs = [take(GROUP * W0) for _ in range(2)]
        oh = [take(GROUP * P) for _ in range(2)]
        back = [take(GROUP * D) for _ in range(DEPTH)]
        oh_t = [take(GROUP * P) for _ in range(2)]
        type_oh = [take(GROUP * RELS) for _ in range(2)]
        zed = take(GROUP * RELS)
        assert at <= A_END
        idx8_all = sb("idx8", [P, DEPTH * GROUP], I32)
        idx8 = [idx8_all[:, n * GROUP:(n + 1) * GROUP] for n in range(DEPTH)]
        reset2 = part(A_WT, TILES)
        after2 = part(A_EM, TILES)
        reset_min = sb("reset_min", [P, CHUNKS])
        after_min = sb("after_min", [P, CHUNKS])
        idx_c = sb("idx_c", [P, P], I32)
        hl_c = sb("hl_c", [P, P], BF16)
        hl_s = sb("hl_s", [P, P], BF16)
        type_c = sb("type_c", [P, P])
        e_c = sb("e_c", [P, P])
        wt_c = sb("wt_c", [P, P])
        leaky = sb("leaky", [P, P])
        scan_y = sb("scan_y", [P, P])
        scan_z = sb("scan_z", [P, P])
        scan_v = sb("scan_v", [P, P])
        after_c = sb("after_c", [P, P])
        expo = sb("expo", [P, P + 1])
        rescale = sb("rescale", [P, 1])
        scratch3 = part(A_WT, HEAD_TILES * D).rearrange("p (t d) -> p t d", d=D)
        stg = [part(A_T + n * TAB * ROW, TAB * ROW).rearrange("p (m r) -> p m r", r=ROW) for n in range(2)]
        emb_t = [part(A_T + (2 + n) * TAB * P, TAB * P)[0:D + 1, :] for n in range(2)]
        assert A_T + 4 * TAB * P <= A_END

        banks = [bank(f"bank{n}") for n in range(8)]

        loaded = sem("loaded")
        const_ready = sem("const_ready")
        pool_step = sem("pool_step")
        dve_step = sem("dve_step")
        stage_in = sem("stage_in")
        stage_free = sem("stage_free")
        blank_ready = sem("blank_ready")
        blank_done = sem("blank_done")
        hist_oh = sem("hist_oh")
        hist_mm = sem("hist_mm")
        to_pe = sem("to_pe")
        from_pe = sem("from_pe")
        tile_i_ready = sem("tile_i_ready")
        tile_saved = sem("tile_saved")
        tile_loaded = sem("tile_loaded")
        rec_ready = sem("rec_ready")
        oh_ready = sem("oh_ready")
        hb_ready = sem("hb_ready")
        ot_ready = sem("ot_ready")
        lo_t_ready = sem("lo_t_ready")
        counts_ready = sem("counts_ready")
        updated = sem("updated")
        queried = sem("queried")
        rank_read = sem("rank_read")
        heads_read = sem("heads_read")
        rank_step = sem("rank_step")
        lot_begun = sem("lot_begun")
        dest_ready = sem("dest_ready")
        scattered = [sem(f"scattered{k}") for k in range(DEPTH)]
        srec_in = sem("srec_in")
        sort_read = sem("sort_read")
        flip_ready = sem("flip_ready")
        flip_mm = sem("flip_mm")
        flipped = sem("flipped")
        act_in = sem("act_in")
        act_out = sem("act_out")
        node_in = sem("node_in")
        node_ready = sem("node_ready")
        node_out = sem("node_out")
        tab_ready = [None, sem("tab_ready1"), sem("tab_ready2")]
        tab_emb = [None, sem("tab_emb1"), sem("tab_emb2")]
        tab_t = [None, sem("tab_t1"), sem("tab_t2")]
        tab_copied = [None, sem("tab_copied1"), sem("tab_copied2")]
        tab_mm = [None, sem("tab_mm1"), sem("tab_mm2")]
        tab_staged = [None, sem("tab_staged1"), sem("tab_staged2")]
        tab_out = [None, [sem("tab_out1a"), sem("tab_out1b")], [sem("tab_out2a"), sem("tab_out2b")]]
        idx_ready = [sem(f"idx_ready{p}") for p in range(3)]
        gathered = [[sem(f"gathered{p}{k}") for k in range(DEPTH)] for p in range(3)]
        hl_ready = [None] + [sem(f"hl_ready{p}") for p in (1, 2)]
        hlb_ready = [None] + [sem(f"hlb_ready{p}") for p in (1, 2)]
        oht_ready = [None] + [sem(f"oht_ready{p}") for p in (1, 2)]
        toh_ready = [None] + [sem(f"toh_ready{p}") for p in (1, 2)]
        p_done = [None] + [sem(f"p_done{p}") for p in (1, 2)]
        z_step = [None] + [sem(f"z_step{p}") for p in (1, 2)]
        score_done = [None] + [sem(f"score_done{p}") for p in (1, 2)]
        kept = [None] + [[sem(f"kept{p}{k}") for k in range(DEPTH)] for p in (1, 2)]
        back_in = [None] + [[sem(f"back_in{p}{k}") for k in range(DEPTH)] for p in (1, 2)]
        sum_begin = [sem(f"sum_begin{p}") for p in range(3)]
        rhs_ready = [sem(f"rhs_ready{p}") for p in range(3)]
        scaled = [sem(f"scaled{p}") for p in range(3)]
        summed = [sem(f"summed{p}") for p in range(3)]
        added = [sem(f"added{p}") for p in range(3)]
        stored = sem("stored")
        moves_begun = sem("moves_begun")
        lots_begun = sem("lots_begun")
        flags_ready = sem("flags_ready")
        flags_out = sem("flags_out")
        flags_in = sem("flags_in")
        chunk_step = [None] + [sem(f"chunk_step{p}") for p in (1, 2)]
        rescaled = [None] + [sem(f"rescaled{p}") for p in (1, 2)]
        scan_step = [None] + [sem(f"scan_step{p}") for p in (1, 2)]
        scan_ask = [None] + [sem(f"scan_ask{p}") for p in (1, 2)]
        scan_ans = [None] + [sem(f"scan_ans{p}") for p in (1, 2)]
        exp_ask = [None] + [sem(f"exp_ask{p}") for p in (1, 2)]
        exp_done = [None] + [sem(f"exp_done{p}") for p in (1, 2)]

        block = ctx.enter_context(nc.Block())

        IN_ROUNDS = IN_GROUPS // UNROLL
        RANK_ROUNDS = IN_GROUPS // DEPTH
        GATHER_ROUNDS = GROUPS // DEPTH
        ROUNDS = GROUPS // UNROLL
        flips = [(em, scan_a, True)]
        flips += [(weight, scan_a, True), (scan_b, weight, False), (scan_c, em, False)]

        carry_col = small[:, 0:1]
        reset_col = small[:, 1:2]
        carry_in = small[:, 2:3]
        edge_col = small[:, 3:4]
        edge_in = small[:, 4:5]
        max_row = rows1[:, 0:P]
        reset_row = rows1[:, P:2 * P]
        carried_row = rows1[:, 2 * P:3 * P + 4]
        back_row = rows1[:, 3 * P + 4:4 * P + 8]
        factor_row = rows1[:, 4 * P + 8:5 * P + 8]

        def chunk_loop(engine, body, last):
            body(0)
            body(1)
            with engine.Fori(2, CHUNKS - 1) as c:
                body(c)
            for c in range(CHUNKS - 1, last):
                body(c)

        def is_chunk(c, *which):
            return isinstance(c, int) and c in which

        @block.sync
        def _(sp):
            sp.dma_start(params[:, 0:1], beta_d[:].unsqueeze(0).to_broadcast([P, 1])).then_inc(loaded, 16)
            sp.dma_start(params[:, 1:2], eps_d[:].unsqueeze(0).to_broadcast([P, 1])).then_inc(loaded, 16)
            sp.dma_start(fcw_sb[:], fcw_d).then_inc(loaded, 16)
            sp.dma_start(fcwb[:, D:D + 1], fcb_d[:].unsqueeze(1)).then_inc(loaded, 16)
            sp.dma_start(rel_sb[:], rel_d).then_inc(loaded, 16)
            for n, (col, view) in enumerate([(src_d, stage_i), (dst_d, stage_i), (type_d, stage_i), (weight_d, stage_f)]):
                sp.wait_ge(stage_free, n + 1)
                sp.dma_start(view[0:P - 1, 0:PER_PART],
                             col[0:(P - 1) * PER_PART].rearrange("(p j) -> p j", p=P - 1)).then_inc(stage_in, 16)
                sp.dma_start(view[P - 1:P, 0:LAST_PART],
                             col[(P - 1) * PER_PART:EDGES].unsqueeze(0)).then_inc(stage_in, 16)
            sp.wait_ge(blank_ready, 2)
            sp.dma_start(sorted_d.rearrange("(p j) f -> p (j f)", p=P), blank).then_inc(blank_done, 16)
            sp.wait_ge(tile_i_ready, 1)
            sp.dma_start(tile_of_d.rearrange("(r k) -> r k", k=BLOCKS), tile_i).then_inc(tile_saved, 16)
            sp.wait_ge(tile_saved, 16)
            sp.dma_start(tile_of, tile_of_d.unsqueeze(0)).then_inc(tile_loaded, 16)
            for k in range(DEPTH):
                sp.wait_ge(scattered[k], 16 * GROUP * RANK_ROUNDS)
            sp.wait_ge(sort_read, 1)
            sp.dma_start(part(S_REC, 4 * TILES), sorted_d.rearrange("(p j) f -> p (j f)", p=P)).then_inc(srec_in, 16)

            sp.wait_ge(flags_ready, 1)
            for n in range(2):
                sp.dma_start(flags_d[n].rearrange("(r c) -> r c", r=P), same[:, n:n + TILES]).then_inc(flags_out, 16)

            def load_nodes(view3, table, n_ready, whole=True):
                sp.wait_ge(node_ready, n_ready)
                if whole:
                    sp.dma_start(view3, table.rearrange("(t p) d -> p t d", p=P)).then_inc(node_in, 16)
                else:
                    sp.dma_start(view3[:, 0:HEAD_TILES - 1, :],
                                 table[0:(HEAD_TILES - 1) * P, :].rearrange("(t p) d -> p t d", p=P)).then_inc(node_in, 16)
                    sp.dma_start(view3[0:LAST_NODES, HEAD_TILES - 1, :],
                                 table[(HEAD_TILES - 1) * P:NODES, :]).then_inc(node_in, 16)

            load_nodes(val3, x_d, 1, whole=False)
            sp.wait_ge(node_ready, 2)
            sp.dma_start(xn_d.rearrange("(t p) d -> p t d", p=P), val3).then_inc(node_out, 16)
            load_nodes(val3, x_d, 3, whole=False)
            load_nodes(tmp3, xn_d, 3)
            sp.wait_ge(node_ready, 4)
            sp.dma_start(x1_d.rearrange("(t p) d -> p t d", p=P), val3).then_inc(node_out, 16)
            sp.wait_ge(flags_out, 32)
            for n, to in enumerate((reset2, after2)):
                sp.dma_start(to.rearrange("r (c p) -> r c p", p=P),
                             flags_d[n].rearrange("(c r p) -> r c p", r=P, p=P)).then_inc(flags_in, 16)
            for p in (1, 2):
                for n in range(TAB_STEPS):
                    sp.wait_ge(tab_staged[p], n + 1)
                    sp.dma_start(hop_d[n * TAB * P:(n + 1) * TAB * P, :].rearrange("(m p) r -> p m r", p=P),
                                 stg[n % 2]).then_inc(tab_out[p][n % 2], 16)

                def hop_chunk(c):
                    for g in range(CHUNK_GROUPS):
                        ahead, kb = (g + 2) // CHUNK_GROUPS, (g + 2) % DEPTH
                        if not (is_chunk(c, 0) and not ahead) and not (is_chunk(c, CHUNKS) and ahead):
                            grp = CHUNK_GROUPS * (c - 1) + g + 2
                            times = CHUNK_GROUPS // DEPTH * (c - 1 + ahead) + (g + 2) % CHUNK_GROUPS // DEPTH
                            sp.wait_ge(kept[p][kb], 16 * (times + 1))
                            sp.sem_inc(moves_begun, 1)
                            at_least(sp, scaled[p], grp - DEPTH + 1)
                            sp.sem_inc(moves_begun, 1)
                            sp.dma_start(back[kb], rows_d[bass.ds(grp * P, P), :]).then_inc(back_in[p][kb], 16)
                        if not is_chunk(c, CHUNKS):
                            grp, k = CHUNK_GROUPS * c + g, g % DEPTH
                            sp.wait_ge(gathered[p][k], 16 * GROUP * (CHUNK_GROUPS // DEPTH * c + g // DEPTH + 1))
                            sp.sem_inc(moves_begun, 1)
                            sp.dma_start(rows_d[bass.ds(grp * P, P), :].rearrange("p (s d) -> p s d", d=D),
                                         rows[k].rearrange("p (s r) -> p s r", r=ROW)[:, :, 0:D]).then_inc(kept[p][k], 16)
                chunk_loop(sp, hop_chunk, CHUNKS + 1)
                sp.wait_ge(node_ready, 4 + p)
                sp.dma_start(tmp3, hop_d.rearrange("(t p) r -> p t r", p=P)[:, :, 0:D]).then_inc(node_in, 16)
            sp.wait_ge(node_ready, 7)
            sp.dma_start(tmp3, x1_d.rearrange("(t p) d -> p t d", p=P)).then_inc(node_in, 16)
            sp.wait_ge(node_ready, 8)
            sp.dma_start(out_d[0:(HEAD_TILES - 1) * P, :].rearrange("(t p) d -> p t d", p=P),
                         val3[:, 0:HEAD_TILES - 1, :]).then_inc(stored, 16)
            sp.dma_start(out_d[(HEAD_TILES - 1) * P:NODES, :],
                         val3[0:LAST_NODES, HEAD_TILES - 1, :]).then_inc(stored, 16)
            sp.wait_ge(stored, 32)

        @block.gpsimd
        def _(pool):
            g = indirect = nc.gpsimd
            steps = [0]

            def link(ins):
                steps[0] += 1
                ins.then_inc(pool_step, 1)
                pool.wait_ge(pool_step, steps[0])

            def diagonal(out, base):
                link(g.memset(out[:], 0.0))
                link(g.affine_select(out=out[:], in_=out[:], compare_op=ALU.not_equal, fill=1.0, base=base,
                                     pattern=[[-1, P]], channel_multiplier=1))

            diagonal(identity, 0)
            diagonal(from_prev, 1)
            diagonal(from_next, -1)
            link(g.memset(earlier2[:], 1.0))
            link(g.affine_select(out=earlier, in_=earlier, compare_op=ALU.is_gt, fill=0.0, base=0,
                                 pattern=[[-1, P]], channel_multiplier=1))
            link(g.memset(lower_of[:], 1.0))
            link(g.affine_select(out=lower_of[:], in_=lower_of[:], compare_op=ALU.is_gt, fill=0.0, base=0,
                                 pattern=[[1, P]], channel_multiplier=-1))
            link(g.memset(ones[:], 1.0))
            link(g.memset(zeros_bf[:], 0.0))
            link(g.memset(zeros_wide[:], 0.0))
            link(g.iota(iota_i[:], pattern=[[1, P]], base=0, channel_multiplier=0))
            link(g.iota(iota_col_i[:], pattern=[[0, 1]], base=0, channel_multiplier=1))
            link(g.iota(tile_no_i[:], pattern=[[1, BLOCKS]], base=0, channel_multiplier=BLOCKS))
            g.memset(fcwa[:, D:D + 1], 0.0).then_inc(const_ready, 1)

            pool.wait_ge(blank_done, 16)

            def scatter_round(i):
                for k in range(DEPTH):
                    pool.wait_ge(dest_ready, DEPTH * i + k + 1)
                    pool.sem_inc(lot_begun, 1)
                    for s in range(GROUP):
                        g.indirect_dma_start(
                            out=sorted_d, out_offset=bass.IndirectOffsetOnAxis(ap=dest8[k][:, s:s + 1], axis=0),
                            in_=rec8[k][:, 4 * s:4 * s + 4], in_offset=None,
                            bounds_check=POSITIONS - 1, oob_is_err=False).then_inc(scattered[k], 16)
            rounds(pool, RANK_ROUNDS, scatter_round)

            pool.wait_ge(node_out, 16)

            def gather_round0(i):
                for k in range(DEPTH):
                    grp = DEPTH * i + k
                    pool.wait_ge(idx_ready[0], grp + 1)
                    at_least(pool, scaled[0], grp - DEPTH + 1)
                    pool.sem_inc(lot_begun, 1)
                    for s in range(GROUP):
                        g.indirect_dma_start(
                            out=rows[k][:, s * D:(s + 1) * D], out_offset=None, in_=xn_d,
                            in_offset=bass.IndirectOffsetOnAxis(ap=idx8[k][:, s:s + 1], axis=0)).then_inc(gathered[0][k], 16)
            rounds(pool, GATHER_ROUNDS, gather_round0)

            for p in (1, 2):
                for b in range(2):
                    pool.wait_ge(tab_out[p][b], 16 * (TAB_STEPS // 2))

                def hop_chunk(c):
                    for g in range(CHUNK_GROUPS):
                        grp, k = CHUNK_GROUPS * c + g, g % DEPTH
                        if g % (CHUNK_GROUPS // 2) == 0:
                            pool.wait_ge(idx_ready[p], 2 * c + g // (CHUNK_GROUPS // 2) + 1)
                        at_least(pool, score_done[p], grp - DEPTH + 1)
                        at_least(pool, kept[p][k], 16 * (CHUNK_GROUPS // DEPTH * c + g // DEPTH))
                        pool.sem_inc(lot_begun, 1)
                        for s in range(GROUP):
                            indirect.indirect_dma_start(
                                out=rows[k][:, s * ROW:(s + 1) * ROW], out_offset=None, in_=hop_d,
                                in_offset=bass.IndirectOffsetOnAxis(ap=idx_c[:, g * GROUP + s:g * GROUP + s + 1], axis=0),
                            ).then_inc(gathered[p][k], 16)
                chunk_loop(pool, hop_chunk, CHUNKS)

        def flip_from(n, k):
            src, dst, linear = flips[n]
            return src.rearrange("p (r k) -> p k r", k=BLOCKS)[:, k, :] if linear else src[:, k * P:(k + 1) * P]

        def flip_to(n, k, count):
            src, dst, linear = flips[n]
            if linear:
                return dst[:, k * P:(k + count) * P].rearrange("p (k r) -> p k r", k=count)
            return dst.rearrange("p (r k) -> p k r", k=BLOCKS)[:, k:k + count, :]

        flip_lots = [(k, min(4, BLOCKS - k)) for k in range(0, BLOCKS, 4)]
        FLIP_STEPS = len(flip_lots)
        flip_banks = [banks[5], banks[6]]

        @block.scalar
        def _(act):
            a = nc.scalar
            waits = [0]

            def copy_lo(grp, b):
                act.wait_ge(ot_ready, grp + 1)
                at_least(act, queried, PAIRS * (grp - 1))
                a.copy(lo_t[b], banks[6 + b][:].bitcast(BF16)).then_inc(lo_t_ready, 1)

            def sort_round(i):
                for k in range(DEPTH):
                    grp = DEPTH * i + k
                    for s in range(PAIRS):
                        n = grp * PAIRS + s
                        act.wait_ge(updated, n + 1)
                        at_least(act, queried, n - 1)
                        a.copy(counts[s % 2], banks[0][:, 0:HEAD_TILES]).then_inc(counts_ready, 1)
                        if s == PAIRS - 1 and not (isinstance(grp, int) and grp == IN_GROUPS - 1):
                            copy_lo(grp + 1, (k + 1) % 2)
            copy_lo(0, 0)
            rounds(act, RANK_ROUNDS, sort_round)

            def flip(n):
                for m, (k, count) in enumerate(flip_lots):
                    act.wait_ge(flip_mm, FLIP_STEPS * n + m + 1)
                    a.copy(flip_to(n, k, count),
                           flip_banks[m % 2][:, 0:count * P].rearrange("p (k r) -> p k r", k=count)).then_inc(flipped, 1)

            def request(fn):
                waits[0] += 1
                act.wait_ge(act_in, waits[0])
                fn().then_inc(act_out, 1)

            def scale_round(p):
                def one(i):
                    for k in range(DEPTH):
                        grp, b = DEPTH * i + k, k % 2
                        act.wait_ge(gathered[0][k], 16 * GROUP * (i + 1))
                        act.wait_ge(rhs_ready[p], grp + 1)
                        for s in range(GROUP):
                            ins = a.activation(rhs[b][:, s * W0:s * W0 + D], rows[k][:, s * D:(s + 1) * D],
                                               ACT.Copy, scale=rhs[b][:, s * W0 + D:s * W0 + D + 1])
                        ins.then_inc(scaled[p], 1)
                return one

            def table(p):
                act.wait_ge(tab_ready[p], 1)
                for n in range(TAB_STEPS):
                    b = n % 2
                    at_least(act, tab_out[p][b], 16 * (n // 2))
                    a.copy(stg[b][:, :, 0:D], val3[:, n * TAB:(n + 1) * TAB, :]).then_inc(tab_emb[p], 1)
                    act.wait_ge(tab_t[p], n + 1)
                    at_least(act, tab_mm[p], n - 1)
                    a.copy(emb_t[b][0:D, 0:4 * P], banks[2 * b][0:D, :])
                    a.copy(emb_t[b][0:D, 4 * P:TAB * P], banks[2 * b + 1][0:D, 0:(TAB - 4) * P]).then_inc(tab_copied[p], 1)

            flip(0)
            request(lambda: a.activation(small_sd, small_sd, ACT.Sqrt))
            request(lambda: a.activation(small_sd, small_sd, ACT.Sqrt))
            flip(1)
            request(lambda: a.activation(scan_b, scan_b, ACT.Sqrt))
            request(lambda: a.activation(scan_b, scan_b, ACT.Exp))
            flip(2)
            flip(3)
            rounds(act, GATHER_ROUNDS, scale_round(0))
            request(lambda: a.activation(small_sd, small_sd, ACT.Exp))
            request(lambda: a.activation(small_sd, small_sd, ACT.Sqrt))
            for p in (1, 2):
                table(p)

                def hop_chunk(c):
                    if not is_chunk(c, 0):
                        for g in range(CHUNK_GROUPS):
                            grp, k, b = CHUNK_GROUPS * (c - 1) + g, g % DEPTH, g % 2
                            act.wait_ge(back_in[p][k], 16 * (CHUNK_GROUPS // DEPTH * (c - 1) + g // DEPTH + 1))
                            act.wait_ge(rhs_ready[p], grp + 1)
                            for s in range(GROUP):
                                ins = a.activation(rhs[b][:, s * W0:s * W0 + D], back[k][:, s * D:(s + 1) * D],
                                                   ACT.Copy, scale=rhs[b][:, s * W0 + D:s * W0 + D + 1])
                            ins.then_inc(scaled[p], 1)
                    if not is_chunk(c, CHUNKS):
                        act.wait_ge(exp_ask[p], c + 1)
                        a.activation(expo[:], expo[:], ACT.Exp).then_inc(exp_done[p], 1)
                chunk_loop(act, hop_chunk, CHUNKS + 1)
                request(lambda: a.activation(small_sd, small_sd, ACT.Sqrt))

        @block.vector
        def _(dve):
            v = nc.vector
            steps = [0]
            asked = [0]
            act_asked = [0]
            flips_asked = [0]

            def link(ins):
                steps[0] += 1
                ins.then_inc(dve_step, 1)
                dve.wait_ge(dve_step, steps[0])

            def ask():
                asked[0] += 1
                dve.sem_inc(to_pe, 1)
                dve.wait_ge(from_pe, asked[0])

            def ask_act():
                act_asked[0] += 1
                dve.sem_inc(act_in, 1)
                dve.wait_ge(act_out, act_asked[0])

            def flip():
                flips_asked[0] += 1
                dve.sem_inc(flip_ready, 1)
                dve.wait_ge(flipped, FLIP_STEPS * flips_asked[0])

            def node_step():
                dve.sem_inc(node_ready, 1)

            dve.wait_ge(const_ready, 1)
            link(v.tensor_copy(iota_row[:], iota_i[:]))
            link(v.tensor_copy(iota_bf[:], iota_i[:]))
            link(v.tensor_copy(iota_col[:], iota_col_i[:]))
            link(v.tensor_copy(tile_no[:], tile_no_i[:]))
            link(v.tensor_copy(identity_bf[:], identity[:]))

            for n in range(4):
                if n < 3:
                    link(v.memset(stage_f if n == 3 else stage_i, -1 if n == 0 else 0))
                else:
                    link(v.memset(stage_f, 0.0))
                dve.sem_inc(stage_free, 1)
                dve.wait_ge(stage_in, 32 * (n + 1))
                link(v.tensor_copy(rec[:, :, n], stage_f if n == 3 else stage_i))
                if n == 0:
                    link(v.tensor_single_scalar(half_i, stage_i, 127, ALU.bitwise_and))
                    link(v.tensor_copy(lo_bf, half_i))
                    link(v.tensor_single_scalar(half_i, stage_i, 7, ALU.arith_shift_right))
                    link(v.tensor_copy(hi_bf, half_i))
            link(v.memset(blank, 0.0))
            link(v.memset(blank.rearrange("p (j f) -> p j f", f=4)[:, :, 0], -1.0))
            dve.sem_inc(blank_ready, 2)
            dve.wait_ge(loaded, 16 * 5)
            link(v.tensor_scalar_add(params[:, 2:3], params[:, 1:2], 1.0))
            link(v.tensor_copy(fcwb[:, 0:D], fcw_sb[:, D:2 * D]))
            link(v.tensor_copy(fcwa[:, 0:D], fcw_sb[:, 0:D]))
            ask()
            link(v.tensor_copy(relT[:], banks[7][0:D, 0:RELS]))
            ask()
            link(v.tensor_copy(ab[:], banks[7][0:D + 1, 0:2 * RELS]))
            dve.wait_ge(blank_done, 16)

            def one_hot_lo(b, first):
                return v.tensor_tensor(oh_lo[b].rearrange("p (s c) -> p s c", s=GROUP),
                                       iota_bf[:].unsqueeze(1).to_broadcast([P, GROUP, P]),
                                       lo_bf[:, bass.ds(first, GROUP)].unsqueeze(2).to_broadcast([P, GROUP, P]),
                                       ALU.is_equal)

            def one_hot_hi(b, first):
                return v.tensor_tensor(oh_hi[b].rearrange("p (s c) -> p s c", s=GROUP),
                                       iota_bf[:, 0:HEAD_TILES].unsqueeze(1).to_broadcast([P, GROUP, HEAD_TILES]),
                                       hi_bf[:, bass.ds(first, GROUP)].unsqueeze(2).to_broadcast([P, GROUP, HEAD_TILES]),
                                       ALU.is_equal)

            def hist_round(i):
                for b in range(2):
                    grp = 2 * i + b
                    at_least(dve, hist_mm, grp - 1)
                    one_hot_lo(b, grp * GROUP)
                    one_hot_hi(b, grp * GROUP).then_inc(hist_oh, 1)
            rounds(dve, IN_ROUNDS, hist_round)
            dve.wait_ge(hist_mm, IN_GROUPS + 1)
            link(v.tensor_copy(hist, banks[6][:, 0:HEAD_TILES]))
            ask()
            link(v.tensor_scalar(tiles_i, banks[7][:, 0:HEAD_TILES], 127.0, None, ALU.add))
            link(v.tensor_single_scalar(tiles_i, tiles_i, 7, ALU.arith_shift_right))
            link(v.tensor_scalar(tiles_f, tiles_i, 1.0, None, ALU.max))
            link(v.tensor_tensor_scan(out=cum, data0=ones[:, 0:HEAD_TILES], data1=tiles_f, initial=0.0,
                                      op0=ALU.mult, op1=ALU.add))
            link(v.tensor_tensor(cum_x, cum, tiles_f, ALU.subtract))
            link(v.scalar_tensor_tensor(start_pos, cum_x, float(P), banks[7][:, P:P + HEAD_TILES], ALU.mult, ALU.add))
            for k in range(BLOCKS):
                link(v.tensor_scalar(junk2[0], cum, tile_no[:, k:k + 1], 0.0, ALU.is_le, ALU.add,
                                     accum_out=tile_f[:, k:k + 1]))
            link(v.tensor_scalar(tile_i, tile_f, float(HEAD_TILES - 1), None, ALU.min))
            dve.sem_inc(tile_i_ready, 1)
            dve.sem_inc(to_pe, 1)

            def prepare_rank(i, k):
                grp, b = DEPTH * i + k, k % 2
                at_least(dve, scattered[k], 16 * GROUP * i)
                v.tensor_copy(rec8[k].rearrange("p (s f) -> p s f", f=4),
                              rec[:, bass.ds(grp * GROUP, GROUP), :]).then_inc(rec_ready, 1)
                yield
                at_least(dve, queried, PAIRS * (grp - 1))
                one_hot_lo(b, grp * GROUP)
                yield
                one_hot_hi(b, grp * GROUP).then_inc(oh_ready, 1)
                yield

            def rank(grp, k):
                b = k % 2
                dve.wait_ge(rec_ready, grp + 1)
                dve.wait_ge(oh_ready, grp + 1)
                at_least(dve, rank_step, 3 * grp)
                for h in range(2):
                    dve.wait_ge(hb_ready, 2 * grp + h + 1)
                    at_least(dve, rank_read, 2 * grp)
                    for s in range(4 * h, 4 * h + 4):
                        width = P * (1 + s % 2)
                        ins = v.scalar_tensor_tensor(
                            junk[s][:, 0:width], banks[1 + h][:, (s % 4 + 1) * P - width:(s % 4 + 1) * P],
                            rec8[k][:, 4 * s:4 * s + 1], earlier2[:, 2 * P - width:2 * P],
                            ALU.is_equal, ALU.mult, accum_out=occ8[b][:, s:s + 1])
                    ins.then_inc(heads_read, 1)
                for h in range(2):
                    dve.wait_ge(queried, PAIRS * grp + 2 * h + 2)
                    for s in range(4 * h, 4 * h + 4):
                        ins = v.tensor_tensor_reduce(
                            out=junk2[s],
                            in0=banks[4 + h][:, (s % 4) * HEAD_TILES:(s % 4 + 1) * HEAD_TILES],
                            in1=oh_hi[b][:, s * HEAD_TILES:(s + 1) * HEAD_TILES], scale=1.0, scalar=0.0,
                            op0=ALU.mult, op1=ALU.add, accum_out=base8[b][:, s:s + 1])
                    ins.then_inc(rank_read, 1)
                dve.wait_ge(rank_read, 2 * grp + 2)
                v.tensor_tensor(pos8[b], occ8[b], base8[b], ALU.add).then_inc(rank_step, 1)

            def destinations(grp, k):
                b = k % 2
                dve.wait_ge(rank_step, 3 * grp + 1)
                at_least(dve, dest_ready, grp)
                v.tensor_single_scalar(pos_lo, pos8[b], 127, ALU.bitwise_and)
                v.tensor_single_scalar(pos_hi, pos8[b], 7, ALU.arith_shift_right)
                v.tensor_scalar(pad8, rec8[k].rearrange("p (s f) -> p s f", f=4)[:, :, 0], 0.0, OUT_OF_BOUNDS,
                                ALU.is_lt, ALU.mult).then_inc(rank_step, 1)
                yield
                dve.wait_ge(rank_step, 3 * grp + 2)
                v.scalar_tensor_tensor(dest_f, pos_lo, float(TILES), pos_hi, ALU.mult, ALU.add).then_inc(rank_step, 1)
                yield
                dve.wait_ge(rank_step, 3 * grp + 3)
                v.tensor_tensor(dest8[k], dest_f, pad8, ALU.add).then_inc(dest_ready, 1)
                yield

            def rank_round(i):
                for k in range(DEPTH):
                    grp = DEPTH * i + k
                    preparing = prepare_rank(i, k)
                    placing = iter(()) if isinstance(grp, int) and grp < 2 else destinations(grp - 2, (k - 2) % DEPTH)
                    for _ in range(3):
                        next(preparing)
                        next(placing, None)
                    if not (isinstance(grp, int) and grp == 0):
                        rank(grp - 1, (k - 1) % DEPTH)
            rounds(dve, RANK_ROUNDS, rank_round)
            for _ in destinations(IN_GROUPS - 2, DEPTH - 2):
                pass
            rank(IN_GROUPS - 1, DEPTH - 1)
            for _ in destinations(IN_GROUPS - 1, DEPTH - 1):
                pass
            dve.wait_ge(dest_ready, IN_GROUPS)
            for k in range(DEPTH):
                dve.wait_ge(scattered[k], 16 * GROUP * RANK_ROUNDS)
            dve.sem_inc(sort_read, 1)

            dve.wait_ge(srec_in, 16)
            dve.wait_ge(tile_loaded, 16)
            link(v.tensor_copy(em, srec[:, :, 0]))
            link(v.tensor_copy(tail_i, srec[:, :, 1]))
            link(v.tensor_copy(types, srec[:, :, 2]))
            link(v.tensor_copy(weight, srec[:, :, 3]))
            same_i = part(A_NS, TILES, I32)
            link(v.tensor_copy(same_i, em))
            link(v.tensor_single_scalar(same_i, same_i, 127, ALU.bitwise_and))
            link(v.tensor_scalar(scan_a, em, 0.0, -1000.0, ALU.is_lt, ALU.mult))
            link(v.tensor_tensor(local_head, same_i, scan_a, ALU.add))
            flip()
            link(v.tensor_copy(edge_col, scan_a[:, TILES - 1:TILES]))
            ask()
            link(v.tensor_copy(edge_in, banks[7][:, 0:1]))
            link(v.tensor_tensor(same[:, 1:TILES], scan_a[:, 1:TILES], scan_a[:, 0:TILES - 1], ALU.is_equal))
            link(v.tensor_tensor(same[:, 0:1], scan_a[:, 0:1], edge_in, ALU.is_equal))
            link(v.memset(same[0:1, 0:1], 0.0))
            ask()
            link(v.tensor_copy(same[:, TILES:TILES + 1], banks[7][:, 0:1]))
            dve.sem_inc(flags_ready, 1)
            first = same[:, 0:TILES]
            after = same[:, 1:TILES + 1]

            def layernorm(v3, t3):
                mean = small_mean
                link(v.tensor_reduce(mean, v3, AX.X, ALU.add))
                link(v.tensor_scalar(mean, mean, 1.0 / D, None, ALU.mult))
                link(v.tensor_tensor(v3, v3, mean.unsqueeze(2).to_broadcast([P, HEAD_TILES, D]), ALU.subtract))
                link(v.tensor_tensor(t3, v3, v3, ALU.mult))
                link(v.tensor_reduce(small_sd, t3, AX.X, ALU.add))
                link(v.tensor_scalar(small_sd, small_sd, 1.0 / D, 1e-5, ALU.mult, ALU.add))
                ask_act()
                link(v.reciprocal(small_sd, small_sd))
                link(v.tensor_tensor(v3, v3, small_sd.unsqueeze(2).to_broadcast([P, HEAD_TILES, D]), ALU.mult))
                link(v.tensor_scalar(v3, v3, 0.0, None, ALU.max))

            def unit_rows(v3, t3):
                link(v.tensor_tensor(t3, v3, v3, ALU.mult))
                link(v.tensor_reduce(small_sd, t3, AX.X, ALU.add))
                ask_act()
                link(v.tensor_scalar(small_sd, small_sd, 1e-12, None, ALU.max))
                link(v.reciprocal(small_sd, small_sd))
                link(v.tensor_tensor(v3, v3, small_sd.unsqueeze(2).to_broadcast([P, HEAD_TILES, D]), ALU.mult))

            link(v.memset(val, 0.0))
            node_step()
            dve.wait_ge(node_in, 32)
            layernorm(val3, tmp3)
            unit_rows(val3, tmp3)
            node_step()
            dve.wait_ge(node_out, 16)

            def row_carry(back, biggest):
                ask()
                link(v.tensor_copy(rows1[:, 0:2 * P], banks[7][0:1, 0:2 * P]))
                step = -1 if back else 1
                if back:
                    link(v.memset(carried_row[:, P + 3:P + 4], 0.0))
                    out = carried_row[:, 3:P + 3]
                else:
                    link(v.memset(carried_row[:, 0:1], NEG if biggest else 0.0))
                    out = carried_row[:, 1:P + 1]
                link(v.tensor_tensor_scan(
                    out=out[:, ::step], data0=reset_row[:, ::step], data1=max_row[:, ::step],
                    initial=NEG if biggest else 0.0,
                    op0=ALU.add if biggest else ALU.mult, op1=ALU.max if biggest else ALU.add))
                ask()
                link(v.tensor_copy(carry_in, banks[7][:, 2 * P:2 * P + 1]))

            def forward(out, data0, data1, biggest):
                ops = dict(op0=ALU.add, op1=ALU.max) if biggest else dict(op0=ALU.mult, op1=ALU.add)
                init = NEG if biggest else 0.0
                link(v.tensor_tensor_scan(out=out, data0=data0, data1=data1, initial=init, **ops))
                link(v.tensor_copy(carry_col, out[:, TILES - 1:TILES]))
                link(v.tensor_reduce(reset_col, data0, AX.X, ALU.min))
                row_carry(False, biggest)
                link(v.tensor_tensor_scan(out=out, data0=data0, data1=data1, initial=carry_in, **ops))

            def spread(out, at_end):
                ops = dict(op0=ALU.mult, op1=ALU.add)
                link(v.tensor_tensor_scan(out=out[:, ::-1], data0=after[:, ::-1], data1=at_end[:, ::-1],
                                          initial=0.0, **ops))
                link(v.tensor_copy(carry_col, out[:, 0:1]))
                link(v.tensor_reduce(reset_col, after, AX.X, ALU.min))
                row_carry(True, False)
                link(v.tensor_tensor_scan(out=out[:, ::-1], data0=after[:, ::-1], data1=at_end[:, ::-1],
                                          initial=carry_in, **ops))

            def only_last(out, in_):
                link(v.tensor_tensor(out, in_, after, ALU.mult))
                link(v.tensor_tensor(out, in_, out, ALU.subtract))

            flip()
            link(v.tensor_tensor(scan_b, scan_a, scan_a, ALU.mult))
            forward(scan_c, first, scan_b, False)
            only_last(scan_d, scan_c)
            spread(scan_b, scan_d)
            ask_act()
            link(v.tensor_scalar(scan_b, scan_b, 1e-12, None, ALU.max))
            link(v.reciprocal(scan_b, scan_b))
            link(v.tensor_tensor(scan_a, scan_a, scan_b, ALU.mult))
            link(v.tensor_scalar(scan_a, scan_a, params[:, 0:1], None, ALU.mult))

            def head_max():
                link(v.tensor_scalar(scan_b, first, 1.0, -NEG, ALU.subtract, ALU.mult))
                forward(scan_c, scan_b, scan_a, True)
                only_last(scan_d, scan_c)
                spread(scan_b, scan_d)

            head_max()
            link(v.tensor_scalar(scan_b, scan_b, params[:, 0:1], None, ALU.max))
            link(v.tensor_scalar(scan_c, scan_b, params[:, 0:1], None, ALU.subtract))
            only_last(scan_d, scan_c)
            link(v.tensor_copy(scan_c, scan_d))
            link(v.tensor_tensor(scan_b, scan_a, scan_b, ALU.subtract))
            ask_act()
            flip()
            flip()

            def sums(p):
                link(v.memset(acc, 0.0))
                dve.sem_inc(sum_begin[p], 1)

                def indices(i, k):
                    at_least(dve, gathered[0][k], 16 * GROUP * i)
                    v.tensor_copy(idx8[k], tail_i[:, bass.ds((DEPTH * i + k) * GROUP, GROUP)]).then_inc(idx_ready[0], 1)

                def prepare(grp, b):
                    at_least(dve, summed[p], 2 * grp - 2)
                    r3 = rhs[b].rearrange("p (s c) -> p s c", c=W0)
                    v.tensor_copy(r3[:, :, D], weight[:, bass.ds(grp * GROUP, GROUP)])
                    v.tensor_copy(r3[:, :, D + 1], em[:, bass.ds(grp * GROUP, GROUP)])
                    v.tensor_tensor(oh[b].rearrange("p (s c) -> p s c", s=GROUP),
                                    iota_row[:].unsqueeze(1).to_broadcast([P, GROUP, P]),
                                    local_head[:, bass.ds(grp * GROUP, GROUP)].unsqueeze(2).to_broadcast([P, GROUP, P]),
                                    ALU.is_equal).then_inc(rhs_ready[p], 1)

                def add(grp, b):
                    _, tiles = nc.values_load_multi_w_load_instructions(
                        tile_of[:, bass.ds(grp * GROUP, GROUP)], engines=[mybir.EngineType.DVE], min_val=0,
                        max_val=HEAD_TILES - 1, skip_runtime_bounds_check_because="clamped when made")
                    for h in range(2):
                        dve.wait_ge(summed[p], 2 * grp + h + 1)
                        at_least(dve, added[p], 2 * grp + h)
                        to = acc[:, bass.ds(tiles[HALF * h] * W0, WINDOW)]
                        v.tensor_tensor(to, to, banks[2 * b + h][:, 0:WINDOW], ALU.add).then_inc(added[p], 1)

                def sum_round(i):
                    for k in range(DEPTH):
                        if not isinstance(i, int) or DEPTH * i + k + 2 < GROUPS:
                            indices(i + (k + 2) // DEPTH, (k + 2) % DEPTH)
                        prepare(DEPTH * i + k, k % 2)
                        if not (isinstance(i, int) and i == k == 0):
                            add(DEPTH * i + k - 1, (k - 1) % 2)
                indices(0, 0)
                indices(0, 1)
                rounds(dve, GATHER_ROUNDS, sum_round)
                add(GROUPS - 1, 1)
                dve.wait_ge(added[p], 2 * GROUPS)

            sums(0)
            link(v.tensor_copy(small_mean, acc3[:, :, D + 1]))
            link(v.tensor_scalar(small_sd, small_mean, -1.0, None, ALU.mult))
            ask_act()
            link(v.memset(val, 0.0))
            node_step()
            dve.wait_ge(node_in, 32 + 48)
            sd3 = small_sd.unsqueeze(2).to_broadcast([P, HEAD_TILES, D])
            link(v.tensor_tensor(small_mean, acc3[:, :, D], small_sd, ALU.add))
            link(v.tensor_scalar(small_mean, small_mean, 1e-16, None, ALU.add))
            link(v.reciprocal(small_mean, small_mean))
            link(v.tensor_tensor(scratch3, tmp3, sd3, ALU.mult))
            link(v.tensor_tensor(acc3[:, :, 0:D], acc3[:, :, 0:D], scratch3, ALU.add))
            link(v.tensor_tensor(acc3[:, :, 0:D], acc3[:, :, 0:D],
                                 small_mean.unsqueeze(2).to_broadcast([P, HEAD_TILES, D]), ALU.mult))
            link(v.tensor_scalar(tmp, tmp, params[:, 2:3], None, ALU.mult))
            link(v.tensor_tensor(tmp3, tmp3, acc3[:, :, 0:D], ALU.add))
            link(v.tensor_tensor(val, val, tmp, ALU.add))
            node_step()
            dve.wait_ge(node_out, 32)
            layernorm(val3, tmp3)

            def scan_chunk(p, c, between):
                done = [0]
                answers = [0]

                def clink(ins):
                    done[0] += 1
                    ins.then_inc(scan_step[p], 1)
                    dve.wait_ge(scan_step[p], HOP_STEPS * c + done[0])

                def ask_pe():
                    answers[0] += 1
                    dve.sem_inc(scan_ask[p], 1)
                    dve.wait_ge(scan_ans[p], HOP_ASKS * c + answers[0])

                reset = reset2[:, bass.ds(c * P, P)]
                dve.wait_ge(score_done[p], CHUNK_GROUPS * (c + 1))
                v.tensor_copy(after_c[:], after2[:, bass.ds(c * P, P)])
                ask_pe()
                clink(v.tensor_scalar(scan_v[:], banks[6][:, 0:P], LEAKY, None, ALU.mult))
                clink(v.tensor_tensor(leaky[:], scan_v[:], banks[6][:, 0:P], ALU.max))
                clink(v.tensor_tensor_scan(out=scan_y[:], data0=reset, data1=leaky[:], initial=NEG,
                                           op0=ALU.add, op1=ALU.max))
                clink(v.tensor_copy(reset_col, reset_min[:, bass.ds(c, 1)]))
                ask_pe()
                clink(v.tensor_copy(rows1[:, 0:2 * P], banks[7][0:1, 0:2 * P]))
                clink(v.tensor_copy(carried_row[:, 0:1], carried_row[:, P:P + 1]))
                clink(v.tensor_tensor_scan(out=carried_row[:, 1:P + 1], data0=reset_row, data1=max_row,
                                           initial=carried_row[:, 0:1], op0=ALU.add, op1=ALU.max))
                ask_pe()
                clink(v.tensor_copy(carry_in, banks[7][:, 2 * P:2 * P + 1]))
                clink(v.tensor_tensor_scan(out=scan_y[:], data0=reset, data1=leaky[:], initial=carry_in,
                                           op0=ALU.add, op1=ALU.max))
                clink(v.tensor_tensor(scan_v[:], scan_y[:], after_c[:], ALU.mult))
                clink(v.tensor_tensor(scan_v[:], scan_y[:], scan_v[:], ALU.subtract))
                clink(v.tensor_tensor_scan(out=scan_z[:, ::-1], data0=after_c[:, ::-1], data1=scan_v[:, ::-1],
                                           initial=0.0, op0=ALU.mult, op1=ALU.add))
                clink(v.tensor_copy(reset_col, after_min[:, bass.ds(c, 1)]))
                ask_pe()
                clink(v.tensor_copy(rows1[:, 0:2 * P], banks[7][0:1, 0:2 * P]))
                clink(v.tensor_tensor_scan(out=back_row[:, 0:P][:, ::-1], data0=reset_row[:, ::-1],
                                           data1=max_row[:, ::-1], initial=0.0, op0=ALU.mult, op1=ALU.add))
                ask_pe()
                clink(v.tensor_copy(carry_in, banks[7][:, 2 * P:2 * P + 1]))
                clink(v.tensor_tensor_scan(out=scan_z[:, ::-1], data0=after_c[:, ::-1], data1=scan_v[:, ::-1],
                                           initial=carry_in, op0=ALU.mult, op1=ALU.add))
                clink(v.tensor_tensor(expo[:, 0:P], leaky[:], scan_z[:], ALU.subtract))
                last = expo[0:1, P:P + 1]
                clink(v.memset(expo[:, P:P + 1], 0.0))
                clink(v.tensor_tensor(last, carried_row[:, 0:1], scan_z[0:1, 0:1], ALU.subtract))
                clink(v.scalar_tensor_tensor(last, reset2[0:1, bass.ds(c * P, 1)], 0.0, last, ALU.is_equal, ALU.mult))
                dve.sem_inc(exp_ask[p], 1)
                between()
                dve.wait_ge(exp_done[p], c + 1)
                clink(v.tensor_scalar(last, last, 1.0, None, ALU.subtract))
                clink(v.tensor_scalar(factor_row, iota_row[0:1, :], local_head[0:1, bass.ds(c * P, 1)], last, ALU.is_equal, ALU.mult))
                clink(v.tensor_scalar(factor_row, factor_row, 1.0, None, ALU.add))
                ask_pe()
                clink(v.tensor_copy(wt_c[:], banks[6][:, P:2 * P]))
                clink(v.tensor_copy(rescale[:], banks[7][:, 2 * P + 1:2 * P + 2]))
                assert (done[0], answers[0]) == (HOP_STEPS, HOP_ASKS), (done, answers)

            def hop(p):
                link(v.memset(acc, 0.0))
                link(v.memset(back_row[:, P:P + 1], 0.0))
                link(v.memset(carried_row[:, P:P + 1], NEG))
                half = P // 2

                def indices(c, n):
                    v.tensor_copy(idx_c[:, n * half:(n + 1) * half],
                                  tail_i[:, bass.ds(c * P + n * half, half)]).then_inc(idx_ready[p], 1)

                def prepare_score(c, g):
                    grp, b = CHUNK_GROUPS * c + g, g % 2
                    at_least(dve, p_done[p], grp - 1)
                    dve.wait_ge(hlb_ready[p], grp + 1)
                    v.tensor_scalar(oh_t[b], banks[4 + b][:].bitcast(BF16), iota_col[:], None,
                                    ALU.is_equal).then_inc(oht_ready[p], 1)
                    v.tensor_tensor(type_oh[b].rearrange("p (s c) -> p s c", s=GROUP),
                                    iota_row[:, 0:RELS].unsqueeze(1).to_broadcast([P, GROUP, RELS]),
                                    type_c[:, g * GROUP:(g + 1) * GROUP].unsqueeze(2).to_broadcast([P, GROUP, RELS]),
                                    ALU.is_equal).then_inc(toh_ready[p], 1)

                def prepare_sum(c, g):
                    grp, b = CHUNK_GROUPS * (c - 1) + g, g % 2
                    at_least(dve, summed[p], 2 * grp - 2)
                    v.tensor_copy(rhs[b].rearrange("p (s c) -> p s c", c=W0)[:, :, D], wt_c[:, g * GROUP:(g + 1) * GROUP])
                    v.tensor_tensor(oh[b].rearrange("p (s c) -> p s c", s=GROUP),
                                    iota_row[:].unsqueeze(1).to_broadcast([P, GROUP, P]),
                                    hl_s[:, g * GROUP:(g + 1) * GROUP].unsqueeze(2).to_broadcast([P, GROUP, P]),
                                    ALU.is_equal).then_inc(rhs_ready[p], 1)

                def score_ops(c, g):
                    grp, b, k = CHUNK_GROUPS * c + g, g % 2, g % DEPTH
                    z3 = zed.rearrange("p (s c) -> p s c", s=GROUP)
                    dve.wait_ge(gathered[p][k], 16 * GROUP * (CHUNK_GROUPS // DEPTH * c + g // DEPTH + 1))
                    dve.wait_ge(p_done[p], grp + 1)
                    at_least(dve, score_done[p], grp)
                    v.tensor_tensor(z3, banks[b][:, 0:GROUP * RELS].rearrange("p (s c) -> p s c", s=GROUP),
                                    rows[k].rearrange("p (s r) -> p s r", r=ROW)[:, :, D:D + RELS],
                                    ALU.add).then_inc(z_step[p], 1)
                    yield
                    dve.wait_ge(toh_ready[p], grp + 1)
                    dve.wait_ge(z_step[p], 2 * grp + 1)
                    v.tensor_tensor(zed, zed, type_oh[b], ALU.mult).then_inc(z_step[p], 1)
                    yield
                    dve.wait_ge(z_step[p], 2 * grp + 2)
                    v.tensor_reduce(e_c[:, g * GROUP:(g + 1) * GROUP], z3, AX.X, ALU.add).then_inc(score_done[p], 1)
                    yield

                def add_ops(c, g):
                    grp = CHUNK_GROUPS * (c - 1) + g
                    _, tiles = nc.values_load_multi_w_load_instructions(
                        tile_of[:, bass.ds(grp * GROUP, GROUP)], engines=[mybir.EngineType.DVE], min_val=0,
                        max_val=HEAD_TILES - 1, skip_runtime_bounds_check_because="clamped when made")
                    if g == 0:
                        at_least(dve, added[p], 2 * CHUNK_GROUPS * (c - 1))
                        to = acc[:, bass.ds(tiles[0] * W0, D + 1)]
                        v.tensor_scalar(to, to, rescale[:], None, ALU.mult).then_inc(rescaled[p], 1)
                        dve.wait_ge(rescaled[p], c)
                    for h in range(2):
                        dve.wait_ge(summed[p], 2 * grp + h + 1)
                        at_least(dve, added[p], 2 * grp + h)
                        to = acc[:, bass.ds(tiles[HALF * h] * W0, WINDOW)]
                        v.tensor_tensor(to, to, banks[2 + h][:, 0:WINDOW], ALU.add).then_inc(added[p], 1)
                        yield

                def work(c, g):
                    scores = score_ops(c, g - 1) if not is_chunk(c, CHUNKS) and g else iter(())
                    if g == 1 and not is_chunk(c, 0, 1):
                        adds = add_ops(c - 1, CHUNK_GROUPS - 1)
                    elif g < 2 or is_chunk(c, 0) or (g == CHUNK_GROUPS and not is_chunk(c, CHUNKS)):
                        adds = iter(())
                    else:
                        adds = add_ops(c, g - 2)
                    next(scores, None)
                    if not is_chunk(c, 0) and g < CHUNK_GROUPS:
                        prepare_sum(c, g)
                    next(scores, None)
                    next(adds, None)
                    next(scores, None)
                    next(adds, None)

                def hop_chunk(c):
                    scoring = not is_chunk(c, CHUNKS)
                    if not is_chunk(c, 0):
                        v.tensor_copy(hl_s[:], hl_c[:]).then_inc(chunk_step[p], 1)
                        dve.wait_ge(chunk_step[p], c)
                    if scoring:
                        v.tensor_copy(hl_c[:], local_head[:, bass.ds(c * P, P)])
                        v.tensor_copy(type_c[:], types[:, bass.ds(c * P, P)]).then_inc(hl_ready[p], 1)
                        dve.wait_ge(hl_ready[p], c + 1)
                    for g in range(CHUNK_GROUPS):
                        if g == CHUNK_GROUPS // 2 + 1 and not is_chunk(c, CHUNKS - 1, CHUNKS):
                            indices(c + 1, 0)
                        if scoring:
                            prepare_score(c, g)
                        work(c, g)
                    work(c, CHUNK_GROUPS)
                    if not is_chunk(c, CHUNKS - 1, CHUNKS):
                        indices(c + 1, 1)
                    if scoring:
                        scan_chunk(p, c, lambda: is_chunk(c, 0) or list(add_ops(c, CHUNK_GROUPS - 2)))
                    if is_chunk(c, CHUNKS):
                        for _ in add_ops(c, CHUNK_GROUPS - 1):
                            pass

                indices(0, 0)
                indices(0, 1)
                chunk_loop(dve, hop_chunk, CHUNKS + 1)
                dve.wait_ge(added[p], 2 * GROUPS)

            dve.wait_ge(flags_in, 32)
            link(v.tensor_scalar(reset2, reset2, 1.0, -NEG, ALU.subtract, ALU.mult))
            link(v.tensor_scalar(not_last[:], iota_col[:], float(P - 1), None, ALU.is_lt))
            ends = after2.rearrange("r (c p) -> r c p", p=P)[:, :, P - 1]
            link(v.tensor_scalar(ends, ends, not_last[:], None, ALU.mult))
            link(v.tensor_reduce(reset_min[:], reset2.rearrange("r (c p) -> r c p", p=P), AX.X, ALU.min))
            link(v.tensor_reduce(after_min[:], after2.rearrange("r (c p) -> r c p", p=P), AX.X, ALU.min))

            for p in (1, 2):
                link(v.memset(part(A_T, 2 * TAB * ROW), 0.0))
                link(v.memset(part(A_T + 2 * TAB * P, 2 * TAB * P), 1.0))
                dve.sem_inc(tab_ready[p], 1)
                for n in range(TAB_STEPS):
                    b = n % 2
                    dve.wait_ge(tab_mm[p], n + 1)
                    for m, count in ((0, 4), (4, TAB - 4)):
                        both = banks[4 + 2 * b + m // 4][:, 0:count * 2 * RELS].rearrange("p (m c) -> p m c", m=count)
                        v.tensor_copy(stg[b][:, m:m + count, D:D + RELS], both[:, :, 0:RELS])
                        first_rel = (n * TAB + m) * RELS
                        ins = v.tensor_copy(p_tab[:, first_rel:first_rel + count * RELS].rearrange("p (m c) -> p m c", m=count),
                                            both[:, :, RELS:2 * RELS])
                    ins.then_inc(tab_staged[p], 1)
                for b in range(2):
                    dve.wait_ge(tab_out[p][b], 16 * (TAB_STEPS // 2))
                hop(p)
                node_step()
                link(v.tensor_scalar(small_mean, acc3[:, :, D], 1e-30, None, ALU.max))
                link(v.reciprocal(small_mean, small_mean))
                link(v.tensor_tensor(val3, acc3[:, :, 0:D], small_mean.unsqueeze(2).to_broadcast([P, HEAD_TILES, D]),
                                     ALU.mult))
                dve.wait_ge(node_in, 80 + 16 * p)
                link(v.tensor_tensor(val, val, tmp, ALU.add))
                unit_rows(val3, tmp3)
            node_step()
            dve.wait_ge(node_in, 80 + 48)
            link(v.tensor_tensor(val, val, tmp, ALU.add))
            node_step()

        @block.tensor
        def _(pe):
            t = nc.tensor
            asked = [0]

            def run(lot):
                asked[0] += 1
                pe.wait_ge(to_pe, asked[0])
                for kind, out, lhs, r in lot[:-1]:
                    (t.transpose(out, lhs, r) if kind == "T" else t.matmul(out, lhs, r, start=True, stop=True))
                kind, out, lhs, r = lot[-1]
                (t.transpose(out, lhs, r) if kind == "T"
                 else t.matmul(out, lhs, r, start=True, stop=True)).then_inc(from_pe, 1)

            def carry(back):
                run([("T", banks[7][0:1, 0:P], carry_col, identity[:]),
                     ("T", banks[7][0:1, P:2 * P], reset_col, identity[:])])
                at = 4 if back else 0
                run([("T", banks[7][:, 2 * P:2 * P + 1], carried_row[:, at:at + P], identity[0:1, 0:1])])

            run([("T", banks[7][0:D, 0:RELS], rel_sb[:], identity[0:RELS, 0:RELS])])
            run([("M", banks[7][0:D + 1, 0:RELS], fcwb[:], relT[:]),
                 ("M", banks[7][0:D + 1, RELS:2 * RELS], fcwa[:], relT[:])])

            count = banks[6][:, 0:HEAD_TILES]
            t.matmul(count, zeros_bf[:], zeros_bf[:, 0:HEAD_TILES], start=True, stop=False, skip_group_check=True)

            def hist_round(i):
                for b in range(2):
                    pe.wait_ge(hist_oh, 2 * i + b + 1)
                    for s in range(GROUP):
                        ins = t.matmul(count, oh_lo[b][:, s * P:(s + 1) * P],
                                       oh_hi[b][:, s * HEAD_TILES:(s + 1) * HEAD_TILES],
                                       start=False, stop=False, skip_group_check=True)
                    ins.then_inc(hist_mm, 1)
            rounds(pe, IN_ROUNDS, hist_round)
            t.matmul(count, zeros_bf[:], zeros_bf[:, 0:HEAD_TILES], start=False, stop=True,
                     skip_group_check=True).then_inc(hist_mm, 1)
            run([("M", banks[7][:, 0:HEAD_TILES], ones[:], hist),
                 ("M", banks[7][:, P:P + HEAD_TILES], lower_of[:], hist)])

            nxt = banks[0][:, 0:HEAD_TILES]
            asked[0] += 1
            pe.wait_ge(to_pe, asked[0])
            t.matmul(nxt, identity[:], start_pos, start=True, stop=False, skip_group_check=True).then_inc(updated, 1)

            def heads_as_rows(grp, k, h):
                pe.wait_ge(rec_ready, grp + 1)
                at_least(pe, heads_read, 2 * grp + h - 1)
                for s in range(4 * h, 4 * h + 4):
                    ins = t.transpose(banks[1 + h][:, (s % 4) * P:(s % 4 + 1) * P],
                                      rec8[k][:, 4 * s:4 * s + 1].to_broadcast([P, P]), identity[:])
                ins.then_inc(hb_ready, 1)

            def lo_transposed(grp, b):
                pe.wait_ge(oh_ready, grp + 1)
                at_least(pe, lo_t_ready, grp - 1)
                for s in range(GROUP):
                    ins = t.transpose(banks[6 + b][:].bitcast(BF16)[:, s * P:(s + 1) * P],
                                      oh_lo[b][:, s * P:(s + 1) * P], identity_bf[:])
                ins.then_inc(ot_ready, 1)

            def rank_round(i):
                for k in range(DEPTH):
                    grp, b = DEPTH * i + k, k % 2
                    more = not (isinstance(grp, int) and grp == IN_GROUPS - 1)
                    for q in range(PAIRS):
                        n, h = grp * PAIRS + q, q // 2
                        pe.wait_ge(counts_ready, n + 1)
                        for s in (2 * q, 2 * q + 1):
                            ins = t.matmul(nxt, oh_lo[b][:, s * P:(s + 1) * P],
                                           oh_hi[b][:, s * HEAD_TILES:(s + 1) * HEAD_TILES],
                                           start=False, stop=False, skip_group_check=True)
                        ins.then_inc(updated, 1)
                        if q == 0:
                            pe.wait_ge(lo_t_ready, grp + 1)
                        if q % 2 == 0:
                            at_least(pe, rank_read, 2 * grp + h - 1)
                        for s in (2 * q, 2 * q + 1):
                            ins = t.matmul(banks[4 + h][:, (s % 4) * HEAD_TILES:(s % 4 + 1) * HEAD_TILES],
                                           lo_t[b][:, s * P:(s + 1) * P], counts[q % 2], start=True, stop=True)
                        ins.then_inc(queried, 1)
                        if q < 2:
                            heads_as_rows(grp, k, q)
                        if more and q == 2:
                            lo_transposed(grp + 1, (k + 1) % 2)
            lo_transposed(0, 0)
            rounds(pe, RANK_ROUNDS, rank_round)

            def flip(n):
                pe.wait_ge(flip_ready, n + 1)
                for m, (k, count) in enumerate(flip_lots):
                    at_least(pe, flipped, FLIP_STEPS * n + m - 1)
                    for c in range(count):
                        ins = t.transpose(flip_banks[m % 2][:, c * P:(c + 1) * P], flip_from(n, k + c), identity[:])
                    ins.then_inc(flip_mm, 1)

            flip(0)
            run([("M", banks[7][:, 0:1], from_prev[:], edge_col)])
            run([("M", banks[7][:, 0:1], from_next[:], same[:, 0:1])])
            flip(1)
            carry(False)
            carry(True)
            carry(False)
            carry(True)
            flip(2)
            flip(3)

            def in_window(window, tile, first, n, width):
                if n == 0:
                    return window[:, 0:width]
                slot = nc.s_assert_within(tile - first, 0, n, skip_runtime_bounds_check_because=
                                          "every head tile has an edge tile, so the next is at most one further")
                return window[:, bass.ds(slot * W0, width)]

            def add_window(window, tiles, h, one_hot, right, width):
                first = tiles[HALF * h]
                t.matmul(window[:, 0:WINDOW], zeros_bf[:], zeros_wide[:, 0:WINDOW], start=True, stop=False,
                         skip_group_check=True)
                for n in range(HALF):
                    s = HALF * h + n
                    ins = t.matmul(in_window(window, tiles[s], first, n, width), one_hot[:, s * P:(s + 1) * P],
                                   right[:, s * W0:s * W0 + width], start=False, stop=n == HALF - 1,
                                   skip_group_check=True)
                return ins

            def sums(p):
                def one(i):
                    for b in range(2):
                        grp = 2 * i + b
                        pe.wait_ge(rhs_ready[p], grp + 1)
                        pe.wait_ge(scaled[p], grp + 1)
                        at_least(pe, added[p], 2 * grp - 2)
                        _, tiles = nc.values_load_multi_w_load_instructions(
                            tile_of[:, bass.ds(grp * GROUP, GROUP)], engines=[mybir.EngineType.PE], min_val=0,
                            max_val=HEAD_TILES - 1, skip_runtime_bounds_check_because="clamped when made")
                        for h in range(2):
                            add_window(banks[2 * b + h], tiles, h, oh[b], rhs[b], W0).then_inc(summed[p], 1)
                rounds(pe, ROUNDS, one)

            sums(0)
            for p in (1, 2):
                pe.wait_ge(tab_ready[p], 1)

                for n in range(TAB_STEPS):
                    b = n % 2
                    pe.wait_ge(tab_emb[p], n + 1)
                    at_least(pe, tab_copied[p], n - 1)
                    for m in range(TAB):
                        ins = t.transpose(banks[2 * b + m // 4][:, (m % 4) * P:(m % 4 + 1) * P], stg[b][:, m, :],
                                          identity[:])
                    ins.then_inc(tab_t[p], 1)
                    pe.wait_ge(tab_copied[p], n + 1)
                    at_least(pe, tab_staged[p], n - 1)
                    for m in range(TAB):
                        ins = t.matmul(banks[4 + 2 * b + m // 4][:, (m % 4) * 2 * RELS:(m % 4 + 1) * 2 * RELS],
                                       emb_t[b][:, m * P:(m + 1) * P], ab[:], start=True, stop=True)
                    ins.then_inc(tab_mm[p], 1)
                pe.wait_ge(tab_staged[p], TAB_STEPS)

                def chunk_heads_as_rows(c, g):
                    grp = CHUNK_GROUPS * c + g
                    at_least(pe, oht_ready[p], grp - 1)
                    for s in range(GROUP):
                        ins = t.transpose(banks[4 + g % 2][:].bitcast(BF16)[:, s * P:(s + 1) * P],
                                          hl_c[:, g * GROUP + s:g * GROUP + s + 1].to_broadcast([P, P]), identity_bf[:])
                    ins.then_inc(hlb_ready[p], 1)

                def head_tiles(c, g):
                    return nc.values_load_multi_w_load_instructions(
                        tile_of[:, bass.ds((CHUNK_GROUPS * c + g) * GROUP, GROUP)], engines=[mybir.EngineType.PE],
                        min_val=0, max_val=HEAD_TILES - 1, skip_runtime_bounds_check_because="clamped when made")[1]

                def head_terms(c, g):
                    grp, b = CHUNK_GROUPS * c + g, g % 2
                    tiles = head_tiles(c, g)
                    at_least(pe, z_step[p], 2 * grp - 3)
                    pe.wait_ge(oht_ready[p], grp + 1)
                    for s in range(GROUP):
                        ins = t.matmul(banks[b][:, s * RELS:(s + 1) * RELS], oh_t[b][:, s * P:(s + 1) * P],
                                       p_tab[:, bass.ds(tiles[s] * RELS, RELS)], start=True, stop=True)
                    ins.then_inc(p_done[p], 1)

                def weighted_sum(c, g, h, tiles):
                    grp, b = CHUNK_GROUPS * (c - 1) + g, g % 2
                    if h == 0:
                        pe.wait_ge(rhs_ready[p], grp + 1)
                        pe.wait_ge(scaled[p], grp + 1)
                    at_least(pe, added[p], 2 * grp + h - 1)
                    add_window(banks[2 + h], tiles, h, oh[b], rhs[b], D + 1).then_inc(summed[p], 1)

                def hop_chunk(c):
                    scoring, summing = not is_chunk(c, CHUNKS), not is_chunk(c, 0)
                    if scoring:
                        pe.wait_ge(hl_ready[p], c + 1)
                        chunk_heads_as_rows(c, 0)
                    for g in range(CHUNK_GROUPS):
                        if scoring:
                            head_terms(c, g)
                            if g + 1 < CHUNK_GROUPS:
                                chunk_heads_as_rows(c, g + 1)
                        if summing and g and not (scoring and g == CHUNK_GROUPS - 1):
                            tiles = head_tiles(c - 1, g - 1)
                            weighted_sum(c, g - 1, 0, tiles)
                            weighted_sum(c, g - 1, 1, tiles)
                    if summing and scoring:
                        tiles = head_tiles(c - 1, CHUNK_GROUPS - 2)
                    elif summing:
                        tiles = head_tiles(c - 1, CHUNK_GROUPS - 1)
                        weighted_sum(c, CHUNK_GROUPS - 1, 0, tiles)
                        weighted_sum(c, CHUNK_GROUPS - 1, 1, tiles)
                    if scoring:
                        def to_rows(carried):
                            return [(banks[7][0:1, 0:P], carried, identity[:]),
                                    (banks[7][0:1, P:2 * P], reset_col, identity[:])]
                        lots = [
                            [(banks[6][:, 0:P], e_c[:], identity[:])],
                            to_rows(scan_y[:, P - 1:P]),
                            [(banks[7][:, 2 * P:2 * P + 1], carried_row[:, 0:P], identity[0:1, 0:1])],
                            to_rows(scan_z[:, 0:1]),
                            [(banks[7][:, 2 * P:2 * P + 1], back_row[:, 1:P + 1], identity[0:1, 0:1])],
                            [(banks[6][:, P:2 * P], expo[:, 0:P], identity[:]),
                             (banks[7][:, 2 * P + 1:2 * P + 2], factor_row, identity[0:1, 0:1])],
                        ]
                        assert len(lots) == HOP_ASKS
                        for n, lot in enumerate(lots):
                            pe.wait_ge(scan_ask[p], HOP_ASKS * c + n + 1)
                            pe.sem_inc(lots_begun, 1)
                            for out, lhs, r in lot:
                                ins = t.transpose(out, lhs, r)
                            ins.then_inc(scan_ans[p], 1)
                            if summing and n in (0, 2):
                                weighted_sum(c, CHUNK_GROUPS - 2, n // 2, tiles)
                        if summing:
                            tiles = head_tiles(c - 1, CHUNK_GROUPS - 1)
                            weighted_sum(c, CHUNK_GROUPS - 1, 0, tiles)
                            weighted_sum(c, CHUNK_GROUPS - 1, 1, tiles)
                chunk_loop(pe, hop_chunk, CHUNKS + 1)


_INS = ['x', 'src', 'dst', 'edge_type_50', 'edge_weight', 'L0_gnn_beta', 'L0_gnn_eps', 'L1_gnn_relation_emb',
        'L1_gnn_fc_w', 'L1_gnn_fc_b']


def kernel(**inputs):
    import numpy as _np
    import concourse.bacc as _bacc
    from concourse import mybir as _mybir
    from concourse.bass_utils import run_bass_kernel_spmd as _run

    nc = _bacc.Bacc("TRN2", target_bir_lowering=False, num_devices=1)
    arrays, args = {}, []
    for name in _INS:
        a = _np.ascontiguousarray(inputs[name])
        arrays[f"in_{name}"] = a
        args.append(nc.dram_tensor(f"in_{name}", a.shape, _mybir.dt.from_np(a.dtype), kind="ExternalInput").ap())
    out = nc.dram_tensor("out_x", (NODES, D), _mybir.dt.float32, kind="ExternalOutput").ap()
    build(nc, *args, out)
    r = _run(nc, [arrays], core_ids=[0])
    return r.results[0]["out_x"]
```
